# Optimizing a Trainium2 kernel written in Bass

```python
import numpy as np
import jax
import jax.numpy as jnp

def _softmax(x, axis=-1):
    return jax.nn.softmax(x, axis=axis)

def _gelu(x):
    return jax.nn.gelu(x, approximate=True)

def _silu(x):
    return jax.nn.silu(x)

def _sigmoid(x):
    return jax.nn.sigmoid(x)

def _layernorm(x, axis=-1, eps=1e-05):
    m = jnp.mean(x, axis=axis, keepdims=True)
    v = jnp.var(x, axis=axis, keepdims=True)
    return (x - m) / jnp.sqrt(v + eps)

def _scatter_add(tgt, idx, src, axis=0):
    return tgt.at[idx].add(src)

def _segment_sum(src, seg, n):
    return jax.ops.segment_sum(src, seg, n)
kernel_name = 'mk_lm_tower_d2_tok_ids512_r4_66ef11'

def setup_inputs(seed: int=0):
    np.random.seed(seed)
    _w = jnp.asarray

    def _rec_inputs():
        import jax
        import jax.numpy as jnp
        _rk = jax.random.key(seed)
        x = jax.random.randint(jax.random.fold_in(_rk, 1), (64, 128), 0, 50257, jnp.int32)
        return x
    x = _rec_inputs()

    def _L0_tok_setup():
        import jax, jax.numpy as jnp
        import numpy as np
        VOCAB = 50257
        FEAT = 128
        EPS = 1e-12
        key = jax.random.key(seed)
        k1, k2, k3 = jax.random.split(key, 3)
        token_ids = jax.random.randint(k1, (32, 1024), 0, VOCAB)
        W = jax.random.normal(k2, (FEAT, VOCAB), dtype=jnp.float32) * 0.02
        b = jax.random.normal(k3, (FEAT,), dtype=jnp.float32) * 0.02
        return {'token_ids': token_ids, 'W': W, 'b': b}
    _L0_tok_all = _L0_tok_setup()
    _L0_tok_in = {k: v for k, v in _L0_tok_all.items() if k in ('W', 'b')}
    del _L0_tok_all

    def _L0_attn_setup():
        import jax, jax.numpy as jnp
        import numpy as np
        B, N, D_MODEL, H, DK, DV = (8, 128, 128, 8, 64, 64)
        MAX_DIST = 128
        NUM_REL = 2 * MAX_DIST - 1
        key = jax.random.key(seed)
        ks = jax.random.split(key, 12)
        s = 0.02
        return {'X': jax.random.normal(ks[0], (B, N, D_MODEL), jnp.float32), 'Wq': jax.random.normal(ks[1], (D_MODEL, H * DK), jnp.float32) * s, 'bq': jnp.zeros((H * DK,), jnp.float32), 'Wk': jax.random.normal(ks[2], (D_MODEL, H * DK), jnp.float32) * s, 'bk': jnp.zeros((H * DK,), jnp.float32), 'Wv': jax.random.normal(ks[3], (D_MODEL, H * DV), jnp.float32) * s, 'bv': jnp.zeros((H * DV,), jnp.float32), 'Wo': jax.random.normal(ks[4], (H * DV, D_MODEL), jnp.float32) * s, 'bo': jnp.zeros((D_MODEL,), jnp.float32), 'P_k': jax.random.normal(ks[5], (NUM_REL, H), jnp.float32), 'P_v': jax.random.normal(ks[6], (NUM_REL, H, DV), jnp.float32)}
    _L0_attn_all = _L0_attn_setup()
    _L0_attn_in = {k: v for k, v in _L0_attn_all.items() if k in ('Wq', 'bq', 'Wk', 'bk', 'Wv', 'bv', 'Wo', 'bo', 'P_k', 'P_v')}
    del _L0_attn_all

    def _L0_ffn_setup():
        import jax, jax.numpy as jnp
        import numpy as np
        H = 128
        F = 512
        E = 16
        SHARED = 2
        TOP_K = 4
        B, S = (2, 512)

        def _mlp(x, w1, b1, w2, b2):
            return jax.nn.gelu(x @ w1 + b1, approximate=False) @ w2 + b2
        key = jax.random.key(seed)
        ks = jax.random.split(key, 10)
        sc = 0.02
        return {'hidden_states': jax.random.normal(ks[0], (B, S, H), dtype=jnp.float32), 'gate_w': jax.random.normal(ks[1], (E, H), dtype=jnp.float32) * sc, 're_w1': jax.random.normal(ks[2], (E, H, F), dtype=jnp.float32) * sc, 're_b1': jnp.zeros((E, F), dtype=jnp.float32), 're_w2': jax.random.normal(ks[3], (E, F, H), dtype=jnp.float32) * sc, 're_b2': jnp.zeros((E, H), dtype=jnp.float32), 'se_w1': jax.random.normal(ks[4], (SHARED, H, F), dtype=jnp.float32) * sc, 'se_b1': jnp.zeros((SHARED, F), dtype=jnp.float32), 'se_w2': jax.random.normal(ks[5], (SHARED, F, H), dtype=jnp.float32) * sc, 'se_b2': jnp.zeros((SHARED, H), dtype=jnp.float32)}
    _L0_ffn_all = _L0_ffn_setup()
    _L0_ffn_in = {k: v for k, v in _L0_ffn_all.items() if k in ('gate_w', 're_w1', 're_b1', 're_w2', 're_b2', 'se_w1', 'se_b1', 'se_w2', 'se_b2')}
    del _L0_ffn_all

    def _L1_attn_setup():
        import jax, jax.numpy as jnp
        import numpy as np
        H = 8
        EPS = 1e-05

        def _ln(x, g=None, b=None):
            m = jnp.mean(x, axis=-1, keepdims=True)
            v = jnp.mean((x - m) ** 2, axis=-1, keepdims=True)
            y = (x - m) * jax.lax.rsqrt(v + EPS)
            if g is not None:
                y = y * g + b
            return y
        key = jax.random.key(seed)
        B, N, C = (1, 1024, 128)
        inner = 128
        ks = jax.random.split(key, 8)
        sc = 1.0 / np.sqrt(C).astype(np.float32)
        return {'x': jax.random.normal(ks[0], (B, N, C), jnp.float32), 'w_q': jax.random.normal(ks[1], (C, inner), jnp.float32) * sc, 'b_q': jnp.zeros((inner,), jnp.float32), 'w_k': jax.random.normal(ks[2], (C, inner), jnp.float32) * sc, 'b_k': jnp.zeros((inner,), jnp.float32), 'w_v': jax.random.normal(ks[3], (C, inner), jnp.float32) * sc, 'b_v': jnp.zeros((inner,), jnp.float32), 'g_q': jnp.ones((inner,), jnp.float32), 'be_q': jnp.zeros((inner,), jnp.float32), 'g_k': jnp.ones((inner,), jnp.float32), 'be_k': jnp.zeros((inner,), jnp.float32), 'w_o': jax.random.normal(ks[4], (inner, C), jnp.float32) * sc, 'b_o': jnp.zeros((C,), jnp.float32)}
    _L1_attn_all = _L1_attn_setup()
    _L1_attn_in = {k: v for k, v in _L1_attn_all.items() if k in ('w_q', 'b_q', 'w_k', 'b_k', 'w_v', 'b_v', 'g_q', 'be_q', 'g_k', 'be_k', 'w_o', 'b_o')}
    del _L1_attn_all

    def _L1_ffn_setup():
        import jax, jax.numpy as jnp
        import numpy as np
        K_INPUT, K_PROCESS, K_OUTPUT = (64, 128, 64)

        def _gelu(x):
            return jax.nn.gelu(x, approximate=False)
        key = jax.random.key(seed)
        ks = jax.random.split(key, 6)
        d_model, n_in, n_proc, n_out, d_pv = (128, 512, 256, 512, 64)
        B, S = (2, 256)

        def xavier(k, shape):
            std = (2.0 / (shape[0] + shape[1])) ** 0.5
            return jax.random.normal(k, shape, dtype=jnp.float32) * std
        return {'x': jax.random.normal(ks[0], (B, S, d_model), dtype=jnp.float32), 'input_patterns': xavier(ks[1], (n_in, d_model)), 'process_input_weights': xavier(ks[2], (n_proc, n_in)), 'process_values': xavier(ks[3], (n_proc, d_pv)), 'output_input_weights': xavier(ks[4], (n_out, d_pv)), 'output_patterns': xavier(ks[5], (n_out, d_model))}
    _L1_ffn_all = _L1_ffn_setup()
    _L1_ffn_in = {k: v for k, v in _L1_ffn_all.items() if k in ('input_patterns', 'process_input_weights', 'process_values', 'output_input_weights', 'output_patterns')}
    del _L1_ffn_all
    return {'x': x, 'L0_tok_W': _L0_tok_in['W'], 'L0_tok_b': _L0_tok_in['b'], 'L0_attn_Wq': _L0_attn_in['Wq'], 'L0_attn_bq': _L0_attn_in['bq'], 'L0_attn_Wk': _L0_attn_in['Wk'], 'L0_attn_bk': _L0_attn_in['bk'], 'L0_attn_Wv': _L0_attn_in['Wv'], 'L0_attn_bv': _L0_attn_in['bv'], 'L0_attn_Wo': _L0_attn_in['Wo'], 'L0_attn_bo': _L0_attn_in['bo'], 'L0_attn_P_k': _L0_attn_in['P_k'], 'L0_attn_P_v': _L0_attn_in['P_v'], 'L0_ffn_gate_w': _L0_ffn_in['gate_w'], 'L0_ffn_re_w1': _L0_ffn_in['re_w1'], 'L0_ffn_re_b1': _L0_ffn_in['re_b1'], 'L0_ffn_re_w2': _L0_ffn_in['re_w2'], 'L0_ffn_re_b2': _L0_ffn_in['re_b2'], 'L0_ffn_se_w1': _L0_ffn_in['se_w1'], 'L0_ffn_se_b1': _L0_ffn_in['se_b1'], 'L0_ffn_se_w2': _L0_ffn_in['se_w2'], 'L0_ffn_se_b2': _L0_ffn_in['se_b2'], 'L1_attn_w_q': _L1_attn_in['w_q'], 'L1_attn_b_q': _L1_attn_in['b_q'], 'L1_attn_w_k': _L1_attn_in['w_k'], 'L1_attn_b_k': _L1_attn_in['b_k'], 'L1_attn_w_v': _L1_attn_in['w_v'], 'L1_attn_b_v': _L1_attn_in['b_v'], 'L1_attn_g_q': _L1_attn_in['g_q'], 'L1_attn_be_q': _L1_attn_in['be_q'], 'L1_attn_g_k': _L1_attn_in['g_k'], 'L1_attn_be_k': _L1_attn_in['be_k'], 'L1_attn_w_o': _L1_attn_in['w_o'], 'L1_attn_b_o': _L1_attn_in['b_o'], 'L1_ffn_input_patterns': _L1_ffn_in['input_patterns'], 'L1_ffn_process_input_weights': _L1_ffn_in['process_input_weights'], 'L1_ffn_process_values': _L1_ffn_in['process_values'], 'L1_ffn_output_input_weights': _L1_ffn_in['output_input_weights'], 'L1_ffn_output_patterns': _L1_ffn_in['output_patterns']}

def reference(x, L0_tok_W, L0_tok_b, L0_attn_Wq, L0_attn_bq, L0_attn_Wk, L0_attn_bk, L0_attn_Wv, L0_attn_bv, L0_attn_Wo, L0_attn_bo, L0_attn_P_k, L0_attn_P_v, L0_ffn_gate_w, L0_ffn_re_w1, L0_ffn_re_b1, L0_ffn_re_w2, L0_ffn_re_b2, L0_ffn_se_w1, L0_ffn_se_b1, L0_ffn_se_w2, L0_ffn_se_b2, L1_attn_w_q, L1_attn_b_q, L1_attn_w_k, L1_attn_b_k, L1_attn_w_v, L1_attn_b_v, L1_attn_g_q, L1_attn_be_q, L1_attn_g_k, L1_attn_be_k, L1_attn_w_o, L1_attn_b_o, L1_ffn_input_patterns, L1_ffn_process_input_weights, L1_ffn_process_values, L1_ffn_output_input_weights, L1_ffn_output_patterns):
    import jax
    import jax.numpy as jnp

    def _L0_tok_ref(token_ids, W, b):
        import jax, jax.numpy as jnp
        import numpy as np
        VOCAB = 50257
        FEAT = 128
        EPS = 1e-12
        feats = W.T[token_ids] + b
        norm = jnp.sqrt(jnp.sum(feats * feats, axis=-1, keepdims=True))
        return feats / jnp.maximum(norm, EPS)

    def _L0_attn_ref(X, Wq, bq, Wk, bk, Wv, bv, Wo, bo, P_k, P_v):
        import jax, jax.numpy as jnp
        import numpy as np
        B, N, D_MODEL, H, DK, DV = (8, 128, 128, 8, 64, 64)
        MAX_DIST = 128
        NUM_REL = 2 * MAX_DIST - 1
        b, n, d = X.shape
        scale = 1.0 / jnp.sqrt(jnp.float32(DK))
        Q = (X @ Wq + bq).reshape(b, n, H, DK).transpose(0, 2, 1, 3)
        K = (X @ Wk + bk).reshape(b, n, H, DK).transpose(0, 2, 1, 3)
        V = (X @ Wv + bv).reshape(b, n, H, DV).transpose(0, 2, 1, 3)
        zero_offset = NUM_REL // 2
        rel = zero_offset + (jnp.arange(n)[None, :] - jnp.arange(n)[:, None])
        A_k = P_k[rel]
        scores = (jnp.einsum('bhid,bhjd->bhij', Q, K) + A_k.transpose(2, 0, 1)[None]) * scale
        attn = jax.nn.softmax(scores, axis=-1)
        A_v = P_v[rel]
        out = jnp.einsum('bhij,bhjd->bhid', attn, V) + jnp.einsum('bhij,ijhd->bhid', attn, A_v)
        out = out.transpose(0, 2, 1, 3).reshape(b, n, H * DV)
        return out @ Wo + bo

    def _L0_ffn_ref(hidden_states, gate_w, re_w1, re_b1, re_w2, re_b2, se_w1, se_b1, se_w2, se_b2):
        import jax, jax.numpy as jnp
        import numpy as np
        H = 128
        F = 512
        E = 16
        SHARED = 2
        TOP_K = 4
        B, S = (2, 512)

        def _mlp(x, w1, b1, w2, b2):
            return jax.nn.gelu(x @ w1 + b1, approximate=False) @ w2 + b2
        b, s, h = hidden_states.shape
        x = hidden_states.reshape(-1, h)
        gate_probs = jax.nn.softmax(x @ gate_w.T, axis=-1)
        top_v, top_i = jax.lax.top_k(gate_probs, TOP_K)
        top_v = jax.nn.softmax(top_v, axis=-1)
        combine = jnp.einsum('tk,tke->te', top_v, jax.nn.one_hot(top_i, E, dtype=x.dtype))
        routed = jnp.zeros_like(x)
        for e in range(E):
            routed = routed + combine[:, e:e + 1] * _mlp(x, re_w1[e], re_b1[e], re_w2[e], re_b2[e])
        shared = jnp.zeros_like(x)
        for j in range(SHARED):
            shared = shared + _mlp(x, se_w1[j], se_b1[j], se_w2[j], se_b2[j])
        shared = shared / SHARED
        return (routed + shared).reshape(b, s, h)

    def _L1_attn_ref(x, w_q, b_q, w_k, b_k, w_v, b_v, g_q, be_q, g_k, be_k, w_o, b_o):
        import jax, jax.numpy as jnp
        import numpy as np
        H = 8
        EPS = 1e-05

        def _ln(x, g=None, b=None):
            m = jnp.mean(x, axis=-1, keepdims=True)
            v = jnp.mean((x - m) ** 2, axis=-1, keepdims=True)
            y = (x - m) * jax.lax.rsqrt(v + EPS)
            if g is not None:
                y = y * g + b
            return y
        B, N, C = x.shape
        silu = jax.nn.silu
        xn = _ln(x)
        q = silu(xn) @ w_q + b_q
        k = silu(xn) @ w_k + b_k
        v = silu(xn) @ w_v + b_v
        q = _ln(q, g_q, be_q)
        k = _ln(k, g_k, be_k)
        inner = q.shape[-1]
        q = q * inner ** (-0.5)
        d = inner // H
        qh = q.reshape(B, N, H, d).transpose(0, 2, 1, 3)
        kh = k.reshape(B, N, H, d).transpose(0, 2, 1, 3)
        vh = v.reshape(B, N, H, d).transpose(0, 2, 1, 3)
        w = jax.nn.softmax(jnp.einsum('bhid,bhjd->bhij', qh, kh), axis=-1)
        o = jnp.einsum('bhij,bhjd->bhid', w, vh)
        o = o.transpose(0, 2, 1, 3).reshape(B, N, inner)
        return silu(o) @ w_o + b_o

    def _L1_ffn_ref(x, input_patterns, process_input_weights, process_values, output_input_weights, output_patterns):
        import jax, jax.numpy as jnp
        import numpy as np
        K_INPUT, K_PROCESS, K_OUTPUT = (64, 128, 64)

        def _gelu(x):
            return jax.nn.gelu(x, approximate=False)
        B, S, d_model = x.shape
        n_in = input_patterns.shape[0]
        input_acts = _gelu(jnp.einsum('bsd,nd->bsn', x, input_patterns))
        top_in_acts, top_in_idx = jax.lax.top_k(input_acts, K_INPUT)
        bi = jnp.arange(B)[:, None, None]
        si = jnp.arange(S)[None, :, None]
        input_repr = jnp.zeros((B, S, n_in), dtype=x.dtype).at[bi, si, top_in_idx].set(top_in_acts)
        process_acts = _gelu(jnp.einsum('bsn,pn->bsp', input_repr, process_input_weights))
        top_p_acts, top_p_idx = jax.lax.top_k(process_acts, K_PROCESS)
        sel_values = process_values[top_p_idx]
        p_weights = jax.nn.softmax(top_p_acts, axis=-1)
        agg_value = jnp.einsum('bsk,bskd->bsd', p_weights, sel_values)
        output_acts = _gelu(jnp.einsum('bsd,od->bso', agg_value, output_input_weights))
        top_o_acts, top_o_idx = jax.lax.top_k(output_acts, K_OUTPUT)
        sel_patterns = output_patterns[top_o_idx]
        out = jnp.einsum('bsk,bskm->bsm', top_o_acts, sel_patterns)
        return out
    h = _L0_tok_ref(x, L0_tok_W, L0_tok_b)
    h = h + _L0_attn_ref(_layernorm(h, axis=-1), L0_attn_Wq, L0_attn_bq, L0_attn_Wk, L0_attn_bk, L0_attn_Wv, L0_attn_bv, L0_attn_Wo, L0_attn_bo, L0_attn_P_k, L0_attn_P_v)
    h = h + _L0_ffn_ref(_layernorm(h, axis=-1), L0_ffn_gate_w, L0_ffn_re_w1, L0_ffn_re_b1, L0_ffn_re_w2, L0_ffn_re_b2, L0_ffn_se_w1, L0_ffn_se_b1, L0_ffn_se_w2, L0_ffn_se_b2)
    h = h + _L1_attn_ref(_layernorm(h, axis=-1), L1_attn_w_q, L1_attn_b_q, L1_attn_w_k, L1_attn_b_k, L1_attn_w_v, L1_attn_b_v, L1_attn_g_q, L1_attn_be_q, L1_attn_g_k, L1_attn_be_k, L1_attn_w_o, L1_attn_b_o)
    h = h + _L1_ffn_ref(_layernorm(h, axis=-1), L1_ffn_input_patterns, L1_ffn_process_input_weights, L1_ffn_process_values, L1_ffn_output_input_weights, L1_ffn_output_patterns)
    return h

_drawn_inputs = setup_inputs


def setup_inputs(seed=0):
    import zlib

    import numpy as np

    out = dict(_drawn_inputs(seed))
    spreads = {'L0_attn_bq': (0.0, 0.591),
     'L0_attn_bk': (0.0, 0.8),
     'L0_attn_bv': (0.0, 0.1),
     'L0_attn_bo': (0.0, 0.1),
     'L0_ffn_re_b1': (0.0, 0.1),
     'L0_ffn_re_b2': (0.0, 0.1),
     'L0_ffn_se_b1': (0.0, 0.1),
     'L0_ffn_se_b2': (0.0, 0.1),
     'L1_attn_b_q': (0.0, 0.8),
     'L1_attn_b_k': (0.0, 0.8),
     'L1_attn_b_v': (0.0, 0.1),
     'L1_attn_g_q': (1.0, 0.6),
     'L1_attn_be_q': (0.0, 0.8),
     'L1_attn_g_k': (1.0, 0.6),
     'L1_attn_be_k': (0.0, 0.8),
     'L1_attn_b_o': (0.0, 0.1)}
    factors = {'L0_attn_Wq': 3.317,
     'L0_attn_Wk': 3.182,
     'L1_attn_w_q': 3.175,
     'L1_attn_w_k': 4.167,
     'L1_ffn_input_patterns': 8.0,
     'L1_ffn_process_input_weights': 8.0,
     'L1_ffn_process_values': 8.0,
     'L1_ffn_output_input_weights': 8.0,
     'L1_ffn_output_patterns': 8.0}
    for name, (base, spread) in spreads.items():
        noise = np.random.default_rng([zlib.crc32(name.encode()), seed]).standard_normal(out[name].shape)
        drawn = base * np.exp(spread * noise) if base else spread * noise
        out[name] = jnp.asarray(drawn.astype(out[name].dtype))
    for name, factor in factors.items():
        out[name] = (out[name] * factor).astype(out[name].dtype)
    return out
```

```python
from contextlib import ExitStack

import concourse.bass as bass
from concourse import mybir

ALU = mybir.AluOpType
ACT = mybir.ActivationFunctionType
F32 = mybir.dt.float32
U32 = mybir.dt.uint32
X = mybir.AxisListType.X
ds = bass.ds

P = 128
SEQ = 64
QT = 4
G = SEQ // QT
W4 = QT * P
EPS = 1e-5
ONE = 1


def wait_apart(eng, cst, sem, value):
    value = ONE + value
    if not isinstance(value, int):
        value = eng.snap(eng.compute_val(value))
        eng.wait_ge(cst["consts_done"], ONE + 3)
    eng.wait_ge(sem, value)


def tokens_phase(nc, d, cst, scr):
    with ExitStack() as ctx:
        def sb(name, shape, dt=F32):
            return ctx.enter_context(nc.sbuf_tensor(f"tok_{name}", shape, dt))

        sems = []

        def sem(name):
            sems.append(ctx.enter_context(nc.semaphore(f"tok_{name}")))
            return sems[-1]

        ids = sb("ids", [P, SEQ], U32)
        ids_now = sb("ids_now", [P, 2, QT], U32)
        feat = sb("feat", [P, 2, QT, P])
        tok_b = sb("tok_b", [P, P])
        out_b = sb("out_b", [P, P])
        h_all = sb("h_all", [P, SEQ, P])
        square = sb("square", [P, QT, P])
        ssq = sb("ssq", [P, SEQ])
        inv = sb("inv", [P, SEQ])
        stats = sb("stats", [P, QT, 6])
        mv = sb("mv", [P, QT, 2])
        mean = sb("mean", [P, SEQ])
        rstd = sb("rstd", [P, SEQ])
        shift = sb("shift", [P, SEQ])
        h_out = sb("h_out", [P, 2, QT, P])
        xn = sb("xn", [P, 2, QT, P])
        xt = sb("xt", [P, 2, W4])
        ps = [ctx.enter_context(nc.psum_tensor(f"tok_ps_xt{i}", [P, W4], F32)) for i in range(2)]

        ids_in = sem("ids_in")
        bias_in = sem("bias_in")
        ids_copied = sem("ids_copied")
        gathered = [ctx.enter_context(nc.semaphore(f"tok_gathered{i}")) for i in range(2)]
        feat_used = sem("feat_used")
        dve = sem("dve_step")
        ssq_done = sem("ssq_done")
        inv_done = sem("inv_done")
        var_done = sem("var_done")
        rstd_done = sem("rstd_done")
        h_out_done = sem("h_out_done")
        h_stored = [sem("h_stored0"), sem("h_stored1")]
        xn_done = sem("xn_done")
        xt_ready = sem("xt_ready")
        xt_copied = sem("xt_copied")
        xt_stored = [sem("xt_stored0"), sem("xt_stored1")]

        block = ctx.enter_context(nc.Block())

        @block.sync
        def _(sp):
            for s in sems + [cst["pool_step"], cst["consts_done"]]:
                sp.sem_inc(s, ONE)
            sp.dma_start(ids[:, :], d["ids"].bitcast(U32)).then_inc(ids_in, 16)
            sp.dma_start(tok_b[:, :], d["tok_b"].partition_broadcast(P)).then_inc(bias_in, 16)
            sp.dma_start(out_b[:, :], d["bo"].partition_broadcast(P)).then_inc(bias_in, 16)
            with sp.Fori(0, G // 2) as gg:
                g = gg * 2
                for p in range(2):
                    sp.wait_ge(h_out_done, ONE + g + p + 1)
                    sp.dma_start(scr["h"][ds(g + p, 1), :, :].rearrange("a p n -> (a p) n"),
                                 h_out[:, p].rearrange("p q n -> p (q n)")).then_inc(h_stored[p], 16)
            with sp.Fori(0, G // 2) as gg:
                g = gg * 2
                for p in range(2):
                    sp.wait_ge(xt_copied, ONE + g + p + 1)
                    sp.dma_start(scr["xt"][ds(g + p, 1), :, :].rearrange("a p n -> (a p) n"),
                                 xt[:, p]).then_inc(xt_stored[p], 16)
            for p in range(2):
                sp.wait_ge(h_stored[p], ONE + 16 * (G // 2))
                sp.wait_ge(xt_stored[p], ONE + 16 * (G // 2))

        @block.gpsimd
        def _(pool):
            nc.gpsimd.memset(cst["ident"][:, :], 0.0).then_inc(cst["pool_step"], 1)
            pool.wait_ge(cst["pool_step"], ONE + 1)
            nc.gpsimd.affine_select(out=cst["ident"][:, :], in_=cst["ident"][:, :], compare_op=ALU.not_equal,
                                    fill=1.0, base=0, pattern=[[-1, P]],
                                    channel_multiplier=1).then_inc(cst["consts_done"], 1)
            nc.gpsimd.memset(cst["neg_half"][:, :], -0.5).then_inc(cst["consts_done"], 1)
            nc.gpsimd.memset(cst["ones_row"][:, :], 1.0).then_inc(cst["consts_done"], 1)
            pool.wait_ge(ids_in, ONE + 16)
            with pool.Fori(0, G // 2) as gg:
                g = gg * 2
                for p in range(2):
                    pool.wait_ge(feat_used, ONE + g)
                    nc.gpsimd.tensor_copy(ids_now[:, p, :], ids[:, ds((g + p) * QT, QT)]).then_inc(ids_copied, 1)
                    wait_apart(pool, cst, ids_copied, g + p + 1)
                    for q in range(QT):
                        nc.gpsimd.indirect_dma_start(
                            out=feat[:, p, q, :], out_offset=None, in_=d["wt"],
                            in_offset=bass.IndirectOffsetOnAxis(ap=ids_now[:, p, q:q + 1], axis=0),
                        ).then_inc(gathered[p], 16)
            pool.wait_ge(cst["consts_done"], ONE + 3)
            pool.wait_ge(ssq_done, ONE + 1)
            nc.gpsimd.tensor_tensor(inv[:, :], ssq[:, :], cst["neg_half"][:, 0:SEQ], ALU.pow).then_inc(inv_done, 1)
            pool.wait_ge(var_done, ONE + G)
            nc.gpsimd.tensor_tensor(rstd[:, :], rstd[:, :], cst["neg_half"][:, 0:SEQ], ALU.pow).then_inc(rstd_done, 1)

        @block.vector
        def _(v):
            v.wait_ge(bias_in, ONE + 32)
            bias4 = tok_b[:, :].unsqueeze(1).broadcast_to([P, QT, P])
            out4 = out_b[:, :].unsqueeze(1).broadcast_to([P, QT, P])
            with v.Fori(0, G // 2) as gg:
                g = gg * 2
                for p in range(2):
                    t = ds((g + p) * QT, QT)
                    v.wait_ge(gathered[p], g * (8 * QT) + 16 * QT)
                    nc.vector.tensor_tensor(h_all[:, t, :], feat[:, p], bias4, ALU.add).then_inc(feat_used, 1)
                    v.wait_ge(feat_used, ONE + g + p + 1)
                    nc.vector.tensor_tensor(square[:, :, :], h_all[:, t, :], h_all[:, t, :],
                                            ALU.mult).then_inc(dve, 1)
                    v.wait_ge(dve, ONE + 2 * (g + p) + 1)
                    nc.vector.tensor_reduce(ssq[:, t], square[:, :, :], X, ALU.add).then_inc(dve, 1)
            v.wait_ge(dve, ONE + 2 * G)
            nc.vector.tensor_scalar(ssq[:, :], ssq[:, :], 1e-24, None, ALU.max).then_inc(ssq_done, 1)
            v.wait_ge(inv_done, ONE + 1)
            with v.Fori(0, G // 2) as gg:
                g = gg * 2
                for p in range(2):
                    t = ds((g + p) * QT, QT)
                    n = g + p
                    nc.vector.tensor_tensor(h_all[:, t, :], h_all[:, t, :],
                                            inv[:, t].unsqueeze(2).broadcast_to([P, QT, P]),
                                            ALU.mult).then_inc(dve, 1)
                    v.wait_ge(dve, ONE + n * 3 + (2 * G + 1))
                    v.wait_ge(h_stored[p], ONE + g * 8)
                    nc.vector.tensor_tensor(h_out[:, p], h_all[:, t, :], out4, ALU.add).then_inc(h_out_done, 1)
                    for q in range(QT):
                        last = nc.vector.bn_stats(stats[:, q, :], h_all[:, ds((g + p) * QT + q, 1), :]
                                                  .rearrange("p a n -> p (a n)"))
                    last.then_inc(dve, 1)
                    wait_apart(v, cst, dve, n * 3 + (2 * G + 2))
                    for q in range(QT):
                        last = nc.vector.bn_aggr(mv[:, q, :], stats[:, q, :])
                    last.then_inc(dve, 1)
                    v.wait_ge(dve, ONE + n * 3 + (2 * G + 3))
                    nc.vector.tensor_copy(mean[:, t], mv[:, :, 0])
                    nc.vector.tensor_scalar(rstd[:, t], mv[:, :, 1], EPS, None, ALU.add).then_inc(var_done, 1)
            v.wait_ge(rstd_done, ONE + 1)
            nc.vector.scalar_tensor_tensor(out=shift[:, :], in0=mean[:, :], scalar=-1.0, in1=rstd[:, :],
                                           op0=ALU.mult, op1=ALU.mult).then_inc(dve, 1)
            v.wait_ge(dve, ONE + 5 * G + 1)
            with v.Fori(0, G // 2) as gg:
                g = gg * 2
                for p in range(2):
                    v.wait_ge(xt_ready, ONE + g)
                    for q in range(QT):
                        i = ds((g + p) * QT + q, 1)
                        last = nc.vector.tensor_scalar(
                            xn[:, p, q, :], h_all[:, i, :].rearrange("p a n -> p (a n)"),
                            rstd[:, i], shift[:, i], ALU.mult, ALU.add)
                    last.then_inc(xn_done, 1)

        @block.tensor
        def _(pe):
            pe.wait_ge(cst["consts_done"], ONE + 3)
            with pe.Fori(0, G // 2) as gg:
                g = gg * 2
                for p in range(2):
                    pe.wait_ge(xn_done, ONE + g + p + 1)
                    pe.wait_ge(xt_copied, ONE + g)
                    for q in range(QT):
                        last = nc.tensor.transpose(ps[p][:, q * P:(q + 1) * P], xn[:, p, q, :], cst["ident"][:, :])
                    last.then_inc(xt_ready, 1)

        @block.scalar
        def _(act):
            with act.Fori(0, G // 2) as gg:
                g = gg * 2
                for p in range(2):
                    act.wait_ge(xt_ready, ONE + g + p + 1)
                    act.wait_ge(xt_stored[p], ONE + g * 8)
                    nc.scalar.copy(xt[:, p], ps[p][:, :]).then_inc(xt_copied, 1)


def attention0_phase(nc, d, cst, scr):
    H, DK, NR = 8, 64, 2 * P - 1
    NP = H // 2
    IB = 8
    NIB = P // IB
    SCALE = float(DK) ** -0.5
    with ExitStack() as ctx:
        def sb(name, shape, dt=F32):
            return ctx.enter_context(nc.sbuf_tensor(f"att_{name}", shape, dt))

        sems = []

        def sem(name):
            sems.append(ctx.enter_context(nc.semaphore(f"att_{name}")))
            return sems[-1]

        def bank(name):
            return ctx.enter_context(nc.psum_tensor(f"att_{name}", [P, W4], F32))

        xg = sb("xg", [P, W4])
        wqkv = sb("wqkv", [P, 3, P])
        bqkv = sb("bqkv", [P, 3])
        rel_k = sb("rel_k", [P, H, P])
        q_t = sb("q_t", [P, W4])
        k_t = sb("k_t", [P, W4])
        v_s = sb("v_s", [P, QT, P])
        s_s = sb("s_s", [P, 2, QT, P])
        top = sb("top", [P, 2, QT])
        ntop = sb("ntop", [P, 2, QT])
        z = sb("z", [P, 2, QT])
        rz = sb("rz", [P, 2, QT])
        p_s = sb("p_s", [P, 2, QT, P])
        p_now = sb("p_now", [P, 2, QT, P])
        p_t = sb("p_t", [P, 2, SEQ, P])
        rel_v = sb("rel_v", [P, 2, 2, IB, DK])
        o_t = sb("o_t", [P, SEQ, P])
        ps_q, ps_k, ps_v, ps_o = (bank(f"ps_{n}") for n in "qkvo")
        ps_s = [bank("ps_s0"), bank("ps_s1")]
        ps_t = [bank("ps_t0"), bank("ps_t1")]

        x_in = sem("x_in")
        w_in = sem("w_in")
        rk_in = sem("rk_in")
        rv_in = [sem("rv_in0"), sem("rv_in1")]
        q_ready = sem("q_ready")
        k_ready = sem("k_ready")
        v_ready = sem("v_ready")
        qk_copied = sem("qk_copied")
        v_copied = sem("v_copied")
        s_ready = sem("s_ready")
        s_added = sem("s_added")
        top_done = sem("top_done")
        ntop_done = sem("ntop_done")
        exp_done = sem("exp_done")
        rz_done = sem("rz_done")
        p_done = sem("p_done")
        t_ready = sem("t_ready")
        t_copied = sem("t_copied")
        t_kept = sem("t_kept")
        o_ready = sem("o_ready")
        o_copied = sem("o_copied")
        r_ready = sem("r_ready")
        r_added = sem("r_added")
        o_stored = sem("o_stored")

        block = ctx.enter_context(nc.Block())
        U = G

        @block.sync
        def _(sp):
            for s in sems:
                sp.sem_inc(s, ONE)
            sp.dma_start(rel_k[:, :, :], bass.AP(tensor=d["pk"].tensor, offset=P - 1,
                                                 ap=[[NR - 1, P], [P * NR, H], [1, P]])).then_inc(rk_in, 16)
            with sp.Fori(0, NP) as hp:
                sp.wait_ge(v_ready, ONE + hp * U)
                sp.dma_start(wqkv[:, :, :], d["wqkv"][ds(hp, 1)].rearrange("a p t n -> (a p) t n")).then_inc(w_in, 16)
                sp.wait_ge(o_copied, ONE + hp * U)
                sp.dma_start(bqkv[:, :], d["bqkv"][ds(hp, 1)].rearrange("a p t -> (a p) t")).then_inc(w_in, 16)
                with sp.Fori(0, U) as g:
                    sp.wait_ge(v_ready, ONE + hp * U + g)
                    sp.dma_start(xg[:, :], scr["xt"][ds(g, 1)].rearrange("a p n -> (a p) n")).then_inc(x_in, 16)
                with sp.Fori(0, NIB // 2) as ibb:
                    ib = ibb * 2
                    for p in range(2):
                        sp.wait_ge(r_ready, ONE + hp * NIB + ib)
                        for h in range(2):
                            src = d["pv"][ds(hp * 2 + h, 1), ds((ib + p) * IB, IB), :]
                            win = bass.AP(tensor=src.tensor, offset=src.offset, ap=[[DK, P], [1, IB * DK]])
                            sp.dma_start(rel_v[:, p, h].rearrange("p i d -> p (i d)"), win).then_inc(rv_in[p], 16)
                sp.wait_ge(r_added, ONE + (hp + 1) * NIB)
                sp.dma_start(scr["o"][ds(hp, 1)].rearrange("a p n -> (a p) n"),
                             o_t[:, :, :].rearrange("p b i -> p (b i)")).then_inc(o_stored, 16)
            sp.wait_ge(o_stored, ONE + 16 * NP)

        @block.tensor
        def _(pe):
            def project(hp, u):
                pe.wait_ge(w_in, ONE + hp * 32 + 32)
                pe.wait_ge(x_in, ONE + u * 16 + 16)
                pe.wait_ge(qk_copied, ONE + u * 2)
                nc.tensor.matmul(ps_q[:, :], wqkv[:, 0, :], xg[:, :], start=True, stop=True).then_inc(q_ready, 1)
                nc.tensor.matmul(ps_k[:, :], wqkv[:, 1, :], xg[:, :], start=True, stop=True).then_inc(k_ready, 1)
                pe.wait_ge(v_copied, ONE + u)
                for t in range(QT):
                    last = nc.tensor.matmul(ps_v[:, t * P:(t + 1) * P], xg[:, t * P:(t + 1) * P], wqkv[:, 2, :],
                                            start=True, stop=True)
                last.then_inc(v_ready, 1)

            def scores(u):
                pe.wait_ge(qk_copied, ONE + u * 2 + 2)
                pe.wait_ge(s_added, ONE + u * 2)
                for t in range(QT):
                    for h in range(2):
                        r = slice(h * DK, (h + 1) * DK)
                        c = slice(t * P, (t + 1) * P)
                        last = nc.tensor.matmul(ps_s[h][:, c], q_t[r, c], k_t[r, c], start=True, stop=True)
                        if t == QT - 1:
                            last.then_inc(s_ready, 1)

            def transposes(u):
                for h in range(2):
                    pe.wait_ge(p_done, ONE + u * 2 + h + 1)
                    pe.wait_ge(t_copied, ONE + u * 2)
                    for t in range(QT):
                        last = nc.tensor.transpose(ps_t[h][:, t * P:(t + 1) * P], p_s[:, h, t, :], cst["ident"][:, :])
                    last.then_inc(t_ready, 1)

            def values(u):
                pe.wait_ge(t_copied, ONE + u * 2 + 2)
                pe.wait_ge(v_copied, ONE + u + 1)
                pe.wait_ge(o_copied, ONE + u)
                for h in range(2):
                    r = slice(h * DK, (h + 1) * DK)
                    for t in range(QT):
                        last = nc.tensor.matmul(ps_o[r, t * P:(t + 1) * P], v_s[:, t, r],
                                                p_now[:, h, t, :], start=True, stop=True)
                last.then_inc(o_ready, 1)

            with pe.Fori(0, NP) as hp:
                pe.wait_ge(r_added, ONE + hp * NIB)
                project(hp, hp * U)
                scores(hp * U)
                with pe.Fori(0, U - 1) as g:
                    u = hp * U + g
                    project(hp, u + 1)
                    transposes(u)
                    scores(u + 1)
                    values(u)
                transposes(hp * U + (U - 1))
                values(hp * U + (U - 1))
                pe.wait_ge(t_kept, ONE + hp * (2 * U) + 2 * U)
                for ib in range(NIB):
                    p = ib % 2
                    pe.wait_ge(rv_in[p], ONE + hp * (16 * NIB) + (ib // 2) * 32 + 32)
                    pe.wait_ge(r_added, ONE + hp * NIB + max(ib - 1, 0))
                    for i in range(IB):
                        for h in range(2):
                            last = nc.tensor.matmul(
                                (ps_q, ps_k)[p][h * DK:(h + 1) * DK, (IB - 1 - i) * SEQ:(IB - i) * SEQ],
                                rel_v[:, p, h, i, :], p_t[:, h, :, P - 1 - (ib * IB + i)], start=True, stop=True)
                    last.then_inc(r_ready, 1)

        @block.scalar
        def _(act):
            def project(hp, u):
                act.wait_ge(w_in, ONE + hp * 32 + 32)
                act.wait_ge(q_ready, ONE + u + 1)
                act.wait_ge(s_ready, ONE + u * 2)
                nc.scalar.activation(q_t[:, :], ps_q[:, :], ACT.Identity, bias=bqkv[:, 0:1]).then_inc(qk_copied, 1)
                act.wait_ge(k_ready, ONE + u + 1)
                nc.scalar.activation(k_t[:, :], ps_k[:, :], ACT.Identity, bias=bqkv[:, 1:2]).then_inc(qk_copied, 1)

            def exps(u):
                act.wait_ge(t_ready, ONE + u * 2)
                act.wait_ge(rz_done, ONE + u * 2)
                for h in range(2):
                    act.wait_ge(ntop_done, ONE + u * 2 + h + 1)
                    for t in range(QT):
                        last = nc.scalar.activation(p_s[:, h, t, :], s_s[:, h, t, :], ACT.Exp,
                                                    bias=ntop[:, h, t:t + 1], scale=SCALE,
                                                    accum_out=z[:, h, t:t + 1])
                    last.then_inc(exp_done, 1)

            def copies(u):
                act.wait_ge(o_ready, ONE + u)
                act.wait_ge(t_kept, ONE + u * 2)
                for h in range(2):
                    act.wait_ge(t_ready, ONE + u * 2 + h + 1)
                    nc.scalar.copy(p_now[:, h].rearrange("p t n -> p (t n)"), ps_t[h][:, :]).then_inc(t_copied, 1)

            def out(hp, u, g):
                act.wait_ge(o_stored, ONE + hp * 16)
                act.wait_ge(o_ready, ONE + u + 1)
                nc.scalar.activation(o_t[:, ds(g * QT, QT), :].rearrange("p t n -> p (t n)"), ps_o[:, :],
                                     ACT.Identity, bias=bqkv[:, 2:3]).then_inc(o_copied, 1)

            with act.Fori(0, NP) as hp:
                project(hp, hp * U)
                exps(hp * U)
                with act.Fori(0, U - 1) as g:
                    u = hp * U + g
                    project(hp, u + 1)
                    copies(u)
                    exps(u + 1)
                    out(hp, u, g)
                copies(hp * U + (U - 1))
                out(hp, hp * U + (U - 1), U - 1)

        @block.gpsimd
        def _(pool):
            with pool.Fori(0, NP) as hp:
                wait_apart(pool, cst, r_ready, hp * NIB)
                with pool.Fori(0, U) as g:
                    for h in range(2):
                        pool.wait_ge(t_copied, ONE + hp * (2 * U) + g * 2 + h + 1)
                        nc.gpsimd.tensor_copy(p_t[:, h, ds(g * QT, QT), :], p_now[:, h]).then_inc(t_kept, 1)

        @block.vector
        def _(v):
            def value_copy(u):
                v.wait_ge(v_ready, ONE + u + 1)
                v.wait_ge(o_ready, ONE + u)
                nc.vector.tensor_copy(v_s[:, :, :].rearrange("p t n -> p (t n)"), ps_v[:, :]).then_inc(v_copied, 1)

            def bias_and_top(hp, u):
                v.wait_ge(exp_done, ONE + u * 2)
                for h in range(2):
                    v.wait_ge(s_ready, ONE + u * 2 + h + 1)
                    nc.vector.tensor_tensor(s_s[:, h], ps_s[h][:, :].rearrange("p (t n) -> p t n", t=QT),
                                            rel_k[:, ds(hp * 2 + h, 1), :].broadcast_to([P, QT, P]),
                                            ALU.add).then_inc(s_added, 1)
                    v.wait_ge(s_added, ONE + u * 2 + h + 1)
                    nc.vector.tensor_reduce(top[:, h], s_s[:, h], X, ALU.max).then_inc(top_done, 1)
                    v.wait_ge(top_done, ONE + u * 2 + h + 1)
                    nc.vector.tensor_scalar(ntop[:, h], top[:, h], -SCALE, None, ALU.mult).then_inc(ntop_done, 1)

            def divide(u):
                for h in range(2):
                    v.wait_ge(exp_done, ONE + u * 2 + h + 1)
                    nc.vector.reciprocal(rz[:, h], z[:, h]).then_inc(rz_done, 1)
                    v.wait_ge(rz_done, ONE + u * 2 + h + 1)
                    nc.vector.tensor_tensor(p_s[:, h], p_s[:, h],
                                            rz[:, h].unsqueeze(2).broadcast_to([P, QT, P]),
                                            ALU.mult).then_inc(p_done, 1)

            v.wait_ge(rk_in, ONE + 16)
            with v.Fori(0, NP) as hp:
                value_copy(hp * U)
                bias_and_top(hp, hp * U)
                divide(hp * U)
                with v.Fori(0, U - 1) as g:
                    u = hp * U + g
                    bias_and_top(hp, u + 1)
                    divide(u + 1)
                    value_copy(u + 1)
                with v.Fori(0, NIB // 2) as ibb:
                    ib = ibb * 2
                    for p in range(2):
                        n = hp * NIB + ib + p
                        wait_apart(v, cst, r_ready, n + 1)
                        if p == 0:
                            v.wait_ge(o_copied, ONE + (hp + 1) * U)
                        o_view = o_t[:, :, ds((P - IB - p * IB) - ib * IB, IB)].rearrange("p b i -> p i b")
                        nc.vector.tensor_tensor(o_view, (ps_q, ps_k)[p][:, :].rearrange("p (i b) -> p i b", i=IB),
                                                o_view, ALU.add).then_inc(r_added, 1)


def mix_phase(nc, d, cst, scr, keep):
    E, TOP = 16, 4
    with ExitStack() as ctx:
        def sb(name, shape, dt=F32):
            return ctx.enter_context(nc.sbuf_tensor(f"mix_{name}", shape, dt))

        sems = []

        def sem(name):
            sems.append(ctx.enter_context(nc.semaphore(f"mix_{name}")))
            return sems[-1]

        wo = sb("wo", [P, 4, P])
        gate = sb("gate", [P, E])
        b2 = sb("b2", [E + 2, P])
        og = sb("og", [P, 2, 4, W4])
        hg = sb("hg", [P, 2, QT, P])
        stats = sb("stats", [P, QT, 6])
        mv = sb("mv", [P, 2, QT, 2])
        rstd = sb("rstd", [P, 2, QT])
        shift = sb("shift", [P, 2, QT])
        xn = sb("xn", [P, 2, QT, P])
        xt = sb("xt", [P, 2, W4])
        logit = sb("logit", [P, SEQ, E])
        prob = sb("prob", [P, SEQ, E])
        above = sb("above", [P, SEQ, E])
        equal = sb("equal", [P, SEQ, E])
        upto = sb("upto", [P, SEQ, E])
        restart = sb("restart", [P, SEQ, E])
        best = sb("best", [P, SEQ, 8])
        row = sb("row", [P, SEQ])
        row2 = sb("row2", [P, SEQ])
        comb_now = sb("comb_now", [P, 2, QT, E + 2])
        comb_t = sb("comb_t", [E + 2, 2, QT, P])
        ps_y = [ctx.enter_context(nc.psum_tensor(f"mix_ps_y{i}", [P, W4], F32)) for i in range(2)]
        ps_t = [ctx.enter_context(nc.psum_tensor(f"mix_ps_t{i}", [P, W4], F32)) for i in range(2)]
        ps_l = [ctx.enter_context(nc.psum_tensor(f"mix_ps_l{i}", [P, W4], F32)) for i in range(2)]

        w_in = sem("w_in")
        g_in = [sem("g_in0"), sem("g_in1")]
        y_ready = sem("y_ready")
        y_added = sem("y_added")
        stats_done = sem("stats_done")
        var_done = sem("var_done")
        rstd_done = sem("rstd_done")
        shift_done = sem("shift_done")
        xn_done = sem("xn_done")
        t_ready = sem("t_ready")
        t_copied = sem("t_copied")
        t_stored = [sem("t_stored0"), sem("t_stored1")]
        l_ready = sem("l_ready")
        l_copied = sem("l_copied")
        step = sem("router_step")
        less_top = sem("less_top")
        exp_done = sem("exp_done")
        restart_done = sem("restart_done")
        comb_done = sem("comb_done")
        c_ready = sem("c_ready")
        c_copied = sem("c_copied")
        b_ready = sem("b_ready")
        b_added = sem("b_added")

        block = ctx.enter_context(nc.Block())
        HG = G // 2

        @block.sync
        def _(sp):
            for s in sems + [keep["h1_kept"], keep["comb_kept"]]:
                sp.sem_inc(s, ONE)
            sp.dma_start(wo[:, :, :], d["wo"]).then_inc(w_in, 16)
            sp.dma_start(gate[:, :], d["gate"]).then_inc(w_in, 16)
            sp.dma_start(b2[:, :], d["b2"]).then_inc(w_in, 16)
            with sp.Fori(0, HG) as gg:
                for p in range(2):
                    sp.wait_ge(y_ready, ONE + gg * 2)
                    sp.wait_ge(xn_done, ONE + gg * 2)
                    sp.wait_ge(keep["h1_kept"], ONE + gg * 2)
                    sp.dma_start(og[:, p], scr["o"][:, :, ds((gg * 2 + p) * W4, W4)]
                                 .rearrange("a p n -> p a n")).then_inc(g_in[p], 16)
                    sp.dma_start(hg[:, p].rearrange("p q n -> p (q n)"), scr["h"][ds(gg * 2 + p, 1)]
                                 .rearrange("a p n -> (a p) n")).then_inc(g_in[p], 16)
            for p in range(2):
                sp.wait_ge(t_stored[p], ONE + 16 * HG)

        @block.tensor
        def _(pe):
            pe.wait_ge(w_in, ONE + 48)
            with pe.Fori(0, HG) as gg:
                for p in range(2):
                    pe.wait_ge(y_added, ONE + gg * 2)
                    pe.wait_ge(g_in[p], ONE + gg * 32 + 32)
                    for t in range(QT):
                        for a in range(4):
                            last = nc.tensor.matmul(ps_y[p][:, t * P:(t + 1) * P], og[:, p, a, t * P:(t + 1) * P],
                                                    wo[:, a, :], start=(a == 0), stop=(a == 3))
                    last.then_inc(y_ready, 1)
                for p in range(2):
                    pe.wait_ge(t_copied, ONE + gg * 2)
                    pe.wait_ge(xn_done, ONE + gg * 2 + p + 1)
                    for t in range(QT):
                        last = nc.tensor.transpose(ps_t[p][:, t * P:(t + 1) * P], xn[:, p, t, :], cst["ident"][:, :])
                    last.then_inc(t_ready, 1)
                for p in range(2):
                    pe.wait_ge(l_copied, ONE + gg * 2)
                    pe.wait_ge(t_copied, ONE + gg * 2 + p + 1)
                    for t in range(QT):
                        last = nc.tensor.matmul(ps_l[p][:, t * E:(t + 1) * E], xt[:, p, t * P:(t + 1) * P],
                                                gate[:, :], start=True, stop=True)
                    last.then_inc(l_ready, 1)
            with pe.Fori(0, HG) as gg:
                for p in range(2):
                    pe.wait_ge(c_copied, ONE + gg * 2)
                    pe.wait_ge(comb_done, ONE + gg * 2 + p + 1)
                    for t in range(QT):
                        last = nc.tensor.transpose(ps_t[p][0:E + 2, t * P:(t + 1) * P], comb_now[:, p, t, :],
                                                   cst["ident"][:, :])
                    last.then_inc(c_ready, 1)
                for p in range(2):
                    pe.wait_ge(b_added, ONE + gg * 2)
                    pe.wait_ge(c_copied, ONE + gg * 2 + p + 1)
                    for t in range(QT):
                        last = nc.tensor.matmul(ps_y[p][:, t * P:(t + 1) * P], comb_t[:, p, t, :], b2[:, :],
                                                start=True, stop=True)
                    last.then_inc(b_ready, 1)

        @block.scalar
        def _(act):
            with act.Fori(0, HG) as gg:
                for p in range(2):
                    act.wait_ge(shift_done, ONE + gg * 2 + p + 1)
                    act.wait_ge(t_ready, ONE + gg * 2)
                    for t in range(QT):
                        last = nc.scalar.activation(xn[:, p, t, :], hg[:, p, t, :], ACT.Identity,
                                                    bias=shift[:, p, t:t + 1], scale=rstd[:, p, t:t + 1])
                    last.then_inc(xn_done, 1)
                for p in range(2):
                    act.wait_ge(t_stored[p], ONE + gg * 16)
                    act.wait_ge(l_ready, ONE + gg * 2)
                    act.wait_ge(t_ready, ONE + gg * 2 + p + 1)
                    nc.scalar.copy(xt[:, p], ps_t[p][:, :]).then_inc(t_copied, 1)
                for p in range(2):
                    act.wait_ge(t_copied, ONE + gg * 2 + p + 1)
                    act.dma_start(scr["xm"][ds(gg * 2 + p, 1)].rearrange("a p n -> (a p) n"),
                                  xt[:, p]).then_inc(t_stored[p], 16)
            flat = lambda x: x[:, :, :].rearrange("p t e -> p (t e)")
            for n in range(2):
                act.wait_ge(less_top, ONE + n + 1)
                nc.scalar.activation(flat(upto), flat(upto), ACT.Exp).then_inc(exp_done, 1)
            with act.Fori(0, HG) as gg:
                for p in range(2):
                    act.wait_ge(b_ready, ONE + gg * 2)
                    act.wait_ge(c_ready, ONE + gg * 2 + p + 1)
                    nc.scalar.copy(comb_t[:, p].rearrange("p t n -> p (t n)"),
                                   ps_t[p][0:E + 2, :]).then_inc(c_copied, 1)

        @block.gpsimd
        def _(pool):
            for name in ("w1", "w2", "b1"):
                pool.dma_start(keep[name][:], d[name]).then_inc(keep["w_in"], 16)
            nc.gpsimd.memset(restart[:, :, :], 1.0).then_inc(restart_done, 1)
            pool.wait_ge(restart_done, ONE + 1)
            nc.gpsimd.memset(restart[:, :, 0:1], 0.0).then_inc(restart_done, 1)
            nc.gpsimd.memset(comb_now[:, :, :, :], 0.5).then_inc(restart_done, 1)
            with pool.Fori(0, HG) as gg:
                for p in range(2):
                    pool.wait_ge(var_done, ONE + gg * 2 + p + 1)
                    nc.gpsimd.tensor_tensor(rstd[:, p], rstd[:, p], cst["neg_half"][:, 0:QT],
                                            ALU.pow).then_inc(rstd_done, 1)

        @block.vector
        def _(v):
            with v.Fori(0, HG) as gg:
                for p in range(2):
                    n = gg * 2 + p
                    v.wait_ge(y_ready, ONE + n + 1)
                    nc.vector.tensor_tensor(hg[:, p].rearrange("p q n -> p (q n)"), ps_y[p][:, :],
                                            hg[:, p].rearrange("p q n -> p (q n)"), ALU.add).then_inc(y_added, 1)
                    v.wait_ge(y_added, ONE + n + 1)
                    for t in range(QT):
                        last = nc.vector.bn_stats(stats[:, t, :], hg[:, p, t, :])
                    last.then_inc(stats_done, 1)
                    wait_apart(v, cst, stats_done, n + 1)
                    for t in range(QT):
                        last = nc.vector.bn_aggr(mv[:, p, t, :], stats[:, t, :])
                    last.then_inc(step, 1)
                    v.wait_ge(xn_done, ONE + gg * 2)
                    v.wait_ge(step, ONE + n + 1)
                    nc.vector.tensor_scalar(rstd[:, p], mv[:, p, :, 1], EPS, None, ALU.add).then_inc(var_done, 1)
                    nc.vector.tensor_copy(keep["h1"][:, ds(n * QT, QT), :], hg[:, p]).then_inc(keep["h1_kept"], 1)
                for p in range(2):
                    v.wait_ge(rstd_done, ONE + gg * 2 + p + 1)
                    nc.vector.scalar_tensor_tensor(out=shift[:, p], in0=mv[:, p, :, 0], scalar=-1.0, in1=rstd[:, p],
                                                   op0=ALU.mult, op1=ALU.mult).then_inc(shift_done, 1)
                for p in range(2):
                    v.wait_ge(l_ready, ONE + gg * 2 + p + 1)
                    nc.vector.tensor_copy(logit[:, ds((gg * 2 + p) * QT, QT), :],
                                          ps_l[p][:, 0:QT * E].rearrange("p (t e) -> p t e", e=E)).then_inc(l_copied, 1)
            wide = [P, SEQ, E]
            at = [G]

            def done(ins):
                at[0] += 1
                ins.then_inc(step, 1)
                v.wait_ge(step, ONE + at[0])

            def rows(x):
                return x.unsqueeze(2).broadcast_to(wide)

            v.wait_ge(l_copied, ONE + G)
            done(nc.vector.tensor_reduce(row[:, :], logit[:, :, :], X, ALU.max))
            nc.vector.tensor_tensor(upto[:, :, :], logit[:, :, :], rows(row[:, :]), ALU.subtract).then_inc(less_top, 1)
            v.wait_ge(exp_done, ONE + 1)
            done(nc.vector.tensor_reduce(row[:, :], upto[:, :, :], X, ALU.add))
            done(nc.vector.reciprocal(row2[:, :], row[:, :]))
            done(nc.vector.tensor_tensor(prob[:, :, :], upto[:, :, :], rows(row2[:, :]), ALU.mult))
            for t in range(SEQ):
                last = nc.vector.max(best[:, t, :], prob[:, t, :])
            done(last)
            done(nc.vector.tensor_tensor(above[:, :, :], prob[:, :, :], rows(best[:, :, TOP - 1]), ALU.is_gt))
            done(nc.vector.tensor_tensor(equal[:, :, :], prob[:, :, :], rows(best[:, :, TOP - 1]), ALU.is_equal))
            done(nc.vector.tensor_reduce(row[:, :], above[:, :, :], X, ALU.add))
            done(nc.vector.tensor_scalar(row2[:, :], row[:, :], -1.0, float(TOP), ALU.mult, ALU.add))
            v.wait_ge(restart_done, ONE + 3)
            flat = lambda x: x[:, :, :].rearrange("p t e -> p (t e)")
            done(nc.vector.tensor_tensor_scan(flat(logit), flat(restart), flat(equal), 0.0, ALU.mult, ALU.add))
            done(nc.vector.tensor_tensor(logit[:, :, :], logit[:, :, :], rows(row2[:, :]), ALU.is_le))
            done(nc.vector.tensor_tensor(logit[:, :, :], logit[:, :, :], equal[:, :, :], ALU.mult))
            done(nc.vector.tensor_tensor(above[:, :, :], above[:, :, :], logit[:, :, :], ALU.add))
            nc.vector.tensor_tensor(upto[:, :, :], prob[:, :, :], rows(best[:, :, 0]), ALU.subtract).then_inc(less_top, 1)
            v.wait_ge(exp_done, ONE + 2)
            done(nc.vector.tensor_tensor(upto[:, :, :], upto[:, :, :], above[:, :, :], ALU.mult))
            done(nc.vector.tensor_reduce(row[:, :], upto[:, :, :], X, ALU.add))
            done(nc.vector.reciprocal(row2[:, :], row[:, :]))
            nc.vector.tensor_tensor(keep["comb"][:, :, :], upto[:, :, :], rows(row2[:, :]), ALU.mult).then_inc(keep["comb_kept"], 1)
            v.wait_ge(keep["comb_kept"], ONE + 1)
            with v.Fori(0, HG) as gg:
                for p in range(2):
                    v.wait_ge(c_ready, ONE + gg * 2)
                    nc.vector.tensor_copy(comb_now[:, p, :, 0:E],
                                          keep["comb"][:, ds((gg * 2 + p) * QT, QT), :]).then_inc(comb_done, 1)
                for p in range(2):
                    t = ds((gg * 2 + p) * QT, QT)
                    v.wait_ge(b_ready, ONE + gg * 2 + p + 1)
                    nc.vector.tensor_tensor(keep["h1"][:, t, :], ps_y[p][:, :].rearrange("p (t n) -> p t n", t=QT),
                                            keep["h1"][:, t, :], ALU.add).then_inc(b_added, 1)


def tower_phase(nc, d, cst, scr, keep, out):
    E, SH, F = 16, 2, 512
    S = E + SH
    FC = F // P
    H1, D1 = 8, 16
    N_IN, N_PR, D_PV, N_OUT = 512, 256, 64, 512
    K_IN, K_PR, K_OUT = 64, 128, 64
    R_IN, R_PR, R_OUT = K_IN // 8, K_PR // 8, K_OUT // 8
    SCALE = float(P) ** -0.5
    GONE, IS_GONE = -3e38, -1e38
    ND = QT * (R_IN + R_PR + R_OUT)
    with ExitStack() as ctx:
        def sb(name, shape, dt=F32):
            return ctx.enter_context(nc.sbuf_tensor(f"tow_{name}", shape, dt))

        sems = []

        def sem(name):
            sems.append(ctx.enter_context(nc.semaphore(f"tow_{name}")))
            return sems[-1]

        w1, w2, b1 = keep["w1"], keep["w2"], keep["b1"]
        h1, comb = keep["h1"], keep["comb"]
        xm = sb("xm", [P, W4])
        hid = sb("hid", [P, 2, FC, W4])
        wqkv = sb("wqkv1", [P, 3 * P])
        bqkv = sb("bqkv1", [P, 3 * P])
        wo = sb("wo1", [P, P])
        bo = sb("bo1", [1, P])
        gb = sb("gb", [P, 4])
        odd = sb("odd", [P, 2])
        gbk = sb("gbk", [P, 2, 2])
        stats = sb("stats", [P, 2 * QT, 6])
        mv = sb("mv", [P, 2 * QT, 2])
        pt = [sb(f"pool_tmp{i}", [P, 2 * QT]) for i in range(6)]
        sx = sb("sx", [P, QT, P])
        xt = sb("xt", [P, W4])
        qkv = sb("qkv", [P, QT, 3 * P])
        qk_n = sb("qk_n", [P, 2, QT, P])
        q_t = sb("q_t", [P, W4])
        k_t = sb("k_t", [P, 2, W4])
        top = sb("top", [P, 2, 4])
        ntop = sb("ntop", [P, 2, 4])
        z = sb("z", [P, QT, H1])
        rz = sb("rz", [P, QT, H1])
        p_s = sb("p_s", [P, 2, 4, P])
        p_t = sb("p_t", [P, 4, P])
        w_in_t = sb("w_in_t", [P, N_IN])
        w_pr_t = sb("w_pr_t", [P, N_IN // P, N_PR])
        w_val = sb("w_val", [P, N_PR // P, D_PV])
        w_oi_t = sb("w_oi_t", [D_PV, N_OUT])
        w_out = sb("w_out", [P, N_OUT // P, P])
        acts = sb("acts", [P, QT, N_IN])
        pacts = sb("pacts", [P, QT, N_PR])
        pexp = sb("pexp", [P, QT, N_PR])
        work = sb("work", [P, 2, N_IN])
        best = sb("best", [P, 2, 8])
        ptop = sb("ptop", [P, QT])
        chosen = sb("chosen", [P, 2, N_IN])
        ch_t = sb("ch_t", [P, N_IN])
        zp = sb("zp", [P, QT])
        rzp = sb("rzp", [P, QT])
        agg_t = sb("agg_t", [D_PV, P])
        h_out = sb("h_out", [P, QT, P])
        bank = lambda name: ctx.enter_context(nc.psum_tensor(f"tow_{name}", [P, W4], F32))
        ps_h = [bank("ps_h0"), bank("ps_h1")]
        ps_y = [bank("ps_y0"), bank("ps_y1")]
        x0, x1, x2, x3 = [bank(f"ps_x{i}") for i in range(4)]

        names = """c_in c_half gbk_done xm_in h_ready hid_done y_ready y_added a_stats a_var a_pool a_scale a_silu a_t
            a_xt a_qkv a_bias a_stats2 a_var2 a_pool2 a_rstd2 a_norm a_qkt a_qkc a_s a_top a_ntop a_exp a_pt a_ptc a_pv
            a_rz a_o a_silu2 a_ot a_otc a_y h2_done f_stats f_var f_pool f_rstd f_norm f_t f_xt f_act f_acted found
            cleared chosen_done f_ct f_ctc f_pr f_practed f_exp f_rz f_agg f_aggc f_oact f_oacted f_out f_res
            out_done""".split()
        sm = {n: sem(n) for n in names}
        block = ctx.enter_context(nc.Block())

        R1 = {4: (0, 3), 5: (3, 7), 6: (7, 10), 7: (10, 13), 8: (13, 16)}
        R2 = {9: (0, 6), 10: (6, 13), 11: (13, 19), 12: (19, 26), 13: (26, 32)}
        R3 = {14: (0, 3), 15: (3, 7), 16: (7, 10), 17: (10, 13), 18: (13, 16)}
        S1 = {4: (0, 1, 2, 3)}
        S2 = {7: (0, 1), 9: (2, 3)}
        SE = {9: (0, 1), 11: (2, 3)}
        S3 = {12: (0, 1), 14: (2, 3)}
        S4 = {17: (0, 1), 18: (2, 3)}

        @block.sync
        def _(sp):
            for s in sems:
                sp.sem_inc(s, ONE)
            for dst, src in ((wqkv[:, :], "wqkv1"), (wo[:, :], "wo1"), (bo[:, :], "bo1"), (gb[:, :], "gb"),
                             (odd[:, :], "odd"), (w_in_t[:, :], "ip"), (w_pr_t[:, :, :], "piw"),
                             (w_val[:, :, :], "pval"), (w_oi_t[:, :], "oiw"), (w_out[:, :, :], "op")):
                sp.dma_start(dst, d[src]).then_inc(sm["c_in"], 16)
            sp.dma_start(bqkv[:, :], d["bqkv1"].partition_broadcast(P)).then_inc(sm["c_in"], 16)

            def load(k):
                sp.wait_ge(sm["h_ready"], ONE + k * (S * FC))
                sp.dma_start(xm[:, :], scr["xm"][ds(k, 1)].rearrange("a p n -> (a p) n")).then_inc(sm["xm_in"], 16)

            def store(j):
                sp.wait_ge(sm["f_res"], ONE + j * QT + QT)
                sp.dma_start(out[ds(j * QT, QT), :, :].rearrange("t p n -> p t n"),
                             h_out[:, :, :]).then_inc(sm["out_done"], 16)

            load(0)
            load(1)
            with sp.Fori(2, G) as k:
                load(k)
                store(k - 2)
            store(G - 2)
            store(G - 1)
            sp.wait_ge(sm["out_done"], ONE + 16 * G)

        @block.gpsimd
        def _(pool):
            nh = cst["neg_half"]
            with pool.Fori(0, G) as j:
                n = [0]

                def done(ins):
                    n[0] += 1
                    ins.then_inc(sm["a_pool"], 1)
                    wait_apart(pool, cst, sm["a_pool"], j * 8 + n[0])

                wait_apart(pool, cst, sm["a_var"], j + 1)
                m, var = mv[:, 0:QT, 0], mv[:, 0:QT, 1]
                r1, sq, r2, sc, sh = (t[:, 0:QT] for t in pt[0:5])
                done(nc.gpsimd.tensor_scalar(sq, var, EPS, None, ALU.add))
                done(nc.gpsimd.tensor_tensor(r1, sq, nh[:, 0:QT], ALU.pow))
                done(nc.gpsimd.tensor_tensor(sq, r1, r1, ALU.mult))
                done(nc.gpsimd.tensor_tensor(sq, sq, var, ALU.mult))
                done(nc.gpsimd.tensor_scalar(sq, sq, EPS, None, ALU.add))
                done(nc.gpsimd.tensor_tensor(r2, sq, nh[:, 0:QT], ALU.pow))
                done(nc.gpsimd.tensor_tensor(sc, r1, r2, ALU.mult))
                done(nc.gpsimd.tensor_tensor(sh, m, sc, ALU.mult))
                nc.gpsimd.tensor_scalar(sh, sh, -1.0, None, ALU.mult).then_inc(sm["a_scale"], 1)
                wait_apart(pool, cst, sm["a_var2"], j + 1)
                nc.gpsimd.tensor_scalar(pt[5][:, :], mv[:, :, 1], EPS, None, ALU.add).then_inc(sm["a_pool2"], 1)
                pool.wait_ge(sm["a_pool2"], ONE + j * 3 + 1)
                nc.gpsimd.tensor_tensor(pt[5][:, :], pt[5][:, :], nh[:, 0:2 * QT], ALU.pow).then_inc(sm["a_pool2"], 1)
                pool.wait_ge(sm["a_pool2"], ONE + j * 3 + 2)
                nc.gpsimd.tensor_tensor(pt[4][:, :], mv[:, :, 0], pt[5][:, :], ALU.mult).then_inc(sm["a_pool2"], 1)
                wait_apart(pool, cst, sm["a_pool2"], j * 3 + 3)
                nc.gpsimd.tensor_scalar(pt[4][:, :], pt[4][:, :], -1.0, None, ALU.mult).then_inc(sm["a_rstd2"], 1)
                wait_apart(pool, cst, sm["f_var"], j + 1)
                nc.gpsimd.tensor_scalar(sq, var, EPS, None, ALU.add).then_inc(sm["f_pool"], 1)
                pool.wait_ge(sm["f_pool"], ONE + j * 3 + 1)
                nc.gpsimd.tensor_tensor(sc, sq, nh[:, 0:QT], ALU.pow).then_inc(sm["f_pool"], 1)
                pool.wait_ge(sm["f_pool"], ONE + j * 3 + 2)
                nc.gpsimd.tensor_tensor(sh, m, sc, ALU.mult).then_inc(sm["f_pool"], 1)
                wait_apart(pool, cst, sm["f_pool"], j * 3 + 3)
                nc.gpsimd.tensor_scalar(sh, sh, -1.0, None, ALU.mult).then_inc(sm["f_rstd"], 1)

        @block.tensor
        def _(pe):
            mm, tr, ident = nc.tensor.matmul, nc.tensor.transpose, cst["ident"]
            col = lambda t: slice(t * P, (t + 1) * P)

            def hidden(k, s):
                if s == 0:
                    pe.wait_ge(sm["xm_in"], ONE + k * 16 + 16)
                for c in range(FC):
                    n = s * FC + c
                    pe.wait_ge(sm["hid_done"], ONE + k * (S * FC) + max(n - 1, 0))
                    mm(ps_h[n % 2][:, :], w1[:, s, col(c)], xm[:, :], start=True, stop=True).then_inc(sm["h_ready"], 1)

            def expert_out(k, s):
                pe.wait_ge(sm["hid_done"], ONE + k * (S * FC) + (s + 1) * FC)
                pe.wait_ge(sm["y_added"], ONE + k * S + max(s - 1, 0))
                for t in range(QT):
                    for c in range(FC):
                        last = mm(ps_y[s % 2][:, col(t)], hid[:, s % 2, c, col(t)], w2[:, s, c, :],
                                  start=(c == 0), stop=(c == FC - 1))
                last.then_inc(sm["y_ready"], 1)

            def attn_in(j):
                pe.wait_ge(sm["f_oacted"], ONE + j * QT)
                pe.wait_ge(sm["a_silu"], ONE + j + 1)
                for t in range(QT):
                    last = tr(x0[:, col(t)], sx[:, t, :], ident[:, :])
                last.then_inc(sm["a_t"], 1)

            def attn_qkv(j):
                pe.wait_ge(sm["f_ctc"], ONE + j * (3 * QT))
                pe.wait_ge(sm["a_xt"], ONE + j + 1)
                for t in range(QT):
                    pe.wait_ge(sm["a_bias"], ONE + j * QT + max(t - 1, 0))
                    mm((x1, x2)[t % 2][:, 0:3 * P], xt[:, col(t)], wqkv[:, :],
                       start=True, stop=True).then_inc(sm["a_qkv"], 1)

            def attn_turn(j):
                pe.wait_ge(sm["f_res"], ONE + j * QT)
                pe.wait_ge(sm["a_norm"], ONE + j + 1)
                for i, x in enumerate((x0, x3)):
                    for t in range(QT):
                        last = tr(x[:, col(t)], qk_n[:, i, t, :], ident[:, :])
                    last.then_inc(sm["a_qkt"], 1)

            def unit(u):
                r = u % 4
                return r, [(2 * (u // 4) + a, b, 2 * r + b) for a in range(2) for b in range(2)]

            def attn_scores(j, u):
                if u >= 2:
                    pe.wait_ge(sm["a_exp"], ONE + j * 8 + u - 1)
                else:
                    pe.wait_ge(sm["a_qkc"], ONE + j * 3 + 3)
                    pe.wait_ge(sm["a_bias"], ONE + j * QT + QT)
                r, cells = unit(u)
                rows = slice(32 * r, 32 * r + 32)
                for c, (t, b, h) in enumerate(cells):
                    last = mm((x0, x1)[u % 2][:, col(c)], q_t[rows, col(t)], k_t[rows, b, col(t)],
                              start=True, stop=True)
                last.then_inc(sm["a_s"], 1)

            def attn_values(j, u):
                pe.wait_ge(sm["a_exp"], ONE + j * 8 + u + 1)
                pe.wait_ge(sm["a_ptc"], ONE + j * 8 + u)
                for c in range(4):
                    last = tr(x2[:, col(c)], p_s[:, u % 2, c, :], ident[:, :])
                last.then_inc(sm["a_pt"], 1)

            def attn_pv(j, u):
                pe.wait_ge(sm["a_ptc"], ONE + j * 8 + u + 1)
                for c, (t, b, h) in enumerate(unit(u)[1]):
                    last = mm(x3[:, t * P + h * D1:t * P + (h + 1) * D1], p_t[:, c, :],
                              qkv[:, t, 2 * P + h * D1:2 * P + (h + 1) * D1], start=True, stop=True)
                last.then_inc(sm["a_pv"], 1)

            def attn(j):
                attn_scores(j, 0)
                attn_scores(j, 1)
                for u in range(8):
                    attn_values(j, u)
                    if u < 6:
                        attn_scores(j, u + 2)
                    attn_pv(j, u)

            def attn_out(j):
                pe.wait_ge(sm["a_silu2"], ONE + j + 1)
                for t in range(QT):
                    last = tr(x0[:, col(t)], sx[:, t, :], ident[:, :])
                last.then_inc(sm["a_ot"], 1)
                pe.wait_ge(sm["a_otc"], ONE + j + 1)
                for t in range(QT):
                    mm(x1[:, col(t)], xt[:, col(t)], wo[:, :], start=True, stop=False)
                    last = mm(x1[:, col(t)], cst["ones_row"][:, :], bo[:, :], start=False, stop=True)
                last.then_inc(sm["a_y"], 1)

            def ffn_in(j):
                pe.wait_ge(sm["f_norm"], ONE + j + 1)
                for t in range(QT):
                    last = tr(x2[:, col(t)], sx[:, t, :], ident[:, :])
                last.then_inc(sm["f_t"], 1)

            def input_acts(j, t):
                pe.wait_ge(sm["f_xt"], ONE + j + 1)
                if t == 1:
                    pe.wait_ge(sm["h2_done"], ONE + j + 1)
                if t >= 2:
                    pe.wait_ge(sm["f_acted"], ONE + j * QT + t - 1)
                mm((x0, x1)[t % 2][:, :], xt[:, col(t)], w_in_t[:, :], start=True, stop=True).then_inc(sm["f_act"], 1)

            def turn_chosen(j, i, t, chunks):
                n = i * QT + t
                pe.wait_ge(sm["chosen_done"], ONE + j * (3 * QT) + n + 1)
                if n:
                    pe.wait_ge(sm["f_ctc"], ONE + j * (3 * QT) + n)
                for c in range(chunks):
                    last = tr(x2[:, col(c)], chosen[:, t % 2, col(c)], ident[:, :])
                last.then_inc(sm["f_ct"], 1)
                pe.wait_ge(sm["f_ctc"], ONE + j * (3 * QT) + n + 1)

            def process_acts(j, t):
                turn_chosen(j, 0, t, N_IN // P)
                pe.wait_ge(sm["f_practed"], ONE + j * QT + t)
                for c in range(N_IN // P):
                    last = mm(x3[:, 0:N_PR], ch_t[:, col(c)], w_pr_t[:, c, :], start=(c == 0), stop=(c == N_IN // P - 1))
                last.then_inc(sm["f_pr"], 1)

            def output_acts(j, t):
                turn_chosen(j, 1, t, N_PR // P)
                pe.wait_ge(sm["f_practed"], ONE + j * QT + QT)
                for c in range(N_PR // P):
                    last = mm(x3[0:D_PV, 0:P], w_val[:, c, :], ch_t[:, col(c)], start=(c == 0), stop=(c == N_PR // P - 1))
                last.then_inc(sm["f_agg"], 1)
                pe.wait_ge(sm["f_aggc"], ONE + j * QT + t + 1)
                if t >= 2:
                    pe.wait_ge(sm["f_oacted"], ONE + j * QT + t - 1)
                mm((x0, x1)[t % 2][:, :], agg_t[:, :], w_oi_t[:, :], start=True, stop=True).then_inc(sm["f_oact"], 1)

            def outputs(j, t):
                turn_chosen(j, 2, t, N_OUT // P)
                pe.wait_ge(sm["f_res"], ONE + j * QT + t)
                for c in range(N_OUT // P):
                    last = mm(x3[:, 0:P], ch_t[:, col(c)], w_out[:, c, :], start=(c == 0), stop=(c == N_OUT // P - 1))
                last.then_inc(sm["f_out"], 1)

            def second_layer(j, s):
                if s == 0:
                    attn_in(j)
                if s == 1:
                    attn_qkv(j)
                if s == 2:
                    attn_turn(j)
                    attn(j)
                if s == 3:
                    attn_out(j)
                    ffn_in(j)
                for t in S1.get(s, ()):
                    input_acts(j, t)
                for t in S2.get(s, ()):
                    process_acts(j, t)
                for t in S3.get(s, ()):
                    output_acts(j, t)
                for t in S4.get(s, ()):
                    outputs(j, t)

            def experts(k, s):
                if s < S:
                    hidden(k, s)
                if s:
                    expert_out(k, s - 1)

            pe.wait_ge(keep["w_in"], 16 * keep["w_loads"])
            pe.wait_ge(sm["c_half"], ONE + 1)
            pe.wait_ge(sm["c_in"], ONE + 16 * 11)
            for s in range(S + 1):
                experts(0, s)
            with pe.Fori(1, G) as k:
                for s in range(S + 1):
                    experts(k, s)
                    second_layer(k - 1, s)
            for s in range(S + 1):
                second_layer(G - 1, s)

        @block.scalar
        def _(act):
            def hidden(k, s):
                act.wait_ge(sm["y_ready"], ONE + k * S + max(s - 1, 0))
                for c in range(FC):
                    n = s * FC + c
                    act.wait_ge(sm["h_ready"], ONE + k * (S * FC) + n + 1)
                    nc.scalar.activation(hid[:, s % 2, c, :], ps_h[n % 2][:, :], ACT.Gelu,
                                         bias=b1[:, s, c:c + 1]).then_inc(sm["hid_done"], 1)

            def attn(j):
                def exps(u):
                    if u >= 2:
                        act.wait_ge(sm["a_pt"], ONE + j * 8 + u - 1)
                    act.wait_ge(sm["a_ntop"], ONE + j * 8 + u + 1)
                    r, tp = u % 4, u // 4
                    for c in range(4):
                        t, h = 2 * tp + c // 2, 2 * r + c % 2
                        last = nc.scalar.activation(p_s[:, u % 2, c, :], (x0, x1)[u % 2][:, c * P:(c + 1) * P],
                                                    ACT.Exp, bias=ntop[:, u % 2, c:c + 1], scale=SCALE,
                                                    accum_out=z[:, t, h:h + 1])
                    last.then_inc(sm["a_exp"], 1)

                def copy(u):
                    act.wait_ge(sm["a_pt"], ONE + j * 8 + u + 1)
                    act.wait_ge(sm["a_pv"], ONE + j * 8 + u)
                    nc.scalar.copy(p_t[:, :, :].rearrange("p c n -> p (c n)"), x2[:, :]).then_inc(sm["a_ptc"], 1)

                act.wait_ge(sm["a_rz"], ONE + j)
                exps(0)
                for u in range(8):
                    if u < 7:
                        exps(u + 1)
                    copy(u)

            def second_layer(j, s):
                def turn_chosen(i, t, n):
                    m = i * QT + t
                    act.wait_ge(sm["f_ct"], ONE + j * (3 * QT) + m + 1)
                    if i == 0:
                        act.wait_ge(sm["f_pr"], ONE + j * QT + t)
                    if i == 1:
                        act.wait_ge(sm["f_agg"], ONE + j * QT + t)
                        act.wait_ge(sm["f_pr"], ONE + j * QT + QT)
                    if i == 2:
                        act.wait_ge(sm["f_out"], ONE + j * QT + t)
                        act.wait_ge(sm["f_agg"], ONE + j * QT + QT)
                    nc.scalar.copy(ch_t[:, 0:n], x2[:, 0:n]).then_inc(sm["f_ctc"], 1)

                if s == 0:
                    act.wait_ge(sm["a_scale"], ONE + j + 1)
                    act.wait_ge(sm["f_t"], ONE + j)
                    for t in range(QT):
                        last = nc.scalar.activation(sx[:, t, :], h1[:, ds(j * QT + t, 1), :].rearrange("p a n -> p (a n)"),
                                                    ACT.Silu, bias=pt[4][:, t:t + 1], scale=pt[3][:, t:t + 1])
                    last.then_inc(sm["a_silu"], 1)
                    act.wait_ge(sm["a_t"], ONE + j + 1)
                    act.wait_ge(sm["f_act"], ONE + j * QT)
                    nc.scalar.copy(xt[:, :], x0[:, :]).then_inc(sm["a_xt"], 1)
                if s == 2:
                    act.wait_ge(sm["a_qkt"], ONE + j * 2 + 1)
                    act.wait_ge(sm["a_s"], ONE + j * 8)
                    nc.scalar.activation(q_t[:, :], x0[:, :], ACT.Identity, bias=gb[:, 1:2], scale=gb[:, 0:1]).then_inc(sm["a_qkc"], 1)
                    act.wait_ge(sm["a_qkt"], ONE + j * 2 + 2)
                    for b in range(2):
                        nc.scalar.activation(k_t[:, b, :], x3[:, :], ACT.Identity, bias=gbk[:, 1, b:b + 1],
                                             scale=gbk[:, 0, b:b + 1]).then_inc(sm["a_qkc"], 1)
                    attn(j)
                if s == 3:
                    act.wait_ge(sm["a_o"], ONE + j + 1)
                    act.wait_ge(sm["a_t"], ONE + j + 1)
                    flat = sx[:, :, :].rearrange("p t n -> p (t n)")
                    nc.scalar.activation(flat, qk_n[:, 0].rearrange("p t n -> p (t n)"), ACT.Silu).then_inc(sm["a_silu2"], 1)
                    act.wait_ge(sm["a_ot"], ONE + j + 1)
                    act.wait_ge(sm["a_qkv"], ONE + j * QT + QT)
                    nc.scalar.copy(xt[:, :], x0[:, :]).then_inc(sm["a_otc"], 1)
                    act.wait_ge(sm["f_t"], ONE + j + 1)
                    act.wait_ge(sm["a_y"], ONE + j + 1)
                    nc.scalar.copy(xt[:, :], x2[:, :]).then_inc(sm["f_xt"], 1)
                for t in S1.get(s, ()):
                    act.wait_ge(sm["f_act"], ONE + j * QT + t + 1)
                    act.wait_ge(sm["chosen_done"], ONE + j * (3 * QT))
                    nc.scalar.activation(acts[:, t, :], (x0, x1)[t % 2][:, :], ACT.Gelu).then_inc(sm["f_acted"], 1)
                for t in S2.get(s, ()):
                    turn_chosen(0, t, N_IN)
                    act.wait_ge(sm["f_pr"], ONE + j * QT + t + 1)
                    nc.scalar.activation(pacts[:, t, :], x3[:, 0:N_PR], ACT.Gelu).then_inc(sm["f_practed"], 1)
                for t in SE.get(s, ()):
                    act.wait_ge(sm["cleared"], ONE + j * ND + QT * R_IN + (t // 2) * (2 * R_PR) + t % 2 + 1)
                    nc.scalar.activation(pexp[:, t, :], pacts[:, t, :], ACT.Exp, bias=ptop[:, t:t + 1]).then_inc(sm["f_exp"], 1)
                for t in S3.get(s, ()):
                    turn_chosen(1, t, N_PR)
                    act.wait_ge(sm["f_agg"], ONE + j * QT + t + 1)
                    act.wait_ge(sm["f_oact"], ONE + j * QT + t)
                    nc.scalar.copy(agg_t[:, :], x3[0:D_PV, 0:P]).then_inc(sm["f_aggc"], 1)
                    act.wait_ge(sm["f_oact"], ONE + j * QT + t + 1)
                    act.wait_ge(sm["f_rz"], ONE + j * QT + t + 1)
                    nc.scalar.activation(acts[:, t, :], (x0, x1)[t % 2][:, :], ACT.Gelu, scale=rzp[:, t:t + 1]).then_inc(sm["f_oacted"], 1)
                for t in S4.get(s, ()):
                    turn_chosen(2, t, N_OUT)

            act.wait_ge(keep["w_in"], 16 * keep["w_loads"])
            act.wait_ge(sm["c_in"], ONE + 16 * 11)
            act.wait_ge(sm["gbk_done"], ONE + 2)
            for s in range(S):
                hidden(0, s)
            with act.Fori(1, G) as k:
                for s in range(S + 1):
                    if s < S:
                        hidden(k, s)
                    second_layer(k - 1, s)
            for s in range(S + 1):
                second_layer(G - 1, s)

        @block.vector
        def _(v):
            tt, ts, stt = nc.vector.tensor_tensor, nc.vector.tensor_scalar, nc.vector.scalar_tensor_tensor
            four = lambda x: x[:, :].rearrange("p (t n) -> p t n", t=QT)
            tile = lambda j, t: h1[:, ds(j * QT + t, 1), :].rearrange("p a n -> p (a n)")
            group = lambda j: h1[:, ds(j * QT, QT), :]

            def add_expert(k, s):
                v.wait_ge(sm["y_ready"], ONE + k * S + s + 1)
                v.wait_ge(sm["y_added"], ONE + k * S + s)
                if s < SH:
                    tt(group(k), four(ps_y[s % 2]), group(k), ALU.add).then_inc(sm["y_added"], 1)
                    return
                for t in range(QT):
                    last = stt(out=tile(k, t), in0=ps_y[s % 2][:, t * P:(t + 1) * P],
                               scalar=comb[:, ds(k * QT + t, 1), s - SH], in1=tile(k, t), op0=ALU.mult, op1=ALU.add)
                last.then_inc(sm["y_added"], 1)

            def attn_first(j):
                v.wait_ge(sm["y_added"], ONE + j * S + S)
                wait_apart(v, cst, sm["f_rstd"], j)
                for t in range(QT):
                    last = nc.vector.bn_stats(stats[:, t, :], tile(j, t))
                last.then_inc(sm["a_stats"], 1)
                wait_apart(v, cst, sm["a_stats"], j + 1)
                for t in range(QT):
                    last = nc.vector.bn_aggr(mv[:, t, :], stats[:, t, :])
                last.then_inc(sm["a_var"], 1)

            def attn_qkv(j):
                v.wait_ge(sm["a_pv"], ONE + j * 8)
                for t in range(QT):
                    v.wait_ge(sm["a_qkv"], ONE + j * QT + t + 1)
                    tt(qkv[:, t, :], (x1, x2)[t % 2][:, 0:3 * P], bqkv[:, :], ALU.add).then_inc(sm["a_bias"], 1)
                v.wait_ge(sm["a_bias"], ONE + j * QT + QT)
                v.wait_ge(sm["a_scale"], ONE + j + 1)
                for i in range(2):
                    for t in range(QT):
                        last = nc.vector.bn_stats(stats[:, i * QT + t, :], qkv[:, t, i * P:(i + 1) * P])
                last.then_inc(sm["a_stats2"], 1)
                wait_apart(v, cst, sm["a_stats2"], j + 1)
                for i in range(2 * QT):
                    last = nc.vector.bn_aggr(mv[:, i, :], stats[:, i, :])
                last.then_inc(sm["a_var2"], 1)
                v.wait_ge(sm["a_rstd2"], ONE + j + 1)
                for i in range(2):
                    for t in range(QT):
                        n = i * QT + t
                        last = ts(qk_n[:, i, t, :], qkv[:, t, i * P:(i + 1) * P], pt[5][:, n:n + 1], pt[4][:, n:n + 1],
                                  ALU.mult, ALU.add)
                last.then_inc(sm["a_norm"], 1)

            def attn(j):
                for u in range(8):
                    v.wait_ge(sm["a_s"], ONE + j * 8 + u + 1)
                    if u >= 2:
                        v.wait_ge(sm["a_exp"], ONE + j * 8 + u - 1)
                    nc.vector.tensor_reduce(top[:, u % 2, :], four((x0, x1)[u % 2]), X, ALU.max).then_inc(sm["a_top"], 1)
                    v.wait_ge(sm["a_top"], ONE + j * 8 + u + 1)
                    ts(ntop[:, u % 2, :], top[:, u % 2, :], -SCALE, None, ALU.mult).then_inc(sm["a_ntop"], 1)
                v.wait_ge(sm["a_exp"], ONE + j * 8 + 8)
                nc.vector.reciprocal(rz[:, :, :].rearrange("p t h -> p (t h)"),
                                     z[:, :, :].rearrange("p t h -> p (t h)")).then_inc(sm["a_rz"], 1)

            def attn_out(j):
                v.wait_ge(sm["a_rz"], ONE + j + 1)
                v.wait_ge(sm["a_pv"], ONE + j * 8 + 8)
                tt(qk_n[:, 0].rearrange("p t (h d) -> p (t h) d", h=H1), x3[:, :].rearrange("p (c d) -> p c d", d=D1),
                   rz[:, :, :].rearrange("p t h -> p (t h)").unsqueeze(2).broadcast_to([P, QT * H1, D1]),
                   ALU.mult).then_inc(sm["a_o"], 1)
                v.wait_ge(sm["a_y"], ONE + j + 1)
                tt(group(j), four(x1), group(j), ALU.add).then_inc(sm["h2_done"], 1)
                wait_apart(v, cst, sm["h2_done"], j + 1)
                for t in range(QT):
                    last = nc.vector.bn_stats(stats[:, t, :], tile(j, t))
                last.then_inc(sm["f_stats"], 1)
                wait_apart(v, cst, sm["f_stats"], j + 1)
                for t in range(QT):
                    last = nc.vector.bn_aggr(mv[:, t, :], stats[:, t, :])
                last.then_inc(sm["f_var"], 1)
                v.wait_ge(sm["f_rstd"], ONE + j + 1)
                v.wait_ge(sm["a_ot"], ONE + j + 1)
                for t in range(QT):
                    last = ts(sx[:, t, :], tile(j, t), pt[3][:, t:t + 1], pt[4][:, t:t + 1], ALU.mult, ALU.add)
                last.then_inc(sm["f_norm"], 1)

            def choose(j, i, n):
                rounds = (R_IN, R_PR, R_OUT)[i]
                width = (N_IN, N_PR, N_OUT)[i]
                r = n % rounds
                tiles = [2 * (n // rounds), 2 * (n // rounds) + 1]
                at = j * ND + QT * sum((R_IN, R_PR, R_OUT)[:i]) + 2 * n
                src = [(acts, pacts, acts)[i][:, t, :] if r == 0 else work[:, t % 2, 0:width] for t in tiles]
                for b, t in enumerate(tiles):
                    if r == 0:
                        wait_apart(v, cst, sm[("f_acted", "f_practed", "f_oacted")[i]], j * QT + t + 1)
                    else:
                        wait_apart(v, cst, sm["cleared"], at - 1 + b)
                    nc.vector.max(best[:, b, :], src[b]).then_inc(sm["found"], 1)
                for b, t in enumerate(tiles):
                    if i == 1 and r == 0:
                        v.wait_ge(sm["found"], ONE + at + 1 + b)
                        ts(ptop[:, t:t + 1], best[:, b, 0:1], -1.0, None, ALU.mult)
                    wait_apart(v, cst, sm["found"], at + 1 + b)
                    nc.vector.match_replace(work[:, b, 0:width], best[:, b, :], src[b], GONE).then_inc(sm["cleared"], 1)
                if r < rounds - 1:
                    return
                for b, t in enumerate(tiles):
                    m = i * QT + t
                    v.wait_ge(sm["cleared"], ONE + at + 1 + b)
                    v.wait_ge(sm["f_ct"], ONE + j * (3 * QT) + max(m - 1, 0))
                    wk, ch = work[:, b, 0:width], chosen[:, b, 0:width]
                    if i == 1:
                        v.wait_ge(sm["f_exp"], ONE + j * QT + t + 1)
                        stt(out=ch, in0=wk, scalar=IS_GONE, in1=pexp[:, t, :], op0=ALU.is_lt, op1=ALU.mult,
                            accum_out=zp[:, t:t + 1]).then_inc(sm["chosen_done"], 1)
                        v.wait_ge(sm["chosen_done"], ONE + j * (3 * QT) + m + 1)
                        nc.vector.reciprocal(rzp[:, t:t + 1], zp[:, t:t + 1]).then_inc(sm["f_rz"], 1)
                    else:
                        stt(out=ch, in0=wk, scalar=IS_GONE, in1=acts[:, t, :], op0=ALU.is_lt,
                            op1=ALU.mult).then_inc(sm["chosen_done"], 1)

            def finish(j, t):
                v.wait_ge(sm["f_out"], ONE + j * QT + t + 1)
                if t == 0:
                    v.wait_ge(sm["out_done"], ONE + j * 16)
                tt(h_out[:, t, :], x3[:, 0:P], tile(j, t), ALU.add).then_inc(sm["f_res"], 1)

            def second_layer(j, s):
                if s == 0:
                    attn_first(j)
                if s == 1:
                    attn_qkv(j)
                if s == 2:
                    attn(j)
                if s == 3:
                    attn_out(j)
                for i, rounds in enumerate((R1, R2, R3)):
                    for n in range(*rounds.get(s, (0, 0))):
                        choose(j, i, n)
                for t in S4.get(s, ()):
                    finish(j, t)

            v.wait_ge(keep["w_in"], 16 * keep["w_loads"])
            shared = w2[:, 0:SH].rearrange("p s c n -> p (s c n)")
            ts(shared, shared, 1.0 / SH, None, ALU.mult).then_inc(sm["c_half"], 1)
            v.wait_ge(sm["c_in"], ONE + 16 * 11)
            for i in range(2):
                ts(gbk[:, i, :], odd[:, :], gb[:, 2 + i:3 + i], None, ALU.mult).then_inc(sm["gbk_done"], 1)
            for s in range(S):
                add_expert(0, s)
            with v.Fori(1, G) as k:
                for s in range(S + 1):
                    if s:
                        add_expert(k, s - 1)
                    second_layer(k - 1, s)
            for s in range(S + 1):
                second_layer(G - 1, s)


def lm_tower(nc, d, out):
    E, SH, FC = 16, 2, 4
    scr = {
        "h": nc.dram_tensor("scr_h", [G, P, W4], F32).ap(),
        "xt": nc.dram_tensor("scr_xt", [G, P, W4], F32).ap(),
        "o": nc.dram_tensor("scr_o", [4, P, SEQ * P], F32).ap(),
        "xm": nc.dram_tensor("scr_xm", [G, P, W4], F32).ap(),
    }
    with ExitStack() as ctx:
        cst = {
            "ident": ctx.enter_context(nc.sbuf_tensor("ident", [P, P], F32)),
            "neg_half": ctx.enter_context(nc.sbuf_tensor("neg_half", [P, SEQ], F32)),
            "ones_row": ctx.enter_context(nc.sbuf_tensor("ones_row", [1, P], F32)),
            "pool_step": ctx.enter_context(nc.semaphore("pool_step")),
            "consts_done": ctx.enter_context(nc.semaphore("consts_done")),
        }
        tokens_phase(nc, d, cst, scr)
        attention0_phase(nc, d, cst, scr)
        keep = {
            "h1": ctx.enter_context(nc.sbuf_tensor("h1", [P, SEQ, P], F32)),
            "comb": ctx.enter_context(nc.sbuf_tensor("comb", [P, SEQ, E], F32)),
            "w1": ctx.enter_context(nc.sbuf_tensor("w1", [P, E + SH, FC * P], F32)),
            "w2": ctx.enter_context(nc.sbuf_tensor("w2", [P, E + SH, FC, P], F32)),
            "b1": ctx.enter_context(nc.sbuf_tensor("b1", [P, E + SH, FC], F32)),
            "h1_kept": ctx.enter_context(nc.semaphore("h1_kept")),
            "comb_kept": ctx.enter_context(nc.semaphore("comb_kept")),
            "w_in": ctx.enter_context(nc.semaphore("experts_in")),
            "w_loads": 3,
        }
        mix_phase(nc, d, cst, scr, keep)
        tower_phase(nc, d, cst, scr, keep, out)


def kernel(**inputs):
    import numpy as np
    import concourse.bacc as bacc
    from concourse import mybir as mb
    from concourse.bass_utils import run_bass_kernel_spmd as run

    a = {k: np.asarray(v) for k, v in inputs.items()}
    L = lambda x: np.ascontiguousarray(x)
    lay = {
        "ids": L(a["x"].T),
        "wt": L(a["L0_tok_W"].T),
        "tok_b": a["L0_tok_b"],
        "bo": a["L0_attn_bo"],
        "wqkv": L(np.stack([a[f"L0_attn_W{n}"].reshape(128, 4, 128) for n in "qkv"], 0).transpose(2, 1, 0, 3)),
        "bqkv": L(np.stack([a[f"L0_attn_b{n}"].reshape(4, 128) for n in "qkv"], 0).transpose(1, 2, 0)),
        "pk": np.tile(a["L0_attn_P_k"].T, (1, 128)),
        "pv": L(a["L0_attn_P_v"].transpose(1, 0, 2)),
        "wo": L(a["L0_attn_Wo"].reshape(4, 128, 128).transpose(1, 0, 2)),
        "gate": L(a["L0_ffn_gate_w"].T),
        "b2": np.concatenate([a["L0_ffn_re_b2"], a["L0_ffn_se_b2"]]),
        "w1": L(np.concatenate([a["L0_ffn_se_w1"], a["L0_ffn_re_w1"]]).transpose(1, 0, 2)),
        "w2": L(np.concatenate([a["L0_ffn_se_w2"], a["L0_ffn_re_w2"]]).reshape(18, 4, 128, 128).transpose(2, 0, 1, 3)),
        "b1": L(np.concatenate([a["L0_ffn_se_b1"], a["L0_ffn_re_b1"]]).reshape(18, 4, 128).transpose(2, 0, 1)),
        "wqkv1": np.concatenate([a[f"L1_attn_w_{n}"] for n in "qkv"], 1),
        "bqkv1": np.concatenate([a[f"L1_attn_b_{n}"] for n in "qkv"]),
        "wo1": a["L1_attn_w_o"],
        "bo1": a["L1_attn_b_o"].reshape(1, 128),
        "gb": L(np.stack([a[f"L1_attn_{n}"] for n in ("g_q", "be_q", "g_k", "be_k")], 1)),
        "odd": np.stack([np.arange(128) // 16 % 2 == b for b in range(2)], 1).astype(np.float32),
        "ip": L(a["L1_ffn_input_patterns"].T),
        "piw": L(a["L1_ffn_process_input_weights"].T.reshape(4, 128, 256).transpose(1, 0, 2)),
        "pval": L(a["L1_ffn_process_values"].reshape(2, 128, 64).transpose(1, 0, 2)),
        "oiw": L(a["L1_ffn_output_input_weights"].T),
        "op": L(a["L1_ffn_output_patterns"].reshape(4, 128, 128).transpose(1, 0, 2)),
    }
    nc = bacc.Bacc("TRN2", target_bir_lowering=False, num_devices=1)
    arrays, args = {}, {}
    for name, arr in lay.items():
        arrays[f"in_{name}"] = arr
        args[name] = nc.dram_tensor(f"in_{name}", arr.shape, mb.dt.from_np(arr.dtype), kind="ExternalInput").ap()
    out = nc.dram_tensor("out_h", (SEQ, P, P), mb.dt.float32, kind="ExternalOutput").ap()
    lm_tower(nc, args, out)
    r = run(nc, [arrays], core_ids=[0])
    return r.results[0]["out_h"]
```

```python
from contextlib import ExitStack

import concourse.bass as bass
from concourse import mybir

ALU = mybir.AluOpType
ACT = mybir.ActivationFunctionType
F32 = mybir.dt.float32
U32 = mybir.dt.uint32
X = mybir.AxisListType.X
ds = bass.ds

P = 128
SEQ = 64
QT = 4
G = SEQ // QT
W4 = QT * P
EPS = 1e-5
ONE = 1


def wait_apart(eng, cst, sem, value):
    value = ONE + value
    if not isinstance(value, int):
        value = eng.snap(eng.compute_val(value))
        eng.wait_ge(cst["consts_done"], ONE + 3)
    eng.wait_ge(sem, value)


def tokens_phase(nc, d, cst, scr):
    with ExitStack() as ctx:
        def sb(name, shape, dt=F32):
            return ctx.enter_context(nc.sbuf_tensor(f"tok_{name}", shape, dt))

        sems = []

        def sem(name):
            sems.append(ctx.enter_context(nc.semaphore(f"tok_{name}")))
            return sems[-1]

        ids = sb("ids", [P, SEQ], U32)
        ids_now = sb("ids_now", [P, 2, QT], U32)
        feat = sb("feat", [P, 2, QT, P])
        tok_b = sb("tok_b", [P, P])
        out_b = sb("out_b", [P, P])
        h_all = sb("h_all", [P, SEQ, P])
        square = sb("square", [P, QT, P])
        ssq = sb("ssq", [P, SEQ])
        inv = sb("inv", [P, SEQ])
        stats = sb("stats", [P, QT, 6])
        mv = sb("mv", [P, QT, 2])
        mean = sb("mean", [P, SEQ])
        rstd = sb("rstd", [P, SEQ])
        shift = sb("shift", [P, SEQ])
        h_out = sb("h_out", [P, 2, QT, P])
        xn = sb("xn", [P, 2, QT, P])
        xt = sb("xt", [P, 2, W4])
        ps = [ctx.enter_context(nc.psum_tensor(f"tok_ps_xt{i}", [P, W4], F32)) for i in range(2)]

        ids_in = sem("ids_in")
        bias_in = sem("bias_in")
        ids_copied = sem("ids_copied")
        gathered = [ctx.enter_context(nc.semaphore(f"tok_gathered{i}")) for i in range(2)]
        feat_used = sem("feat_used")
        dve = sem("dve_step")
        ssq_done = sem("ssq_done")
        inv_done = sem("inv_done")
        var_done = sem("var_done")
        rstd_done = sem("rstd_done")
        h_out_done = sem("h_out_done")
        h_stored = [sem("h_stored0"), sem("h_stored1")]
        xn_done = sem("xn_done")
        xt_ready = sem("xt_ready")
        xt_copied = sem("xt_copied")
        xt_stored = [sem("xt_stored0"), sem("xt_stored1")]

        block = ctx.enter_context(nc.Block())

        @block.sync
        def _(sp):
            for s in sems + [cst["pool_step"], cst["consts_done"]]:
                sp.sem_inc(s, ONE)
            sp.dma_start(ids[:, :], d["ids"].bitcast(U32)).then_inc(ids_in, 16)
            sp.dma_start(tok_b[:, :], d["tok_b"].partition_broadcast(P)).then_inc(bias_in, 16)
            sp.dma_start(out_b[:, :], d["bo"].partition_broadcast(P)).then_inc(bias_in, 16)
            with sp.Fori(0, G // 2) as gg:
                g = gg * 2
                for p in range(2):
                    sp.wait_ge(h_out_done, ONE + g + p + 1)
                    sp.dma_start(scr["h"][ds(g + p, 1), :, :].rearrange("a p n -> (a p) n"),
                                 h_out[:, p].rearrange("p q n -> p (q n)")).then_inc(h_stored[p], 16)
            with sp.Fori(0, G // 2) as gg:
                g = gg * 2
                for p in range(2):
                    sp.wait_ge(xt_copied, ONE + g + p + 1)
                    sp.dma_start(scr["xt"][ds(g + p, 1), :, :].rearrange("a p n -> (a p) n"),
                                 xt[:, p]).then_inc(xt_stored[p], 16)
            for p in range(2):
                sp.wait_ge(h_stored[p], ONE + 16 * (G // 2))
                sp.wait_ge(xt_stored[p], ONE + 16 * (G // 2))

        @block.gpsimd
        def _(pool):
            nc.gpsimd.memset(cst["ident"][:, :], 0.0).then_inc(cst["pool_step"], 1)
            pool.wait_ge(cst["pool_step"], ONE + 1)
            nc.gpsimd.affine_select(out=cst["ident"][:, :], in_=cst["ident"][:, :], compare_op=ALU.not_equal,
                                    fill=1.0, base=0, pattern=[[-1, P]],
                                    channel_multiplier=1).then_inc(cst["consts_done"], 1)
            nc.gpsimd.memset(cst["neg_half"][:, :], -0.5).then_inc(cst["consts_done"], 1)
            nc.gpsimd.memset(cst["ones_row"][:, :], 1.0).then_inc(cst["consts_done"], 1)
            pool.wait_ge(ids_in, ONE + 16)
            with pool.Fori(0, G // 2) as gg:
                g = gg * 2
                for p in range(2):
                    pool.wait_ge(feat_used, ONE + g)
                    nc.gpsimd.tensor_copy(ids_now[:, p, :], ids[:, ds((g + p) * QT, QT)]).then_inc(ids_copied, 1)
                    wait_apart(pool, cst, ids_copied, g + p + 1)
                    for q in range(QT):
                        nc.gpsimd.indirect_dma_start(
                            out=feat[:, p, q, :], out_offset=None, in_=d["wt"],
                            in_offset=bass.IndirectOffsetOnAxis(ap=ids_now[:, p, q:q + 1], axis=0),
                        ).then_inc(gathered[p], 16)
            pool.wait_ge(cst["consts_done"], ONE + 3)
            pool.wait_ge(ssq_done, ONE + 1)
            nc.gpsimd.tensor_tensor(inv[:, :], ssq[:, :], cst["neg_half"][:, 0:SEQ], ALU.pow).then_inc(inv_done, 1)
            pool.wait_ge(var_done, ONE + G)
            nc.gpsimd.tensor_tensor(rstd[:, :], rstd[:, :], cst["neg_half"][:, 0:SEQ], ALU.pow).then_inc(rstd_done, 1)

        @block.vector
        def _(v):
            v.wait_ge(bias_in, ONE + 32)
            bias4 = tok_b[:, :].unsqueeze(1).broadcast_to([P, QT, P])
            out4 = out_b[:, :].unsqueeze(1).broadcast_to([P, QT, P])
            with v.Fori(0, G // 2) as gg:
                g = gg * 2
                for p in range(2):
                    t = ds((g + p) * QT, QT)
                    v.wait_ge(gathered[p], g * (8 * QT) + 16 * QT)
                    nc.vector.tensor_tensor(h_all[:, t, :], feat[:, p], bias4, ALU.add).then_inc(feat_used, 1)
                    v.wait_ge(feat_used, ONE + g + p + 1)
                    nc.vector.tensor_tensor(square[:, :, :], h_all[:, t, :], h_all[:, t, :],
                                            ALU.mult).then_inc(dve, 1)
                    v.wait_ge(dve, ONE + 2 * (g + p) + 1)
                    nc.vector.tensor_reduce(ssq[:, t], square[:, :, :], X, ALU.add).then_inc(dve, 1)
            v.wait_ge(dve, ONE + 2 * G)
            nc.vector.tensor_scalar(ssq[:, :], ssq[:, :], 1e-24, None, ALU.max).then_inc(ssq_done, 1)
            v.wait_ge(inv_done, ONE + 1)
            with v.Fori(0, G // 2) as gg:
                g = gg * 2
                for p in range(2):
                    t = ds((g + p) * QT, QT)
                    n = g + p
                    nc.vector.tensor_tensor(h_all[:, t, :], h_all[:, t, :],
                                            inv[:, t].unsqueeze(2).broadcast_to([P, QT, P]),
                                            ALU.mult).then_inc(dve, 1)
                    v.wait_ge(dve, ONE + n * 3 + (2 * G + 1))
                    v.wait_ge(h_stored[p], ONE + g * 8)
                    nc.vector.tensor_tensor(h_out[:, p], h_all[:, t, :], out4, ALU.add).then_inc(h_out_done, 1)
                    for q in range(QT):
                        last = nc.vector.bn_stats(stats[:, q, :], h_all[:, ds((g + p) * QT + q, 1), :]
                                                  .rearrange("p a n -> p (a n)"))
                    last.then_inc(dve, 1)
                    wait_apart(v, cst, dve, n * 3 + (2 * G + 2))
                    for q in range(QT):
                        last = nc.vector.bn_aggr(mv[:, q, :], stats[:, q, :])
                    last.then_inc(dve, 1)
                    v.wait_ge(dve, ONE + n * 3 + (2 * G + 3))
                    nc.vector.tensor_copy(mean[:, t], mv[:, :, 0])
                    nc.vector.tensor_scalar(rstd[:, t], mv[:, :, 1], EPS, None, ALU.add).then_inc(var_done, 1)
            v.wait_ge(rstd_done, ONE + 1)
            nc.vector.scalar_tensor_tensor(out=shift[:, :], in0=mean[:, :], scalar=-1.0, in1=rstd[:, :],
                                           op0=ALU.mult, op1=ALU.mult).then_inc(dve, 1)
            v.wait_ge(dve, ONE + 5 * G + 1)
            with v.Fori(0, G // 2) as gg:
                g = gg * 2
                for p in range(2):
                    v.wait_ge(xt_ready, ONE + g)
                    for q in range(QT):
                        i = ds((g + p) * QT + q, 1)
                        last = nc.vector.tensor_scalar(
                            xn[:, p, q, :], h_all[:, i, :].rearrange("p a n -> p (a n)"),
                            rstd[:, i], shift[:, i], ALU.mult, ALU.add)
                    last.then_inc(xn_done, 1)

        @block.tensor
        def _(pe):
            pe.wait_ge(cst["consts_done"], ONE + 3)
            with pe.Fori(0, G // 2) as gg:
                g = gg * 2
                for p in range(2):
                    pe.wait_ge(xn_done, ONE + g + p + 1)
                    pe.wait_ge(xt_copied, ONE + g)
                    for q in range(QT):
                        last = nc.tensor.transpose(ps[p][:, q * P:(q + 1) * P], xn[:, p, q, :], cst["ident"][:, :])
                    last.then_inc(xt_ready, 1)

        @block.scalar
        def _(act):
            with act.Fori(0, G // 2) as gg:
                g = gg * 2
                for p in range(2):
                    act.wait_ge(xt_ready, ONE + g + p + 1)
                    act.wait_ge(xt_stored[p], ONE + g * 8)
                    nc.scalar.copy(xt[:, p], ps[p][:, :]).then_inc(xt_copied, 1)


def attention0_phase(nc, d, cst, scr):
    H, DK, NR = 8, 64, 2 * P - 1
    NP = H // 2
    IB = 8
    NIB = P // IB
    RB = 8
    LATE = NIB - 2
    QC = 4
    SCALE = float(DK) ** -0.5
    with ExitStack() as ctx:
        def sb(name, shape, dt=F32):
            return ctx.enter_context(nc.sbuf_tensor(f"att_{name}", shape, dt))

        sems = []

        def sem(name):
            sems.append(ctx.enter_context(nc.semaphore(f"att_{name}")))
            return sems[-1]

        def bank(name):
            return ctx.enter_context(nc.psum_tensor(f"att_{name}", [P, W4], F32))

        xg = sb("xg", [P, W4])
        wqkv = sb("wqkv", [P, 3, P])
        bqkv = sb("bqkv", [P, 3])
        rel_k = sb("rel_k", [P, H, P])
        q_t = sb("q_t", [P, W4])
        k_t = sb("k_t", [P, W4])
        v_s = sb("v_s", [P, QT, P])
        s_s = sb("s_s", [P, 2, QT, P])
        top = sb("top", [P, 2, QT])
        ntop = sb("ntop", [P, 2, QT])
        z = sb("z", [P, 2, QT])
        rz = sb("rz", [P, 2, QT])
        p_s = sb("p_s", [P, 2, QT, P])
        p_now = sb("p_now", [P, 2, QT, P])
        p_t = sb("p_t", [P, 2, SEQ, P])
        rel_v = sb("rel_v", [P, RB, 2, IB, DK])
        o_t = sb("o_t", [P, SEQ, P])
        ps_q, ps_k, ps_v, ps_o = (bank(f"ps_{n}") for n in "qkvo")
        ps_s = [bank("ps_s0"), bank("ps_s1")]
        ps_t = [bank("ps_t0"), bank("ps_t1")]

        x_in = sem("x_in")
        w_in = sem("w_in")
        rk_in = sem("rk_in")
        rv_in = [sem(f"rv_in{i}") for i in range(RB)]
        q_ready = sem("q_ready")
        k_ready = sem("k_ready")
        v_ready = sem("v_ready")
        q_copied = sem("q_copied")
        k_copied = sem("k_copied")
        v_copied = sem("v_copied")
        s_ready = sem("s_ready")
        s_added = sem("s_added")
        top_done = sem("top_done")
        ntop_done = sem("ntop_done")
        exp_done = sem("exp_done")
        rz_done = sem("rz_done")
        p_done = sem("p_done")
        t_ready = sem("t_ready")
        t_copied = sem("t_copied")
        t_kept = sem("t_kept")
        o_ready = sem("o_ready")
        o_copied = sem("o_copied")
        r_ready = sem("r_ready")
        r_added = sem("r_added")
        first_stored = sem("first_stored")
        rest_stored = sem("rest_stored")

        block = ctx.enter_context(nc.Block())
        U = G

        @block.sync
        def _(sp):
            for s in sems:
                sp.sem_inc(s, ONE)
            sp.dma_start(rel_k[:, :, :], bass.AP(tensor=d["pk"].tensor, offset=P - 1,
                                                 ap=[[NR - 1, P], [P * NR, H], [1, P]])).then_inc(rk_in, 16)
            def rel_block(hp, ib):
                for h in range(2):
                    src = d["pv"][ds(hp * 2 + h, 1), ib * IB:(ib + 1) * IB, :]
                    win = bass.AP(tensor=src.tensor, offset=src.offset, ap=[[DK, P], [1, IB * DK]])
                    sp.dma_start(rel_v[:, ib % RB, h].rearrange("p i d -> p (i d)"), win).then_inc(rv_in[ib % RB], 16)

            def weights(hp):
                sp.dma_start(wqkv[:, :, :], d["wqkv"][ds(hp, 1)].rearrange("a p t n -> (a p) t n")).then_inc(w_in, 16)
                sp.dma_start(bqkv[:, :], d["bqkv"][ds(hp, 1)].rearrange("a p t -> (a p) t")).then_inc(w_in, 16)

            def group(g):
                src = scr["xt"][g:g + 1] if isinstance(g, int) else scr["xt"][ds(g, 1)]
                sp.dma_start(xg[:, :], src.rearrange("a p n -> (a p) n")).then_inc(x_in, 16)

            def one_pair(hp, more):
                for ib in range(RB):
                    sp.wait_ge(v_ready, ONE + hp * U + ib + 2)
                    group(ib + 2)
                    sp.wait_ge(r_ready, ONE + hp * NIB)
                    rel_block(hp, ib)
                with sp.Fori(RB + 2, U) as g:
                    sp.wait_ge(v_ready, ONE + hp * U + g)
                    group(g)
                if more:
                    sp.wait_ge(v_ready, ONE + (hp + 1) * U)
                    sp.wait_ge(o_copied, ONE + (hp + 1) * U)
                    weights(hp + 1)
                    group(0)
                for ib in range(RB, NIB):
                    sp.wait_ge(r_ready, ONE + hp * NIB + ib - RB + 1)
                    rel_block(hp, ib)
                if more:
                    sp.wait_ge(v_ready, ONE + (hp + 1) * U + 1)
                    group(1)
                sp.wait_ge(r_added, ONE + (hp + 1) * NIB)
                dst = scr["o"][ds(hp, 1)].rearrange("a p n -> (a p) n")
                src = o_t[:, :, :].rearrange("p b i -> p (b i)")
                sp.dma_start(dst[:, 0:QC * W4], src[:, 0:QC * W4]).then_inc(first_stored, 16)
                sp.dma_start(dst[:, QC * W4:], src[:, QC * W4:]).then_inc(rest_stored, 16)

            weights(0)
            group(0)
            sp.wait_ge(v_ready, ONE + 1)
            group(1)
            with sp.Fori(0, NP - 1) as hp:
                one_pair(hp, True)
            one_pair(NP - 1, False)
            sp.wait_ge(first_stored, ONE + 16 * NP)
            sp.wait_ge(rest_stored, ONE + 16 * NP)

        @block.tensor
        def _(pe):
            def project(hp, u):
                pe.wait_ge(w_in, ONE + hp * 32 + 32)
                pe.wait_ge(x_in, ONE + u * 16 + 16)
                pe.wait_ge(q_copied, ONE + u)
                nc.tensor.matmul(ps_q[:, :], wqkv[:, 0, :], xg[:, :], start=True, stop=True).then_inc(q_ready, 1)
                pe.wait_ge(k_copied, ONE + u)
                nc.tensor.matmul(ps_k[:, :], wqkv[:, 1, :], xg[:, :], start=True, stop=True).then_inc(k_ready, 1)
                pe.wait_ge(v_copied, ONE + u)
                for t in range(QT):
                    last = nc.tensor.matmul(ps_v[:, t * P:(t + 1) * P], xg[:, t * P:(t + 1) * P], wqkv[:, 2, :],
                                            start=True, stop=True)
                last.then_inc(v_ready, 1)

            def scores(u):
                pe.wait_ge(q_copied, ONE + u + 1)
                pe.wait_ge(k_copied, ONE + u + 1)
                for h in range(2):
                    pe.wait_ge(s_added, ONE + u * 2)
                    for t in range(QT):
                        r = slice(h * DK, (h + 1) * DK)
                        c = slice(t * P, (t + 1) * P)
                        last = nc.tensor.matmul(ps_s[h][:, c], q_t[r, c], k_t[r, c], start=True, stop=True)
                        if t == QT - 1:
                            last.then_inc(s_ready, 1)

            def transposes(u, h):
                pe.wait_ge(p_done, ONE + u * 2 + h + 1)
                pe.wait_ge(t_copied, ONE + u * 2)
                for t in range(QT):
                    last = nc.tensor.transpose(ps_t[h][:, t * P:(t + 1) * P], p_s[:, h, t, :], cst["ident"][:, :])
                last.then_inc(t_ready, 1)

            def values(u):
                pe.wait_ge(t_copied, ONE + u * 2 + 2)
                pe.wait_ge(v_copied, ONE + u + 1)
                pe.wait_ge(o_copied, ONE + u)
                for h in range(2):
                    r = slice(h * DK, (h + 1) * DK)
                    for t in range(QT):
                        last = nc.tensor.matmul(ps_o[r, t * P:(t + 1) * P], v_s[:, t, r],
                                                p_now[:, h, t, :], start=True, stop=True)
                last.then_inc(o_ready, 1)

            def one_pair(hp, more):
                wait_apart(pe, cst, r_added, hp * NIB)
                with pe.Fori(0, U - 1) as g:
                    u = hp * U + g
                    project(hp, u + 1)
                    transposes(u, 0)
                    scores(u + 1)
                    transposes(u, 1)
                    values(u)
                for h in range(2):
                    transposes(hp * U + (U - 1), h)
                values(hp * U + (U - 1))
                pe.wait_ge(t_kept, ONE + hp * (2 * U) + 2 * U)
                for ib in range(NIB):
                    if more and ib == LATE:
                        project(hp + 1, (hp + 1) * U)
                        scores((hp + 1) * U)
                    b = ib % RB
                    pe.wait_ge(rv_in[b], ONE + hp * (32 * (NIB // RB)) + (ib // RB) * 32 + 32)
                    pe.wait_ge(r_added, ONE + hp * NIB + max(ib - 1, 0))
                    for i in range(IB):
                        for h in range(2):
                            last = nc.tensor.matmul(
                                ps_t[ib % 2][h * DK:(h + 1) * DK, (IB - 1 - i) * SEQ:(IB - i) * SEQ],
                                rel_v[:, b, h, i, :], p_t[:, h, :, P - 1 - (ib * IB + i)], start=True, stop=True)
                    last.then_inc(r_ready, 1)

            project(0, 0)
            scores(0)
            with pe.Fori(0, NP - 1) as hp:
                one_pair(hp, True)
            one_pair(NP - 1, False)

        @block.scalar
        def _(act):
            def project(hp, u):
                act.wait_ge(w_in, ONE + hp * 32 + 32)
                act.wait_ge(q_ready, ONE + u + 1)
                act.wait_ge(s_ready, ONE + u * 2)
                nc.scalar.activation(q_t[:, :], ps_q[:, :], ACT.Identity, bias=bqkv[:, 0:1]).then_inc(q_copied, 1)

            def exps(u):
                act.wait_ge(t_ready, ONE + u * 2)
                act.wait_ge(rz_done, ONE + u * 2)
                for h in range(2):
                    act.wait_ge(ntop_done, ONE + u * 2 + h + 1)
                    for t in range(QT):
                        last = nc.scalar.activation(p_s[:, h, t, :], s_s[:, h, t, :], ACT.Exp,
                                                    bias=ntop[:, h, t:t + 1], scale=SCALE,
                                                    accum_out=z[:, h, t:t + 1])
                    last.then_inc(exp_done, 1)

            def copies(u):
                act.wait_ge(o_ready, ONE + u)
                act.wait_ge(t_kept, ONE + u * 2)
                for h in range(2):
                    act.wait_ge(t_ready, ONE + u * 2 + h + 1)
                    nc.scalar.copy(p_now[:, h].rearrange("p t n -> p (t n)"), ps_t[h][:, :]).then_inc(t_copied, 1)

            def out(hp, u, g, stored):
                act.wait_ge(stored, ONE + hp * 16)
                act.wait_ge(o_ready, ONE + u + 1)
                nc.scalar.activation(o_t[:, ds(g * QT, QT), :].rearrange("p t n -> p (t n)"), ps_o[:, :],
                                     ACT.Identity, bias=bqkv[:, 2:3]).then_inc(o_copied, 1)

            def one_pair(hp, more):
                project(hp, hp * U + 1)
                copies(hp * U)
                exps(hp * U + 1)
                for lo, hi, stored in ((0, QC, first_stored), (QC, U - 2, rest_stored)):
                    with act.Fori(lo, hi) as g:
                        u = hp * U + g
                        project(hp, u + 2)
                        out(hp, u, g, stored)
                        copies(u + 1)
                        exps(u + 2)
                out(hp, hp * U + (U - 2), U - 2, rest_stored)
                copies(hp * U + (U - 1))
                out(hp, hp * U + (U - 1), U - 1, rest_stored)
                if more:
                    project(hp + 1, (hp + 1) * U)
                    exps((hp + 1) * U)

            project(0, 0)
            exps(0)
            with act.Fori(0, NP - 1) as hp:
                one_pair(hp, True)
            one_pair(NP - 1, False)

        @block.gpsimd
        def _(pool):
            with pool.Fori(0, NP) as hp:
                wait_apart(pool, cst, r_ready, hp * NIB)
                with pool.Fori(0, U) as g:
                    for h in range(2):
                        pool.wait_ge(t_copied, ONE + hp * (2 * U) + g * 2 + h + 1)
                        nc.gpsimd.tensor_copy(p_t[:, h, ds(g * QT, QT), :], p_now[:, h]).then_inc(t_kept, 1)

        @block.vector
        def _(v):
            def key_copy(hp, u):
                v.wait_ge(w_in, ONE + hp * 32 + 32)
                v.wait_ge(k_ready, ONE + u + 1)
                v.wait_ge(s_ready, ONE + u * 2)
                nc.vector.tensor_scalar(k_t[:, :], ps_k[:, :], bqkv[:, 1:2], None, ALU.add).then_inc(k_copied, 1)

            def value_copy(u):
                v.wait_ge(v_ready, ONE + u + 1)
                v.wait_ge(o_ready, ONE + u)
                nc.vector.tensor_copy(v_s[:, :, :].rearrange("p t n -> p (t n)"), ps_v[:, :]).then_inc(v_copied, 1)

            def bias_and_top(hp, u):
                for h in range(2):
                    v.wait_ge(exp_done, ONE + u * 2)
                    v.wait_ge(s_ready, ONE + u * 2 + h + 1)
                    nc.vector.tensor_tensor(s_s[:, h], ps_s[h][:, :].rearrange("p (t n) -> p t n", t=QT),
                                            rel_k[:, ds(hp * 2 + h, 1), :].broadcast_to([P, QT, P]),
                                            ALU.add).then_inc(s_added, 1)
                    v.wait_ge(s_added, ONE + u * 2 + h + 1)
                    nc.vector.tensor_reduce(top[:, h], s_s[:, h], X, ALU.max).then_inc(top_done, 1)
                    v.wait_ge(top_done, ONE + u * 2 + h + 1)
                    nc.vector.tensor_scalar(ntop[:, h], top[:, h], -SCALE, None, ALU.mult).then_inc(ntop_done, 1)

            def divide(u):
                for h in range(2):
                    v.wait_ge(exp_done, ONE + u * 2 + h + 1)
                    nc.vector.reciprocal(rz[:, h], z[:, h]).then_inc(rz_done, 1)
                    v.wait_ge(rz_done, ONE + u * 2 + h + 1)
                    nc.vector.tensor_tensor(p_s[:, h], p_s[:, h],
                                            rz[:, h].unsqueeze(2).broadcast_to([P, QT, P]),
                                            ALU.mult).then_inc(p_done, 1)

            def add_relative(hp, ib):
                wait_apart(v, cst, r_ready, hp * NIB + ib + 1)
                lo = P - IB - ib * IB
                o_view = o_t[:, :, lo:lo + IB].rearrange("p b i -> p i b")
                nc.vector.tensor_tensor(o_view, ps_t[ib % 2][:, :].rearrange("p (i b) -> p i b", i=IB),
                                        o_view, ALU.add).then_inc(r_added, 1)

            def unit(hp, u):
                key_copy(hp, u)
                bias_and_top(hp, u)
                value_copy(u)
                divide(u)

            def one_pair(hp, more):
                with v.Fori(0, U - 1) as g:
                    unit(hp, hp * U + g + 1)
                v.wait_ge(o_copied, ONE + (hp + 1) * U)
                for ib in range(NIB):
                    if more and ib == LATE:
                        unit(hp + 1, (hp + 1) * U)
                    add_relative(hp, ib)

            v.wait_ge(rk_in, ONE + 16)
            unit(0, 0)
            with v.Fori(0, NP - 1) as hp:
                one_pair(hp, True)
            one_pair(NP - 1, False)


def mix_phase(nc, d, cst, scr, keep):
    E, TOP = 16, 4
    with ExitStack() as ctx:
        def sb(name, shape, dt=F32):
            return ctx.enter_context(nc.sbuf_tensor(f"mix_{name}", shape, dt))

        sems = []

        def sem(name):
            sems.append(ctx.enter_context(nc.semaphore(f"mix_{name}")))
            return sems[-1]

        wo = sb("wo", [P, 4, P])
        gate = sb("gate", [P, E])
        b2 = sb("b2", [E + 2, P])
        og = sb("og", [P, 2, 4, W4])
        hg = sb("hg", [P, 2, QT, P])
        stats = sb("stats", [P, QT, 6])
        mv = sb("mv", [P, 2, QT, 2])
        rstd = sb("rstd", [P, 2, QT])
        shift = sb("shift", [P, 2, QT])
        xn = sb("xn", [P, 2, QT, P])
        xt = sb("xt", [P, 2, W4])
        logit = sb("logit", [P, SEQ, E])
        prob = sb("prob", [P, SEQ, E])
        above = sb("above", [P, SEQ, E])
        equal = sb("equal", [P, SEQ, E])
        upto = sb("upto", [P, SEQ, E])
        restart = sb("restart", [P, SEQ, E])
        best = sb("best", [P, SEQ, 8])
        row = sb("row", [P, SEQ])
        row2 = sb("row2", [P, SEQ])
        comb_now = sb("comb_now", [P, 2, QT, E + 2])
        comb_t = sb("comb_t", [E + 2, 2, QT, P])
        ps_y = [ctx.enter_context(nc.psum_tensor(f"mix_ps_y{i}", [P, W4], F32)) for i in range(2)]
        ps_t = [ctx.enter_context(nc.psum_tensor(f"mix_ps_t{i}", [P, W4], F32)) for i in range(2)]
        ps_l = [ctx.enter_context(nc.psum_tensor(f"mix_ps_l{i}", [P, W4], F32)) for i in range(2)]

        w_in = sem("w_in")
        g_in = [sem("g_in0"), sem("g_in1")]
        y_ready = sem("y_ready")
        y_added = sem("y_added")
        stats_done = sem("stats_done")
        var_done = sem("var_done")
        rstd_done = sem("rstd_done")
        shift_done = sem("shift_done")
        xn_done = sem("xn_done")
        t_ready = sem("t_ready")
        t_copied = sem("t_copied")
        t_stored = [sem("t_stored0"), sem("t_stored1")]
        l_ready = sem("l_ready")
        l_copied = sem("l_copied")
        step = sem("router_step")
        less_top = sem("less_top")
        exp_done = sem("exp_done")
        restart_done = sem("restart_done")
        comb_done = sem("comb_done")
        c_ready = sem("c_ready")
        c_copied = sem("c_copied")
        b_ready = sem("b_ready")
        b_added = sem("b_added")

        block = ctx.enter_context(nc.Block())
        HG = G // 2

        @block.sync
        def _(sp):
            for s in sems + [keep["h1_kept"], keep["comb_kept"]]:
                sp.sem_inc(s, ONE)
            sp.dma_start(wo[:, :, :], d["wo"]).then_inc(w_in, 16)
            sp.dma_start(gate[:, :], d["gate"]).then_inc(w_in, 16)
            sp.dma_start(b2[:, :], d["b2"]).then_inc(w_in, 16)
            with sp.Fori(0, HG) as gg:
                for p in range(2):
                    sp.wait_ge(y_ready, ONE + gg * 2)
                    sp.wait_ge(xn_done, ONE + gg * 2)
                    sp.wait_ge(keep["h1_kept"], ONE + gg * 2)
                    sp.dma_start(og[:, p], scr["o"][:, :, ds((gg * 2 + p) * W4, W4)]
                                 .rearrange("a p n -> p a n")).then_inc(g_in[p], 16)
                    sp.dma_start(hg[:, p].rearrange("p q n -> p (q n)"), scr["h"][ds(gg * 2 + p, 1)]
                                 .rearrange("a p n -> (a p) n")).then_inc(g_in[p], 16)
            for p in range(2):
                sp.wait_ge(t_stored[p], ONE + 16 * HG)

        @block.tensor
        def _(pe):
            pe.wait_ge(w_in, ONE + 48)
            with pe.Fori(0, HG) as gg:
                for p in range(2):
                    pe.wait_ge(y_added, ONE + gg * 2)
                    pe.wait_ge(g_in[p], ONE + gg * 32 + 32)
                    for t in range(QT):
                        for a in range(4):
                            last = nc.tensor.matmul(ps_y[p][:, t * P:(t + 1) * P], og[:, p, a, t * P:(t + 1) * P],
                                                    wo[:, a, :], start=(a == 0), stop=(a == 3))
                    last.then_inc(y_ready, 1)
                for p in range(2):
                    pe.wait_ge(t_copied, ONE + gg * 2)
                    pe.wait_ge(xn_done, ONE + gg * 2 + p + 1)
                    for t in range(QT):
                        last = nc.tensor.transpose(ps_t[p][:, t * P:(t + 1) * P], xn[:, p, t, :], cst["ident"][:, :])
                    last.then_inc(t_ready, 1)
                for p in range(2):
                    pe.wait_ge(l_copied, ONE + gg * 2)
                    pe.wait_ge(t_copied, ONE + gg * 2 + p + 1)
                    for t in range(QT):
                        last = nc.tensor.matmul(ps_l[p][:, t * E:(t + 1) * E], xt[:, p, t * P:(t + 1) * P],
                                                gate[:, :], start=True, stop=True)
                    last.then_inc(l_ready, 1)
            with pe.Fori(0, HG) as gg:
                for p in range(2):
                    pe.wait_ge(c_copied, ONE + gg * 2)
                    pe.wait_ge(comb_done, ONE + gg * 2 + p + 1)
                    for t in range(QT):
                        last = nc.tensor.transpose(ps_t[p][0:E + 2, t * P:(t + 1) * P], comb_now[:, p, t, :],
                                                   cst["ident"][:, :])
                    last.then_inc(c_ready, 1)
                for p in range(2):
                    pe.wait_ge(b_added, ONE + gg * 2)
                    pe.wait_ge(c_copied, ONE + gg * 2 + p + 1)
                    for t in range(QT):
                        last = nc.tensor.matmul(ps_y[p][:, t * P:(t + 1) * P], comb_t[:, p, t, :], b2[:, :],
                                                start=True, stop=True)
                    last.then_inc(b_ready, 1)

        @block.scalar
        def _(act):
            with act.Fori(0, HG) as gg:
                for p in range(2):
                    act.wait_ge(shift_done, ONE + gg * 2 + p + 1)
                    act.wait_ge(t_ready, ONE + gg * 2)
                    for t in range(QT):
                        last = nc.scalar.activation(xn[:, p, t, :], hg[:, p, t, :], ACT.Identity,
                                                    bias=shift[:, p, t:t + 1], scale=rstd[:, p, t:t + 1])
                    last.then_inc(xn_done, 1)
                for p in range(2):
                    act.wait_ge(t_stored[p], ONE + gg * 16)
                    act.wait_ge(l_ready, ONE + gg * 2)
                    act.wait_ge(t_ready, ONE + gg * 2 + p + 1)
                    nc.scalar.copy(xt[:, p], ps_t[p][:, :]).then_inc(t_copied, 1)
                for p in range(2):
                    act.wait_ge(t_copied, ONE + gg * 2 + p + 1)
                    act.dma_start(scr["xm"][ds(gg * 2 + p, 1)].rearrange("a p n -> (a p) n"),
                                  xt[:, p]).then_inc(t_stored[p], 16)
            flat = lambda x: x[:, :, :].rearrange("p t e -> p (t e)")
            for n in range(2):
                act.wait_ge(less_top, ONE + n + 1)
                nc.scalar.activation(flat(upto), flat(upto), ACT.Exp).then_inc(exp_done, 1)
            with act.Fori(0, HG) as gg:
                for p in range(2):
                    act.wait_ge(b_ready, ONE + gg * 2)
                    act.wait_ge(c_ready, ONE + gg * 2 + p + 1)
                    nc.scalar.copy(comb_t[:, p].rearrange("p t n -> p (t n)"),
                                   ps_t[p][0:E + 2, :]).then_inc(c_copied, 1)

        @block.gpsimd
        def _(pool):
            for name in ("w1", "w2", "b1"):
                pool.dma_start(keep[name][:], d[name]).then_inc(keep["w_in"], 16)
            nc.gpsimd.memset(restart[:, :, :], 1.0).then_inc(restart_done, 1)
            pool.wait_ge(restart_done, ONE + 1)
            nc.gpsimd.memset(restart[:, :, 0:1], 0.0).then_inc(restart_done, 1)
            nc.gpsimd.memset(comb_now[:, :, :, :], 0.5).then_inc(restart_done, 1)
            with pool.Fori(0, HG) as gg:
                for p in range(2):
                    pool.wait_ge(var_done, ONE + gg * 2 + p + 1)
                    nc.gpsimd.tensor_tensor(rstd[:, p], rstd[:, p], cst["neg_half"][:, 0:QT],
                                            ALU.pow).then_inc(rstd_done, 1)

        @block.vector
        def _(v):
            with v.Fori(0, HG) as gg:
                for p in range(2):
                    n = gg * 2 + p
                    v.wait_ge(y_ready, ONE + n + 1)
                    nc.vector.tensor_tensor(hg[:, p].rearrange("p q n -> p (q n)"), ps_y[p][:, :],
                                            hg[:, p].rearrange("p q n -> p (q n)"), ALU.add).then_inc(y_added, 1)
                    v.wait_ge(y_added, ONE + n + 1)
                    for t in range(QT):
                        last = nc.vector.bn_stats(stats[:, t, :], hg[:, p, t, :])
                    last.then_inc(stats_done, 1)
                    wait_apart(v, cst, stats_done, n + 1)
                    for t in range(QT):
                        last = nc.vector.bn_aggr(mv[:, p, t, :], stats[:, t, :])
                    last.then_inc(step, 1)
                    v.wait_ge(xn_done, ONE + gg * 2)
                    v.wait_ge(step, ONE + n + 1)
                    nc.vector.tensor_scalar(rstd[:, p], mv[:, p, :, 1], EPS, None, ALU.add).then_inc(var_done, 1)
                    nc.vector.tensor_copy(keep["h1"][:, ds(n * QT, QT), :], hg[:, p]).then_inc(keep["h1_kept"], 1)
                for p in range(2):
                    v.wait_ge(rstd_done, ONE + gg * 2 + p + 1)
                    nc.vector.scalar_tensor_tensor(out=shift[:, p], in0=mv[:, p, :, 0], scalar=-1.0, in1=rstd[:, p],
                                                   op0=ALU.mult, op1=ALU.mult).then_inc(shift_done, 1)
                for p in range(2):
                    v.wait_ge(l_ready, ONE + gg * 2 + p + 1)
                    nc.vector.tensor_copy(logit[:, ds((gg * 2 + p) * QT, QT), :],
                                          ps_l[p][:, 0:QT * E].rearrange("p (t e) -> p t e", e=E)).then_inc(l_copied, 1)
            wide = [P, SEQ, E]
            at = [G]

            def done(ins):
                at[0] += 1
                ins.then_inc(step, 1)
                v.wait_ge(step, ONE + at[0])

            def rows(x):
                return x.unsqueeze(2).broadcast_to(wide)

            v.wait_ge(l_copied, ONE + G)
            done(nc.vector.tensor_reduce(row[:, :], logit[:, :, :], X, ALU.max))
            nc.vector.tensor_tensor(upto[:, :, :], logit[:, :, :], rows(row[:, :]), ALU.subtract).then_inc(less_top, 1)
            v.wait_ge(exp_done, ONE + 1)
            done(nc.vector.tensor_reduce(row[:, :], upto[:, :, :], X, ALU.add))
            done(nc.vector.reciprocal(row2[:, :], row[:, :]))
            done(nc.vector.tensor_tensor(prob[:, :, :], upto[:, :, :], rows(row2[:, :]), ALU.mult))
            for t in range(SEQ):
                last = nc.vector.max(best[:, t, :], prob[:, t, :])
            done(last)
            done(nc.vector.tensor_tensor(above[:, :, :], prob[:, :, :], rows(best[:, :, TOP - 1]), ALU.is_gt))
            done(nc.vector.tensor_tensor(equal[:, :, :], prob[:, :, :], rows(best[:, :, TOP - 1]), ALU.is_equal))
            done(nc.vector.tensor_reduce(row[:, :], above[:, :, :], X, ALU.add))
            done(nc.vector.tensor_scalar(row2[:, :], row[:, :], -1.0, float(TOP), ALU.mult, ALU.add))
            v.wait_ge(restart_done, ONE + 3)
            flat = lambda x: x[:, :, :].rearrange("p t e -> p (t e)")
            done(nc.vector.tensor_tensor_scan(flat(logit), flat(restart), flat(equal), 0.0, ALU.mult, ALU.add))
            done(nc.vector.tensor_tensor(logit[:, :, :], logit[:, :, :], rows(row2[:, :]), ALU.is_le))
            done(nc.vector.tensor_tensor(logit[:, :, :], logit[:, :, :], equal[:, :, :], ALU.mult))
            done(nc.vector.tensor_tensor(above[:, :, :], above[:, :, :], logit[:, :, :], ALU.add))
            nc.vector.tensor_tensor(upto[:, :, :], prob[:, :, :], rows(best[:, :, 0]), ALU.subtract).then_inc(less_top, 1)
            v.wait_ge(exp_done, ONE + 2)
            done(nc.vector.tensor_tensor(upto[:, :, :], upto[:, :, :], above[:, :, :], ALU.mult))
            done(nc.vector.tensor_reduce(row[:, :], upto[:, :, :], X, ALU.add))
            done(nc.vector.reciprocal(row2[:, :], row[:, :]))
            nc.vector.tensor_tensor(keep["comb"][:, :, :], upto[:, :, :], rows(row2[:, :]), ALU.mult).then_inc(keep["comb_kept"], 1)
            v.wait_ge(keep["comb_kept"], ONE + 1)
            with v.Fori(0, HG) as gg:
                for p in range(2):
                    v.wait_ge(c_ready, ONE + gg * 2)
                    nc.vector.tensor_copy(comb_now[:, p, :, 0:E],
                                          keep["comb"][:, ds((gg * 2 + p) * QT, QT), :]).then_inc(comb_done, 1)
                for p in range(2):
                    t = ds((gg * 2 + p) * QT, QT)
                    v.wait_ge(b_ready, ONE + gg * 2 + p + 1)
                    nc.vector.tensor_tensor(keep["h1"][:, t, :], ps_y[p][:, :].rearrange("p (t n) -> p t n", t=QT),
                                            keep["h1"][:, t, :], ALU.add).then_inc(b_added, 1)


def tower_phase(nc, d, cst, scr, keep, out):
    E, SH, F = 16, 2, 512
    S = E + SH
    FC = F // P
    H1, D1 = 8, 16
    N_IN, N_PR, D_PV, N_OUT = 512, 256, 64, 512
    K_IN, K_PR, K_OUT = 64, 128, 64
    R_IN, R_PR, R_OUT = K_IN // 8, K_PR // 8, K_OUT // 8
    SCALE = float(P) ** -0.5
    GONE, IS_GONE = -3e38, -1e38
    ND = QT * (R_IN + R_PR + R_OUT)
    with ExitStack() as ctx:
        def sb(name, shape, dt=F32):
            return ctx.enter_context(nc.sbuf_tensor(f"tow_{name}", shape, dt))

        sems = []

        def sem(name):
            sems.append(ctx.enter_context(nc.semaphore(f"tow_{name}")))
            return sems[-1]

        w1, w2, b1 = keep["w1"], keep["w2"], keep["b1"]
        h1, comb = keep["h1"], keep["comb"]
        xm = sb("xm", [P, W4])
        hid = sb("hid", [P, 2, FC, W4])
        wqkv = sb("wqkv1", [P, 3 * P])
        bqkv = sb("bqkv1", [P, 3 * P])
        wo = sb("wo1", [P, P])
        bo = sb("bo1", [1, P])
        gb = sb("gb", [P, 4])
        odd = sb("odd", [P, 2])
        gbk = sb("gbk", [P, 2, 2])
        stats = sb("stats", [P, 2 * QT, 6])
        mv = sb("mv", [P, 2 * QT, 2])
        pt = [sb(f"pool_tmp{i}", [P, 2 * QT]) for i in range(6)]
        sx = sb("sx", [P, QT, P])
        xt = sb("xt", [P, W4])
        qkv = sb("qkv", [P, QT, 3 * P])
        qk_n = sb("qk_n", [P, 2, QT, P])
        q_t = sb("q_t", [P, W4])
        k_t = sb("k_t", [P, 2, W4])
        top = sb("top", [P, 2, 4])
        ntop = sb("ntop", [P, 2, 4])
        z = sb("z", [P, QT, H1])
        rz = sb("rz", [P, QT, H1])
        p_s = sb("p_s", [P, 2, 4, P])
        p_t = sb("p_t", [P, 2, 4, P])
        w_in_t = sb("w_in_t", [P, N_IN])
        w_pr_t = sb("w_pr_t", [P, N_IN // P, N_PR])
        w_val = sb("w_val", [P, N_PR // P, D_PV])
        w_oi_t = sb("w_oi_t", [D_PV, N_OUT])
        w_out = sb("w_out", [P, N_OUT // P, P])
        acts = sb("acts", [P, QT, N_IN])
        oacts = sb("oacts", [P, QT, N_OUT])
        pacts = sb("pacts", [P, QT, N_PR])
        pexp = sb("pexp", [P, 2, N_PR])
        work = sb("work", [P, 2, N_IN])
        best = sb("best", [P, 2, 8])
        ptop = sb("ptop", [P, QT])
        chosen = sb("chosen", [P, 2, N_IN])
        ch_t = sb("ch_t", [P, N_IN])
        zp = sb("zp", [P, QT])
        rzp = sb("rzp", [P, QT])
        agg_t = sb("agg_t", [D_PV, 2, P])
        h_out = sb("h_out", [P, QT, P])
        bank = lambda name: ctx.enter_context(nc.psum_tensor(f"tow_{name}", [P, W4], F32))
        ps_h = [bank("ps_h0"), bank("ps_h1")]
        ps_y = [bank("ps_y0"), bank("ps_y1")]
        x0, x1, x2, x3 = [bank(f"ps_x{i}") for i in range(4)]

        def unit(u):
            r = u % 4
            return r, [(2 * (u // 4) + a, b, 2 * r + b) for a in range(2) for b in range(2)]

        names = """c_in c_half gbk_done xm_in h_ready hid_done y_ready y_added a_stats a_var a_pool a_scale a_silu a_t
            a_xt a_qkv a_bias a_stats2 a_var2 a_pool2 a_rstd2 a_norm a_qkt a_qkc a_s a_top a_ntop a_exp a_pt a_ptc a_pv
            a_rz a_on a_silu2 a_ot a_otc a_y h2_done f_stats f_var f_pool f_rstd f_norm f_t f_xt f_act f_acted found
            cleared chosen_done f_ct f_ctc f_pr f_practed f_exp f_rz f_agg f_aggc f_oact f_oacted f_out f_res
            out_done""".split()
        sm = {n: sem(n) for n in names}
        block = ctx.enter_context(nc.Block())

        R0 = {17: (0, 1), 18: (1, 2)}
        R1 = {0: (2, 5), 1: (5, 8), 2: (8, 10), 3: (10, 13), 4: (13, 16)}
        R2 = {5: (0, 5), 6: (5, 9), 7: (9, 14), 8: (14, 18), 9: (18, 23), 10: (23, 28), 11: (28, 32)}
        R3 = {12: (0, 4), 13: (4, 7), 14: (7, 9), 15: (9, 12), 16: (12, 14), 17: (14, 16)}
        S2 = {3: (0, 1), 5: (2, 3)}
        SE = {7: (0, 1), 9: (2, 3)}
        S3 = {10: (0, 1), 12: (2, 3)}
        S4 = {16: (0, 1), 18: (2, 3)}
        IN, QKV, TURN, SC, OUT, FIN, S1 = 1, 2, 4, 5, 11, 13, 14

        @block.sync
        def _(sp):
            for s in sems:
                sp.sem_inc(s, ONE)
            for dst, src in ((wqkv[:, :], "wqkv1"), (wo[:, :], "wo1"), (bo[:, :], "bo1"), (gb[:, :], "gb"),
                             (odd[:, :], "odd"), (w_in_t[:, :], "ip"), (w_pr_t[:, :, :], "piw"),
                             (w_val[:, :, :], "pval"), (w_oi_t[:, :], "oiw"), (w_out[:, :, :], "op")):
                sp.dma_start(dst, d[src]).then_inc(sm["c_in"], 16)
            sp.dma_start(bqkv[:, :], d["bqkv1"].partition_broadcast(P)).then_inc(sm["c_in"], 16)

            def load(k):
                sp.wait_ge(sm["h_ready"], ONE + k * (S * FC))
                sp.dma_start(xm[:, :], scr["xm"][ds(k, 1)].rearrange("a p n -> (a p) n")).then_inc(sm["xm_in"], 16)

            def store(f):
                sp.wait_ge(sm["f_res"], ONE + f * QT + QT)
                sp.dma_start(out[ds(f * QT, QT), :, :].rearrange("t p n -> p t n"),
                             h_out[:, :, :]).then_inc(sm["out_done"], 16)

            for k in range(3):
                load(k)
            with sp.Fori(3, G) as k:
                load(k)
                store(k - 3)
            for f in range(G - 3, G):
                store(f)
            sp.wait_ge(sm["out_done"], ONE + 16 * G)

        @block.gpsimd
        def _(pool):
            nh = cst["neg_half"]
            with pool.Fori(0, G) as j:
                n = [0]

                def done(ins):
                    n[0] += 1
                    ins.then_inc(sm["a_pool"], 1)
                    wait_apart(pool, cst, sm["a_pool"], j * 8 + n[0])

                wait_apart(pool, cst, sm["a_var"], j + 1)
                m, var = mv[:, 0:QT, 0], mv[:, 0:QT, 1]
                r1, sq, r2, sc, sh = (t[:, 0:QT] for t in pt[0:5])
                done(nc.gpsimd.tensor_scalar(sq, var, EPS, None, ALU.add))
                done(nc.gpsimd.tensor_tensor(r1, sq, nh[:, 0:QT], ALU.pow))
                done(nc.gpsimd.tensor_tensor(sq, r1, r1, ALU.mult))
                done(nc.gpsimd.tensor_tensor(sq, sq, var, ALU.mult))
                done(nc.gpsimd.tensor_scalar(sq, sq, EPS, None, ALU.add))
                done(nc.gpsimd.tensor_tensor(r2, sq, nh[:, 0:QT], ALU.pow))
                done(nc.gpsimd.tensor_tensor(sc, r1, r2, ALU.mult))
                done(nc.gpsimd.tensor_tensor(sh, m, sc, ALU.mult))
                nc.gpsimd.tensor_scalar(sh, sh, -1.0, None, ALU.mult).then_inc(sm["a_scale"], 1)
                wait_apart(pool, cst, sm["a_var2"], j + 1)
                nc.gpsimd.tensor_scalar(pt[5][:, :], mv[:, :, 1], EPS, None, ALU.add).then_inc(sm["a_pool2"], 1)
                pool.wait_ge(sm["a_pool2"], ONE + j * 3 + 1)
                nc.gpsimd.tensor_tensor(pt[5][:, :], pt[5][:, :], nh[:, 0:2 * QT], ALU.pow).then_inc(sm["a_pool2"], 1)
                pool.wait_ge(sm["a_pool2"], ONE + j * 3 + 2)
                nc.gpsimd.tensor_tensor(pt[4][:, :], mv[:, :, 0], pt[5][:, :], ALU.mult).then_inc(sm["a_pool2"], 1)
                wait_apart(pool, cst, sm["a_pool2"], j * 3 + 3)
                nc.gpsimd.tensor_scalar(pt[4][:, :], pt[4][:, :], -1.0, None, ALU.mult).then_inc(sm["a_rstd2"], 1)
                wait_apart(pool, cst, sm["f_var"], j + 1)
                nc.gpsimd.tensor_scalar(sq, var, EPS, None, ALU.add).then_inc(sm["f_pool"], 1)
                pool.wait_ge(sm["f_pool"], ONE + j * 3 + 1)
                nc.gpsimd.tensor_tensor(sc, sq, nh[:, 0:QT], ALU.pow).then_inc(sm["f_pool"], 1)
                pool.wait_ge(sm["f_pool"], ONE + j * 3 + 2)
                nc.gpsimd.tensor_tensor(sh, m, sc, ALU.mult).then_inc(sm["f_pool"], 1)
                wait_apart(pool, cst, sm["f_pool"], j * 3 + 3)
                nc.gpsimd.tensor_scalar(sh, sh, -1.0, None, ALU.mult).then_inc(sm["f_rstd"], 1)

        @block.tensor
        def _(pe):
            mm, tr, ident = nc.tensor.matmul, nc.tensor.transpose, cst["ident"]
            col = lambda t: slice(t * P, (t + 1) * P)

            def hidden(k, s):
                if s == 0:
                    pe.wait_ge(sm["xm_in"], ONE + k * 16 + 16)
                for c in range(FC):
                    n = s * FC + c
                    pe.wait_ge(sm["hid_done"], ONE + k * (S * FC) + max(n - 1, 0))
                    mm(ps_h[n % 2][:, :], w1[:, s, col(c)], xm[:, :], start=True, stop=True).then_inc(sm["h_ready"], 1)

            def expert_out(k, s, half):
                if half == 0:
                    pe.wait_ge(sm["hid_done"], ONE + k * (S * FC) + (s + 1) * FC)
                    pe.wait_ge(sm["y_added"], ONE + k * S + max(s - 1, 0))
                for t in (2 * half, 2 * half + 1):
                    for c in range(FC):
                        last = mm(ps_y[s % 2][:, col(t)], hid[:, s % 2, c, col(t)], w2[:, s, c, :],
                                  start=(c == 0), stop=(c == FC - 1))
                if half == 1:
                    last.then_inc(sm["y_ready"], 1)

            def attn_in(a):
                pe.wait_ge(sm["f_acted"], ONE + a * QT)
                if not isinstance(a, int) or a >= 2:
                    pe.wait_ge(sm["f_oacted"], ONE + (a - 1) * QT)
                pe.wait_ge(sm["a_silu"], ONE + a + 1)
                for t in range(QT):
                    last = tr(x0[:, col(t)], sx[:, t, :], ident[:, :])
                last.then_inc(sm["a_t"], 1)

            def attn_qkv(a, tiles):
                pe.wait_ge(sm["a_xt"], ONE + a + 1)
                for t in tiles:
                    if t >= 2:
                        pe.wait_ge(sm["a_bias"], ONE + a * QT + t - 1)
                    mm((x0, x1)[t % 2][:, 0:3 * P], xt[:, col(t)], wqkv[:, :],
                       start=True, stop=True).then_inc(sm["a_qkv"], 1)

            def attn_turn(a):
                pe.wait_ge(sm["a_norm"], ONE + a + 1)
                for i, x in enumerate((x0, x1)):
                    for t in range(QT):
                        last = tr(x[:, col(t)], qk_n[:, i, t, :], ident[:, :])
                    last.then_inc(sm["a_qkt"], 1)

            def attn_scores(a, u):
                if u >= 2:
                    pe.wait_ge(sm["a_exp"], ONE + a * 8 + u - 1)
                else:
                    pe.wait_ge(sm["a_qkc"], ONE + a * 3 + 3)
                r, cells = unit(u)
                rows = slice(32 * r, 32 * r + 32)
                for c, (t, b, h) in enumerate(cells):
                    last = mm((x0, x1)[u % 2][:, col(c)], q_t[rows, col(t)], k_t[rows, b, col(t)],
                              start=True, stop=True)
                last.then_inc(sm["a_s"], 1)

            def attn_turn_probs(a, u):
                pe.wait_ge(sm["a_exp"], ONE + a * 8 + u + 1)
                pe.wait_ge(sm["a_ptc"], ONE + a * 8 + u)
                for c in range(4):
                    last = tr(x2[:, col(c)], p_s[:, u % 2, c, :], ident[:, :])
                last.then_inc(sm["a_pt"], 1)

            def attn_values(a, u):
                if u == 0 and (not isinstance(a, int) or a >= 1):
                    pe.wait_ge(sm["f_practed"], ONE + (a - 1) * QT + QT)
                if u % 2 == 0:
                    pe.wait_ge(sm["a_on"], ONE + a * 4 + u // 2)
                pe.wait_ge(sm["a_ptc"], ONE + a * 8 + u + 1)
                for c, (t, b, h) in enumerate(unit(u)[1]):
                    last = mm(x3[:, t * P + h * D1:t * P + (h + 1) * D1], p_t[:, u % 2, c, :],
                              qkv[:, t, 2 * P + h * D1:2 * P + (h + 1) * D1], start=True, stop=True)
                last.then_inc(sm["a_pv"], 1)

            def attn_out_turn(a, f):
                pe.wait_ge(sm["a_silu2"], ONE + a + 1)
                if f is not None:
                    pe.wait_ge(sm["f_oacted"], ONE + f * QT + 2)
                for t in range(QT):
                    last = tr(x0[:, col(t)], sx[:, t, :], ident[:, :])
                last.then_inc(sm["a_ot"], 1)

            def attn_out(a):
                pe.wait_ge(sm["a_otc"], ONE + a + 1)
                for t in range(QT):
                    mm(x1[:, col(t)], xt[:, col(t)], wo[:, :], start=True, stop=False)
                    last = mm(x1[:, col(t)], cst["ones_row"][:, :], bo[:, :], start=False, stop=True)
                last.then_inc(sm["a_y"], 1)

            def ffn_in(a, f):
                pe.wait_ge(sm["f_norm"], ONE + a + 1)
                if f is not None:
                    pe.wait_ge(sm["f_oacted"], ONE + f * QT + QT)
                for t in range(QT):
                    last = tr(x0[:, col(t)], sx[:, t, :], ident[:, :])
                last.then_inc(sm["f_t"], 1)

            def input_acts(a, tiles):
                pe.wait_ge(sm["f_xt"], ONE + a + 1)
                for t in tiles:
                    if t >= 2:
                        pe.wait_ge(sm["f_acted"], ONE + a * QT + t - 1)
                    mm((x1, x0)[t % 2][:, :], xt[:, col(t)], w_in_t[:, :], start=True, stop=True).then_inc(sm["f_act"], 1)

            def turn_chosen(f, i, t, chunks):
                n = i * QT + t
                pe.wait_ge(sm["chosen_done"], ONE + f * (3 * QT) + n + 1)
                pe.wait_ge(sm["f_ctc"], ONE + f * (3 * QT) + n)
                for c in range(chunks):
                    last = tr(x2[:, col(c)], chosen[:, t % 2, col(c)], ident[:, :])
                last.then_inc(sm["f_ct"], 1)

            def process_acts(f, t):
                pe.wait_ge(sm["f_ctc"], ONE + f * (3 * QT) + t + 1)
                pe.wait_ge(sm["f_res"], ONE + f * QT)
                pe.wait_ge(sm["f_practed"], ONE + f * QT + t)
                for c in range(N_IN // P):
                    last = mm(x3[:, 0:N_PR], ch_t[:, col(c)], w_pr_t[:, c, :], start=(c == 0), stop=(c == N_IN // P - 1))
                last.then_inc(sm["f_pr"], 1)

            def aggregate(f, a, t):
                if a is not None:
                    pe.wait_ge(sm["a_on"], ONE + a * 4 + 4)
                pe.wait_ge(sm["f_ctc"], ONE + f * (3 * QT) + QT + t + 1)
                pe.wait_ge(sm["f_practed"], ONE + f * QT + QT)
                pe.wait_ge(sm["f_aggc"], ONE + f * QT + t)
                for c in range(N_PR // P):
                    last = mm(x3[0:D_PV, 0:P], w_val[:, c, :], ch_t[:, col(c)], start=(c == 0), stop=(c == N_PR // P - 1))
                last.then_inc(sm["f_agg"], 1)

            def output_acts(f, a, t):
                if a is not None:
                    if t < 2:
                        pe.wait_ge(sm["a_exp"], ONE + a * 8 + 8)
                    else:
                        pe.wait_ge(sm["h2_done"], ONE + a + 1)
                elif t >= 2:
                    pe.wait_ge(sm["f_oacted"], ONE + f * QT + t - 1)
                else:
                    pe.wait_ge(sm["f_acted"], ONE + G * QT)
                pe.wait_ge(sm["f_aggc"], ONE + f * QT + t + 1)
                mm((x0, x1)[t % 2][:, :], agg_t[:, t % 2, :], w_oi_t[:, :], start=True, stop=True).then_inc(sm["f_oact"], 1)

            def outputs(f, t):
                pe.wait_ge(sm["f_ctc"], ONE + f * (3 * QT) + 2 * QT + t + 1)
                pe.wait_ge(sm["f_aggc"], ONE + f * QT + QT)
                pe.wait_ge(sm["f_res"], ONE + f * QT + t)
                for c in range(N_OUT // P):
                    last = mm(x3[:, 0:P], ch_t[:, col(c)], w_out[:, c, :], start=(c == 0), stop=(c == N_OUT // P - 1))
                last.then_inc(sm["f_out"], 1)

            def patterns_first(f, s):
                for i, (plan, chunks) in enumerate(((S2, N_IN // P), (S3, N_PR // P), (S4, N_OUT // P))):
                    if s in plan:
                        turn_chosen(f, i, plan[s][0], chunks)

            def patterns_middle(f, a, s):
                if s in S2:
                    process_acts(f, S2[s][0])
                    turn_chosen(f, 0, S2[s][1], N_IN // P)
                if s in S3:
                    aggregate(f, a, S3[s][0])
                    turn_chosen(f, 1, S3[s][1], N_PR // P)
                if s in S4:
                    outputs(f, S4[s][0])
                    turn_chosen(f, 2, S4[s][1], N_OUT // P)

            def patterns_last(f, a, s):
                if s in S2:
                    process_acts(f, S2[s][1])
                if s in S3:
                    aggregate(f, a, S3[s][1])
                    output_acts(f, a, S3[s][0])
                    output_acts(f, a, S3[s][1])
                if s in S4:
                    outputs(f, S4[s][1])

            def one_pass(k, a, f):
                for s in range(S + 1):
                    if k is not None and s < S:
                        hidden(k, s)
                    if a is not None:
                        for u in range(8):
                            if s == SC + 2 + u // 2:
                                attn_values(a, u)
                        if s == QKV:
                            attn_qkv(a, (0, 1))
                        if s == TURN:
                            attn_turn(a)
                        if s == OUT:
                            attn_out_turn(a, f)
                        if s == FIN:
                            ffn_in(a, f)
                        if s == S1:
                            input_acts(a, (0, 1))
                    if f is not None:
                        patterns_first(f, s)
                    if k is not None and s:
                        expert_out(k, s - 1, 0)
                    if f is not None:
                        patterns_middle(f, a, s)
                    if a is not None:
                        if s == S1:
                            input_acts(a, (2, 3))
                    if k is not None and s:
                        expert_out(k, s - 1, 1)
                    if f is not None:
                        patterns_last(f, a, s)
                    if a is not None:
                        if s == IN:
                            attn_in(a)
                        if s == OUT:
                            attn_out(a)
                        if s == QKV:
                            attn_qkv(a, (2, 3))
                        for u in range(10):
                            if u >= 2 and s == SC + u // 2:
                                attn_turn_probs(a, u - 2)
                            if u < 8 and s == SC + u // 2:
                                attn_scores(a, u)

            pe.wait_ge(keep["w_in"], 16 * keep["w_loads"])
            pe.wait_ge(sm["c_half"], ONE + 1)
            pe.wait_ge(sm["c_in"], ONE + 16 * 11)
            one_pass(0, None, None)
            one_pass(1, 0, None)
            with pe.Fori(2, G) as k:
                one_pass(k, k - 1, k - 2)
            one_pass(None, G - 1, G - 2)
            one_pass(None, None, G - 1)

        @block.scalar
        def _(act):
            def hidden(k, s):
                act.wait_ge(sm["y_ready"], ONE + k * S + max(s - 1, 0))
                for c in range(FC):
                    n = s * FC + c
                    act.wait_ge(sm["h_ready"], ONE + k * (S * FC) + n + 1)
                    nc.scalar.activation(hid[:, s % 2, c, :], ps_h[n % 2][:, :], ACT.Gelu,
                                         bias=b1[:, s, c:c + 1]).then_inc(sm["hid_done"], 1)

            def attn_exps(a, u):
                if u >= 2:
                    act.wait_ge(sm["a_pt"], ONE + a * 8 + u - 1)
                act.wait_ge(sm["a_ntop"], ONE + a * 8 + u + 1)
                for c, (t, b, h) in enumerate(unit(u)[1]):
                    last = nc.scalar.activation(p_s[:, u % 2, c, :], (x0, x1)[u % 2][:, c * P:(c + 1) * P],
                                                ACT.Exp, bias=ntop[:, u % 2, c:c + 1], scale=SCALE,
                                                accum_out=z[:, t, h:h + 1])
                last.then_inc(sm["a_exp"], 1)

            def attn_copy(a, u):
                act.wait_ge(sm["a_pt"], ONE + a * 8 + u + 1)
                act.wait_ge(sm["a_pv"], ONE + a * 8 + max(u - 1, 0))
                nc.scalar.copy(p_t[:, u % 2].rearrange("p c n -> p (c n)"), x2[:, :]).then_inc(sm["a_ptc"], 1)

            def heads_silu(a):
                act.wait_ge(sm["a_on"], ONE + a * 4 + 4)
                act.wait_ge(sm["a_t"], ONE + a + 1)
                flat = sx[:, :, :].rearrange("p t n -> p (t n)")
                nc.scalar.activation(flat, qk_n[:, 0].rearrange("p t n -> p (t n)"), ACT.Silu).then_inc(sm["a_silu2"], 1)

            def attention(a, s, silued):
                if s == IN:
                    act.wait_ge(sm["a_scale"], ONE + a + 1)
                    act.wait_ge(sm["f_t"], ONE + a)
                    for t in range(QT):
                        last = nc.scalar.activation(sx[:, t, :], h1[:, ds(a * QT + t, 1), :].rearrange("p a n -> p (a n)"),
                                                    ACT.Silu, bias=pt[4][:, t:t + 1], scale=pt[3][:, t:t + 1])
                    last.then_inc(sm["a_silu"], 1)
                    act.wait_ge(sm["a_t"], ONE + a + 1)
                    act.wait_ge(sm["f_act"], ONE + a * QT)
                    nc.scalar.copy(xt[:, :], x0[:, :]).then_inc(sm["a_xt"], 1)
                if s == TURN:
                    act.wait_ge(sm["a_qkt"], ONE + a * 2 + 1)
                    act.wait_ge(sm["a_s"], ONE + a * 8)
                    nc.scalar.activation(q_t[:, :], x0[:, :], ACT.Identity, bias=gb[:, 1:2], scale=gb[:, 0:1]).then_inc(sm["a_qkc"], 1)
                    act.wait_ge(sm["a_qkt"], ONE + a * 2 + 2)
                    for b in range(2):
                        nc.scalar.activation(k_t[:, b, :], x1[:, :], ACT.Identity, bias=gbk[:, 1, b:b + 1],
                                             scale=gbk[:, 0, b:b + 1]).then_inc(sm["a_qkc"], 1)
                for u in range(8):
                    if s == SC + 1 + u // 2:
                        attn_exps(a, u)
                for u in range(8):
                    if s == SC + 1 + u // 2:
                        attn_copy(a, u)
                if s == OUT - 1 and not silued:
                    heads_silu(a)
                if s == OUT:
                    act.wait_ge(sm["a_ot"], ONE + a + 1)
                    act.wait_ge(sm["a_qkv"], ONE + a * QT + QT)
                    nc.scalar.copy(xt[:, :], x0[:, :]).then_inc(sm["a_otc"], 1)
                if s == FIN:
                    act.wait_ge(sm["f_t"], ONE + a + 1)
                    act.wait_ge(sm["a_y"], ONE + a + 1)
                    nc.scalar.copy(xt[:, :], x0[:, :]).then_inc(sm["f_xt"], 1)
                if s == S1:
                    for t in range(QT):
                        act.wait_ge(sm["f_act"], ONE + a * QT + t + 1)
                        if not isinstance(a, int) or a >= 1:
                            act.wait_ge(sm["chosen_done"], ONE + (a - 1) * (3 * QT) + QT)
                        nc.scalar.activation(acts[:, t, :], (x1, x0)[t % 2][:, :], ACT.Gelu).then_inc(sm["f_acted"], 1)

            def patterns(f, a, s):
                def turn_chosen(i, t, n):
                    m = i * QT + t
                    act.wait_ge(sm["f_ct"], ONE + f * (3 * QT) + m + 1)
                    if i == 0:
                        act.wait_ge(sm["f_pr"], ONE + f * QT + t)
                        act.wait_ge(sm["f_out"], ONE + f * QT)
                    if i == 1:
                        act.wait_ge(sm["f_agg"], ONE + f * QT + t)
                        act.wait_ge(sm["f_pr"], ONE + f * QT + QT)
                    if i == 2:
                        act.wait_ge(sm["f_out"], ONE + f * QT + t)
                        act.wait_ge(sm["f_agg"], ONE + f * QT + QT)
                    nc.scalar.copy(ch_t[:, 0:n], x2[:, 0:n]).then_inc(sm["f_ctc"], 1)

                def aggregate(t):
                    act.wait_ge(sm["f_agg"], ONE + f * QT + t + 1)
                    if t >= 2:
                        act.wait_ge(sm["f_oact"], ONE + f * QT + t - 1)
                    else:
                        act.wait_ge(sm["f_oact"], ONE + f * QT)
                    nc.scalar.copy(agg_t[:, t % 2, :], x3[0:D_PV, 0:P]).then_inc(sm["f_aggc"], 1)

                def output_act(t):
                    act.wait_ge(sm["f_oact"], ONE + f * QT + t + 1)
                    act.wait_ge(sm["f_rz"], ONE + f * QT + t + 1)
                    nc.scalar.activation(oacts[:, t, :], (x0, x1)[t % 2][:, :], ACT.Gelu, scale=rzp[:, t:t + 1]).then_inc(sm["f_oacted"], 1)

                for t in S2.get(s, ()):
                    turn_chosen(0, t, N_IN)
                    act.wait_ge(sm["f_pr"], ONE + f * QT + t + 1)
                    nc.scalar.activation(pacts[:, t, :], x3[:, 0:N_PR], ACT.Gelu).then_inc(sm["f_practed"], 1)
                for t in SE.get(s, ()):
                    act.wait_ge(sm["cleared"], ONE + f * ND + QT * R_IN + (t // 2) * (2 * R_PR) + t % 2 + 1)
                    if t >= 2:
                        act.wait_ge(sm["chosen_done"], ONE + f * (3 * QT) + QT + t - 1)
                    nc.scalar.activation(pexp[:, t % 2, :], pacts[:, t, :], ACT.Exp, bias=ptop[:, t:t + 1]).then_inc(sm["f_exp"], 1)
                if s in S3:
                    t0, t1 = S3[s]
                    turn_chosen(1, t0, N_PR)
                    aggregate(t0)
                    if s == OUT - 1 and a is not None:
                        heads_silu(a)
                    turn_chosen(1, t1, N_PR)
                    aggregate(t1)
                    output_act(t0)
                    output_act(t1)
                for t in S4.get(s, ()):
                    turn_chosen(2, t, N_OUT)

            def one_pass(k, a, f):
                for s in range(S + 1):
                    if k is not None and s < S:
                        hidden(k, s)
                    if f is not None:
                        patterns(f, a, s)
                    if a is not None:
                        attention(a, s, OUT - 1 in S3 and f is not None)

            act.wait_ge(keep["w_in"], 16 * keep["w_loads"])
            act.wait_ge(sm["c_in"], ONE + 16 * 11)
            act.wait_ge(sm["gbk_done"], ONE + 2)
            one_pass(0, None, None)
            one_pass(1, 0, None)
            with act.Fori(2, G) as k:
                one_pass(k, k - 1, k - 2)
            one_pass(None, G - 1, G - 2)
            one_pass(None, None, G - 1)

        @block.vector
        def _(v):
            tt, ts, stt = nc.vector.tensor_tensor, nc.vector.tensor_scalar, nc.vector.scalar_tensor_tensor
            four = lambda x: x[:, :].rearrange("p (t n) -> p t n", t=QT)
            tile = lambda j, t: h1[:, ds(j * QT + t, 1), :].rearrange("p a n -> p (a n)")
            group = lambda j: h1[:, ds(j * QT, QT), :]

            def add_expert(k, s):
                v.wait_ge(sm["y_ready"], ONE + k * S + s + 1)
                v.wait_ge(sm["y_added"], ONE + k * S + s)
                if s < SH:
                    tt(group(k), four(ps_y[s % 2]), group(k), ALU.add).then_inc(sm["y_added"], 1)
                    return
                for t in range(QT):
                    last = stt(out=tile(k, t), in0=ps_y[s % 2][:, t * P:(t + 1) * P],
                               scalar=comb[:, ds(k * QT + t, 1), s - SH], in1=tile(k, t), op0=ALU.mult, op1=ALU.add)
                last.then_inc(sm["y_added"], 1)

            def attn_first(a):
                v.wait_ge(sm["y_added"], ONE + a * S + S)
                wait_apart(v, cst, sm["f_rstd"], a)
                for t in range(QT):
                    last = nc.vector.bn_stats(stats[:, t, :], tile(a, t))
                last.then_inc(sm["a_stats"], 1)
                wait_apart(v, cst, sm["a_stats"], a + 1)
                for t in range(QT):
                    last = nc.vector.bn_aggr(mv[:, t, :], stats[:, t, :])
                last.then_inc(sm["a_var"], 1)

            def attn_bias(a, tiles):
                v.wait_ge(sm["a_pv"], ONE + a * 8)
                for t in tiles:
                    v.wait_ge(sm["a_qkv"], ONE + a * QT + t + 1)
                    tt(qkv[:, t, :], (x0, x1)[t % 2][:, 0:3 * P], bqkv[:, :], ALU.add).then_inc(sm["a_bias"], 1)

            def attn_moments(a):
                v.wait_ge(sm["a_bias"], ONE + a * QT + QT)
                v.wait_ge(sm["a_scale"], ONE + a + 1)
                for i in range(2):
                    for t in range(QT):
                        last = nc.vector.bn_stats(stats[:, i * QT + t, :], qkv[:, t, i * P:(i + 1) * P])
                last.then_inc(sm["a_stats2"], 1)
                wait_apart(v, cst, sm["a_stats2"], a + 1)
                for i in range(2 * QT):
                    last = nc.vector.bn_aggr(mv[:, i, :], stats[:, i, :])
                last.then_inc(sm["a_var2"], 1)

            def attn_norm(a):
                v.wait_ge(sm["a_rstd2"], ONE + a + 1)
                v.wait_ge(sm["a_silu2"], ONE + a)
                for i in range(2):
                    for t in range(QT):
                        n = i * QT + t
                        last = ts(qk_n[:, i, t, :], qkv[:, t, i * P:(i + 1) * P], pt[5][:, n:n + 1], pt[4][:, n:n + 1],
                                  ALU.mult, ALU.add)
                last.then_inc(sm["a_norm"], 1)

            def attn_top(a, u):
                v.wait_ge(sm["a_s"], ONE + a * 8 + u + 1)
                if u >= 2:
                    v.wait_ge(sm["a_exp"], ONE + a * 8 + u - 1)
                nc.vector.tensor_reduce(top[:, u % 2, :], four((x0, x1)[u % 2]), X, ALU.max).then_inc(sm["a_top"], 1)
                v.wait_ge(sm["a_top"], ONE + a * 8 + u + 1)
                ts(ntop[:, u % 2, :], top[:, u % 2, :], -SCALE, None, ALU.mult).then_inc(sm["a_ntop"], 1)

            def attn_divide(a, j):
                t, h = 2 * (j // 2), 4 * (j % 2)
                v.wait_ge(sm["a_exp"], ONE + a * 8 + 2 * j + 2)
                nc.vector.reciprocal(rz[:, t:t + 2, h:h + 4], z[:, t:t + 2, h:h + 4]).then_inc(sm["a_rz"], 1)
                v.wait_ge(sm["a_rz"], ONE + a * 4 + j + 1)
                v.wait_ge(sm["a_pv"], ONE + a * 8 + 2 * j + 2)
                heads = lambda x: x.rearrange("p t (h d) -> p t h d", h=4)
                tt(heads(qk_n[:, 0, t:t + 2, h * D1:(h + 4) * D1]), heads(four(x3)[:, t:t + 2, h * D1:(h + 4) * D1]),
                   rz[:, t:t + 2, h:h + 4].unsqueeze(3).broadcast_to([P, 2, 4, D1]), ALU.mult).then_inc(sm["a_on"], 1)

            def attn_add(a):
                v.wait_ge(sm["a_y"], ONE + a + 1)
                tt(group(a), four(x1), group(a), ALU.add).then_inc(sm["h2_done"], 1)
                wait_apart(v, cst, sm["h2_done"], a + 1)
                for t in range(QT):
                    last = nc.vector.bn_stats(stats[:, t, :], tile(a, t))
                last.then_inc(sm["f_stats"], 1)
                wait_apart(v, cst, sm["f_stats"], a + 1)
                for t in range(QT):
                    last = nc.vector.bn_aggr(mv[:, t, :], stats[:, t, :])
                last.then_inc(sm["f_var"], 1)

            def ffn_norm(a):
                v.wait_ge(sm["f_rstd"], ONE + a + 1)
                v.wait_ge(sm["a_ot"], ONE + a + 1)
                for t in range(QT):
                    last = ts(sx[:, t, :], tile(a, t), pt[3][:, t:t + 1], pt[4][:, t:t + 1], ALU.mult, ALU.add)
                last.then_inc(sm["f_norm"], 1)

            def choose(f, i, n):
                rounds = (R_IN, R_PR, R_OUT)[i]
                width = (N_IN, N_PR, N_OUT)[i]
                r = n % rounds
                tiles = [2 * (n // rounds), 2 * (n // rounds) + 1]
                at = f * ND + QT * sum((R_IN, R_PR, R_OUT)[:i]) + 2 * n
                src = [(acts, pacts, oacts)[i][:, t, :] if r == 0 else work[:, t % 2, 0:width] for t in tiles]
                for b, t in enumerate(tiles):
                    if r == 0:
                        wait_apart(v, cst, sm[("f_acted", "f_practed", "f_oacted")[i]], f * QT + t + 1)
                    else:
                        wait_apart(v, cst, sm["cleared"], at - 1 + b)
                    nc.vector.max(best[:, b, :], src[b]).then_inc(sm["found"], 1)
                for b, t in enumerate(tiles):
                    if i == 1 and r == 0:
                        v.wait_ge(sm["found"], ONE + at + 1 + b)
                        ts(ptop[:, t:t + 1], best[:, b, 0:1], -1.0, None, ALU.mult)
                    wait_apart(v, cst, sm["found"], at + 1 + b)
                    nc.vector.match_replace(work[:, b, 0:width], best[:, b, :], src[b], GONE).then_inc(sm["cleared"], 1)
                if r < rounds - 1:
                    return
                for b, t in enumerate(tiles):
                    m = i * QT + t
                    v.wait_ge(sm["cleared"], ONE + at + 1 + b)
                    v.wait_ge(sm["f_ct"], ONE + f * (3 * QT) + max(m - 1, 0))
                    wk, ch = work[:, b, 0:width], chosen[:, b, 0:width]
                    if i == 1:
                        v.wait_ge(sm["f_exp"], ONE + f * QT + t + 1)
                        stt(out=ch, in0=wk, scalar=IS_GONE, in1=pexp[:, t % 2, :], op0=ALU.is_lt, op1=ALU.mult,
                            accum_out=zp[:, t:t + 1]).then_inc(sm["chosen_done"], 1)
                        v.wait_ge(sm["chosen_done"], ONE + f * (3 * QT) + m + 1)
                        nc.vector.reciprocal(rzp[:, t:t + 1], zp[:, t:t + 1]).then_inc(sm["f_rz"], 1)
                    else:
                        stt(out=ch, in0=wk, scalar=IS_GONE, in1=(acts, None, oacts)[i][:, t, :], op0=ALU.is_lt,
                            op1=ALU.mult).then_inc(sm["chosen_done"], 1)

            def finish(f, t):
                v.wait_ge(sm["f_out"], ONE + f * QT + t + 1)
                if t == 0:
                    v.wait_ge(sm["out_done"], ONE + f * 16)
                tt(h_out[:, t, :], x3[:, 0:P], tile(f, t), ALU.add).then_inc(sm["f_res"], 1)

            def one_pass(k, a, f):
                for s in range(S + 1):
                    if a is not None:
                        if s == IN - 1:
                            attn_first(a)
                        if s == QKV + 1:
                            attn_norm(a)
                        for u in range(8):
                            if s == SC + 1 + u // 2:
                                attn_top(a, u)
                        if s == OUT + 1:
                            ffn_norm(a)
                    todo = [(i, n) for i, rounds in enumerate((R1, R2, R3)) for n in range(*rounds.get(s, (0, 0)))]
                    if f is not None:
                        for i, n in todo[:1]:
                            choose(f, i, n)
                    if a is not None:
                        if s == QKV:
                            attn_bias(a, (0, 1))
                        if SC + 2 <= s < SC + 6:
                            attn_divide(a, s - SC - 2)
                    if f is not None:
                        for i, n in todo[1:]:
                            choose(f, i, n)
                    if a is not None:
                        for n in range(*R0.get(s, (0, 0))):
                            choose(a, 0, n)
                        if s == QKV:
                            attn_bias(a, (2, 3))
                            attn_moments(a)
                        if s == OUT:
                            attn_add(a)
                    if f is not None and s in S4:
                        finish(f, S4[s][0])
                    if k is not None and s:
                        add_expert(k, s - 1)
                    if f is not None and s in S4:
                        finish(f, S4[s][1])

            v.wait_ge(keep["w_in"], 16 * keep["w_loads"])
            shared = w2[:, 0:SH].rearrange("p s c n -> p (s c n)")
            ts(shared, shared, 1.0 / SH, None, ALU.mult).then_inc(sm["c_half"], 1)
            v.wait_ge(sm["c_in"], ONE + 16 * 11)
            for i in range(2):
                ts(gbk[:, i, :], odd[:, :], gb[:, 2 + i:3 + i], None, ALU.mult).then_inc(sm["gbk_done"], 1)
            one_pass(0, None, None)
            one_pass(1, 0, None)
            with v.Fori(2, G) as k:
                one_pass(k, k - 1, k - 2)
            one_pass(None, G - 1, G - 2)
            one_pass(None, None, G - 1)


def lm_tower(nc, d, out):
    E, SH, FC = 16, 2, 4
    scr = {
        "h": nc.dram_tensor("scr_h", [G, P, W4], F32).ap(),
        "xt": nc.dram_tensor("scr_xt", [G, P, W4], F32).ap(),
        "o": nc.dram_tensor("scr_o", [4, P, SEQ * P], F32).ap(),
        "xm": nc.dram_tensor("scr_xm", [G, P, W4], F32).ap(),
    }
    with ExitStack() as ctx:
        cst = {
            "ident": ctx.enter_context(nc.sbuf_tensor("ident", [P, P], F32)),
            "neg_half": ctx.enter_context(nc.sbuf_tensor("neg_half", [P, SEQ], F32)),
            "ones_row": ctx.enter_context(nc.sbuf_tensor("ones_row", [1, P], F32)),
            "pool_step": ctx.enter_context(nc.semaphore("pool_step")),
            "consts_done": ctx.enter_context(nc.semaphore("consts_done")),
        }
        tokens_phase(nc, d, cst, scr)
        attention0_phase(nc, d, cst, scr)
        keep = {
            "h1": ctx.enter_context(nc.sbuf_tensor("h1", [P, SEQ, P], F32)),
            "comb": ctx.enter_context(nc.sbuf_tensor("comb", [P, SEQ, E], F32)),
            "w1": ctx.enter_context(nc.sbuf_tensor("w1", [P, E + SH, FC * P], F32)),
            "w2": ctx.enter_context(nc.sbuf_tensor("w2", [P, E + SH, FC, P], F32)),
            "b1": ctx.enter_context(nc.sbuf_tensor("b1", [P, E + SH, FC], F32)),
            "h1_kept": ctx.enter_context(nc.semaphore("h1_kept")),
            "comb_kept": ctx.enter_context(nc.semaphore("comb_kept")),
            "w_in": ctx.enter_context(nc.semaphore("experts_in")),
            "w_loads": 3,
        }
        mix_phase(nc, d, cst, scr, keep)
        tower_phase(nc, d, cst, scr, keep, out)


def kernel(**inputs):
    import numpy as np
    import concourse.bacc as bacc
    from concourse import mybir as mb
    from concourse.bass_utils import run_bass_kernel_spmd as run

    a = {k: np.asarray(v) for k, v in inputs.items()}
    L = lambda x: np.ascontiguousarray(x)
    lay = {
        "ids": L(a["x"].T),
        "wt": L(a["L0_tok_W"].T),
        "tok_b": a["L0_tok_b"],
        "bo": a["L0_attn_bo"],
        "wqkv": L(np.stack([a[f"L0_attn_W{n}"].reshape(128, 4, 128) for n in "qkv"], 0).transpose(2, 1, 0, 3)),
        "bqkv": L(np.stack([a[f"L0_attn_b{n}"].reshape(4, 128) for n in "qkv"], 0).transpose(1, 2, 0)),
        "pk": np.tile(a["L0_attn_P_k"].T, (1, 128)),
        "pv": L(a["L0_attn_P_v"].transpose(1, 0, 2)),
        "wo": L(a["L0_attn_Wo"].reshape(4, 128, 128).transpose(1, 0, 2)),
        "gate": L(a["L0_ffn_gate_w"].T),
        "b2": np.concatenate([a["L0_ffn_re_b2"], a["L0_ffn_se_b2"]]),
        "w1": L(np.concatenate([a["L0_ffn_se_w1"], a["L0_ffn_re_w1"]]).transpose(1, 0, 2)),
        "w2": L(np.concatenate([a["L0_ffn_se_w2"], a["L0_ffn_re_w2"]]).reshape(18, 4, 128, 128).transpose(2, 0, 1, 3)),
        "b1": L(np.concatenate([a["L0_ffn_se_b1"], a["L0_ffn_re_b1"]]).reshape(18, 4, 128).transpose(2, 0, 1)),
        "wqkv1": np.concatenate([a[f"L1_attn_w_{n}"] for n in "qkv"], 1),
        "bqkv1": np.concatenate([a[f"L1_attn_b_{n}"] for n in "qkv"]),
        "wo1": a["L1_attn_w_o"],
        "bo1": a["L1_attn_b_o"].reshape(1, 128),
        "gb": L(np.stack([a[f"L1_attn_{n}"] for n in ("g_q", "be_q", "g_k", "be_k")], 1)),
        "odd": np.stack([np.arange(128) // 16 % 2 == b for b in range(2)], 1).astype(np.float32),
        "ip": L(a["L1_ffn_input_patterns"].T),
        "piw": L(a["L1_ffn_process_input_weights"].T.reshape(4, 128, 256).transpose(1, 0, 2)),
        "pval": L(a["L1_ffn_process_values"].reshape(2, 128, 64).transpose(1, 0, 2)),
        "oiw": L(a["L1_ffn_output_input_weights"].T),
        "op": L(a["L1_ffn_output_patterns"].reshape(4, 128, 128).transpose(1, 0, 2)),
    }
    nc = bacc.Bacc("TRN2", target_bir_lowering=False, num_devices=1)
    arrays, args = {}, {}
    for name, arr in lay.items():
        arrays[f"in_{name}"] = arr
        args[name] = nc.dram_tensor(f"in_{name}", arr.shape, mb.dt.from_np(arr.dtype), kind="ExternalInput").ap()
    out = nc.dram_tensor("out_h", (SEQ, P, P), mb.dt.float32, kind="ExternalOutput").ap()
    lm_tower(nc, args, out)
    r = run(nc, [arrays], core_ids=[0])
    return r.results[0]["out_h"]
```

```python
from contextlib import ExitStack

import concourse.bass as bass
from concourse import mybir

ALU = mybir.AluOpType
ACT = mybir.ActivationFunctionType
F32 = mybir.dt.float32
U32 = mybir.dt.uint32
X = mybir.AxisListType.X
ds = bass.ds

P = 128
SEQ = 64
QT = 4
G = SEQ // QT
W4 = QT * P
EPS = 1e-5
ONE = 1


def wait_apart(eng, cst, sem, value):
    value = ONE + value
    if not isinstance(value, int):
        value = eng.snap(eng.compute_val(value))
        eng.wait_ge(cst["consts_done"], ONE + 3)
    eng.wait_ge(sem, value)


def tokens_phase(nc, d, cst, scr):
    with ExitStack() as ctx:
        def sb(name, shape, dt=F32):
            return ctx.enter_context(nc.sbuf_tensor(f"tok_{name}", shape, dt))

        sems = []

        def sem(name):
            sems.append(ctx.enter_context(nc.semaphore(f"tok_{name}")))
            return sems[-1]

        ids = sb("ids", [P, SEQ], U32)
        ids_now = sb("ids_now", [P, 2, QT], U32)
        feat = sb("feat", [P, 2, QT, P])
        tok_b = sb("tok_b", [P, P])
        out_b = sb("out_b", [P, P])
        h_now = sb("h_now", [P, 2, QT, P])
        square = sb("square", [P, 2, QT, P])
        ssq = sb("ssq", [P, 2, QT])
        inv = sb("inv", [P, 2, QT])
        stats = sb("stats", [P, 2, QT, 6])
        mv = sb("mv", [P, 2, QT, 2])
        rstd = sb("rstd", [P, 2, QT])
        shift = sb("shift", [P, 2, QT])
        h_out = sb("h_out", [P, 2, QT, P])
        xn = sb("xn", [P, 2, QT, P])
        xt = sb("xt", [P, 2, W4])
        ps = [ctx.enter_context(nc.psum_tensor(f"tok_ps_xt{i}", [P, W4], F32)) for i in range(2)]

        ids_in = sem("ids_in")
        bias_in = sem("bias_in")
        ids_copied = sem("ids_copied")
        gathered = [ctx.enter_context(nc.semaphore(f"tok_gathered{i}")) for i in range(2)]
        feat_used = sem("feat_used")
        squared = sem("squared")
        summed = sem("summed")
        unit_done = sem("unit_done")
        stats_done = sem("stats_done")
        mv_done = sem("mv_done")
        shift_done = sem("shift_done")
        ssq_done = sem("ssq_done")
        inv_done = sem("inv_done")
        var_done = sem("var_done")
        rstd_done = sem("rstd_done")
        h_out_done = sem("h_out_done")
        h_stored = [sem("h_stored0"), sem("h_stored1")]
        xn_done = sem("xn_done")
        xt_ready = sem("xt_ready")
        xt_copied = sem("xt_copied")
        xt_stored = [sem("xt_stored0"), sem("xt_stored1")]

        block = ctx.enter_context(nc.Block())

        @block.sync
        def _(sp):
            for s in sems + [cst["pool_step"], cst["consts_done"]]:
                sp.sem_inc(s, ONE)
            sp.dma_start(ids[:, :], d["ids"].bitcast(U32)).then_inc(ids_in, 16)
            sp.dma_start(tok_b[:, :], d["tok_b"].partition_broadcast(P)).then_inc(bias_in, 16)
            sp.dma_start(out_b[:, :], d["bo"].partition_broadcast(P)).then_inc(bias_in, 16)
            with sp.Fori(0, G // 2) as gg:
                g = gg * 2
                for p in range(2):
                    sp.wait_ge(h_out_done, ONE + g + p + 1)
                    sp.dma_start(scr["h"][ds(g + p, 1), :, :].rearrange("a p n -> (a p) n"),
                                 h_out[:, p].rearrange("p q n -> p (q n)")).then_inc(h_stored[p], 16)
                    sp.wait_ge(xt_copied, ONE + g + p + 1)
                    sp.dma_start(scr["xt"][ds(g + p, 1), :, :].rearrange("a p n -> (a p) n"),
                                 xt[:, p]).then_inc(xt_stored[p], 16)
            for p in range(2):
                sp.wait_ge(h_stored[p], ONE + 16 * (G // 2))
                sp.wait_ge(xt_stored[p], ONE + 16 * (G // 2))

        @block.gpsimd
        def _(pool):
            nc.gpsimd.memset(cst["ident"][:, :], 0.0).then_inc(cst["pool_step"], 1)
            pool.wait_ge(cst["pool_step"], ONE + 1)
            nc.gpsimd.affine_select(out=cst["ident"][:, :], in_=cst["ident"][:, :], compare_op=ALU.not_equal,
                                    fill=1.0, base=0, pattern=[[-1, P]],
                                    channel_multiplier=1).then_inc(cst["consts_done"], 1)
            nc.gpsimd.memset(cst["neg_half"][:, :], -0.5).then_inc(cst["consts_done"], 1)
            nc.gpsimd.memset(cst["ones_row"][:, :], 1.0).then_inc(cst["consts_done"], 1)
            def gather(n, p):
                if not isinstance(n, int):
                    pool.wait_ge(feat_used, ONE + n - 1)
                t = slice(n * QT, (n + 1) * QT) if isinstance(n, int) else ds(n * QT, QT)
                nc.gpsimd.tensor_copy(ids_now[:, p, :], ids[:, t]).then_inc(ids_copied, 1)
                wait_apart(pool, cst, ids_copied, n + 1)
                for q in range(QT):
                    nc.gpsimd.indirect_dma_start(
                        out=feat[:, p, q, :], out_offset=None, in_=d["wt"],
                        in_offset=bass.IndirectOffsetOnAxis(ap=ids_now[:, p, q:q + 1], axis=0),
                    ).then_inc(gathered[p], 16)

            def inverse_norm(n, p):
                pool.wait_ge(ssq_done, ONE + n + 1)
                nc.gpsimd.tensor_tensor(inv[:, p], ssq[:, p], cst["neg_half"][:, 0:QT], ALU.pow).then_inc(inv_done, 1)

            def inverse_deviation(n, p):
                pool.wait_ge(var_done, ONE + n + 1)
                nc.gpsimd.tensor_tensor(rstd[:, p], rstd[:, p], cst["neg_half"][:, 0:QT], ALU.pow).then_inc(rstd_done, 1)

            pool.wait_ge(ids_in, ONE + 16)
            pool.wait_ge(cst["consts_done"], ONE + 3)
            for p in range(2):
                gather(p, p)
            inverse_norm(0, 0)
            with pool.Fori(1, G // 2) as gg:
                for p in range(2):
                    n = gg * 2 + p
                    gather(n, p)
                    inverse_deviation(n - 2, p)
                    inverse_norm(n - 1, 1 - p)
            inverse_deviation(G - 2, 0)
            inverse_norm(G - 1, 1)
            inverse_deviation(G - 1, 1)

        @block.vector
        def _(v):
            def square_sums(n, p):
                v.wait_ge(gathered[p], (n - p) * (8 * QT) + 16 * QT)
                if not isinstance(n, int):
                    v.wait_ge(xn_done, ONE + n - 1)
                    v.wait_ge(inv_done, ONE + n - 1)
                nc.vector.tensor_tensor(h_now[:, p], feat[:, p], bias4, ALU.add).then_inc(feat_used, 1)
                v.wait_ge(feat_used, ONE + n + 1)
                nc.vector.tensor_tensor(square[:, p], h_now[:, p], h_now[:, p], ALU.mult).then_inc(squared, 1)
                v.wait_ge(squared, ONE + n + 1)
                nc.vector.tensor_reduce(ssq[:, p], square[:, p], X, ALU.add).then_inc(summed, 1)
                v.wait_ge(summed, ONE + n + 1)
                nc.vector.tensor_scalar(ssq[:, p], ssq[:, p], 1e-24, None, ALU.max).then_inc(ssq_done, 1)

            def normalise(n, p):
                v.wait_ge(inv_done, ONE + n + 1)
                nc.vector.tensor_tensor(h_now[:, p], h_now[:, p], inv[:, p].unsqueeze(2).broadcast_to([P, QT, P]),
                                        ALU.mult).then_inc(unit_done, 1)
                wait_apart(v, cst, unit_done, n + 1)
                for q in range(QT):
                    last = nc.vector.bn_stats(stats[:, p, q, :], h_now[:, p, q, :])
                last.then_inc(stats_done, 1)
                wait_apart(v, cst, stats_done, n + 1)
                for q in range(QT):
                    last = nc.vector.bn_aggr(mv[:, p, q, :], stats[:, p, q, :])
                last.then_inc(mv_done, 1)
                v.wait_ge(mv_done, ONE + n + 1)
                nc.vector.tensor_scalar(rstd[:, p], mv[:, p, :, 1], EPS, None, ALU.add).then_inc(var_done, 1)
                v.wait_ge(h_stored[p], ONE + (n - p) * 8)
                nc.vector.tensor_tensor(h_out[:, p], h_now[:, p], out4, ALU.add).then_inc(h_out_done, 1)

            def scales(n, p):
                v.wait_ge(rstd_done, ONE + n + 1)
                nc.vector.scalar_tensor_tensor(out=shift[:, p], in0=mv[:, p, :, 0], scalar=-1.0, in1=rstd[:, p],
                                               op0=ALU.mult, op1=ALU.mult).then_inc(shift_done, 1)

            v.wait_ge(bias_in, ONE + 32)
            bias4 = tok_b[:, :].unsqueeze(1).broadcast_to([P, QT, P])
            out4 = out_b[:, :].unsqueeze(1).broadcast_to([P, QT, P])
            square_sums(0, 0)
            normalise(0, 0)
            square_sums(1, 1)
            with v.Fori(1, G // 2) as gg:
                for p in range(2):
                    n = gg * 2 + p
                    scales(n - 2, p)
                    normalise(n - 1, 1 - p)
                    square_sums(n, p)
            scales(G - 2, 0)
            normalise(G - 1, 1)
            scales(G - 1, 1)

        @block.tensor
        def _(pe):
            pe.wait_ge(cst["consts_done"], ONE + 3)
            with pe.Fori(0, G // 2) as gg:
                g = gg * 2
                for p in range(2):
                    pe.wait_ge(xn_done, ONE + g + p + 1)
                    pe.wait_ge(xt_copied, ONE + g)
                    for q in range(QT):
                        last = nc.tensor.transpose(ps[p][:, q * P:(q + 1) * P], xn[:, p, q, :], cst["ident"][:, :])
                    last.then_inc(xt_ready, 1)

        @block.scalar
        def _(act):
            with act.Fori(0, G // 2) as gg:
                g = gg * 2
                for p in range(2):
                    act.wait_ge(shift_done, ONE + g + p + 1)
                    act.wait_ge(xt_ready, ONE + g)
                    for q in range(QT):
                        last = nc.scalar.activation(xn[:, p, q, :], h_now[:, p, q, :], ACT.Identity,
                                                    bias=shift[:, p, q:q + 1], scale=rstd[:, p, q:q + 1])
                    last.then_inc(xn_done, 1)
                    act.wait_ge(xt_ready, ONE + g + p + 1)
                    act.wait_ge(xt_stored[p], ONE + g * 8)
                    nc.scalar.copy(xt[:, p], ps[p][:, :]).then_inc(xt_copied, 1)


def attention0_phase(nc, d, cst, scr):
    H, DK, NR = 8, 64, 2 * P - 1
    NP = H // 2
    IB = 8
    NIB = P // IB
    RB = 8
    LATE = NIB - 2
    QC = 4
    NC = G // QC
    SCALE = float(DK) ** -0.5
    with ExitStack() as ctx:
        def sb(name, shape, dt=F32):
            return ctx.enter_context(nc.sbuf_tensor(f"att_{name}", shape, dt))

        sems = []

        def sem(name):
            sems.append(ctx.enter_context(nc.semaphore(f"att_{name}")))
            return sems[-1]

        def bank(name):
            return ctx.enter_context(nc.psum_tensor(f"att_{name}", [P, W4], F32))

        xg = sb("xg", [P, W4])
        wqkv = sb("wqkv", [P, 3, P])
        bqkv = sb("bqkv", [P, 3])
        rel_k = sb("rel_k", [P, H, P])
        q_t = sb("q_t", [P, W4])
        k_t = sb("k_t", [P, W4])
        v_s = sb("v_s", [P, QT, P])
        s_s = sb("s_s", [P, 2, QT, P])
        top = sb("top", [P, 2, QT])
        ntop = sb("ntop", [P, 2, QT])
        z = sb("z", [P, 2, QT])
        rz = sb("rz", [P, 2, QT])
        p_s = sb("p_s", [P, 2, QT, P])
        p_now = sb("p_now", [P, 2, QT, P])
        p_t = sb("p_t", [P, 2, SEQ, P])
        rel_v = sb("rel_v", [P, RB, 2, IB, DK])
        o_t = sb("o_t", [P, SEQ, P])
        ps_q, ps_k, ps_v, ps_o = (bank(f"ps_{n}") for n in "qkvo")
        ps_s = [bank("ps_s0"), bank("ps_s1")]
        ps_t = [bank("ps_t0"), bank("ps_t1")]

        x_in = sem("x_in")
        w_in = sem("w_in")
        rk_in = sem("rk_in")
        rv_in = [sem(f"rv_in{i}") for i in range(RB)]
        q_ready = sem("q_ready")
        k_ready = sem("k_ready")
        v_ready = sem("v_ready")
        q_copied = sem("q_copied")
        k_copied = sem("k_copied")
        v_copied = sem("v_copied")
        s_ready = sem("s_ready")
        s_added = sem("s_added")
        top_done = sem("top_done")
        ntop_done = sem("ntop_done")
        exp_done = sem("exp_done")
        rz_done = sem("rz_done")
        p_done = sem("p_done")
        t_ready = sem("t_ready")
        t_copied = sem("t_copied")
        t_kept = sem("t_kept")
        o_ready = sem("o_ready")
        o_copied = sem("o_copied")
        r_ready = sem("r_ready")
        r_added = sem("r_added")
        first_stored = sem("first_stored")
        rest_stored = sem("rest_stored")

        block = ctx.enter_context(nc.Block())
        U = G

        @block.sync
        def _(sp):
            for s in sems:
                sp.sem_inc(s, ONE)
            def rel_block(hp, ib):
                for h in range(2):
                    src = d["pv"][ds(hp * 2 + h, 1), ib * IB:(ib + 1) * IB, :]
                    win = bass.AP(tensor=src.tensor, offset=src.offset, ap=[[DK, P], [1, IB * DK]])
                    sp.dma_start(rel_v[:, ib % RB, h].rearrange("p i d -> p (i d)"), win).then_inc(rv_in[ib % RB], 16)

            def weights(hp):
                sp.dma_start(wqkv[:, :, :], d["wqkv"][ds(hp, 1)].rearrange("a p t n -> (a p) t n")).then_inc(w_in, 16)
                sp.dma_start(bqkv[:, :], d["bqkv"][ds(hp, 1)].rearrange("a p t -> (a p) t")).then_inc(w_in, 16)

            def group(g):
                src = scr["xt"][g:g + 1] if isinstance(g, int) else scr["xt"][ds(g, 1)]
                sp.dma_start(xg[:, :], src.rearrange("a p n -> (a p) n")).then_inc(x_in, 16)

            def one_pair(hp, more):
                for ib in range(RB):
                    sp.wait_ge(v_ready, ONE + hp * U + NC + 1 + ib)
                    group(NC + 1 + ib)
                    sp.wait_ge(r_ready, ONE + hp * NIB)
                    rel_block(hp, ib)
                with sp.Fori(RB + NC + 1, U) as g:
                    sp.wait_ge(v_ready, ONE + hp * U + g)
                    group(g)
                if more:
                    sp.wait_ge(v_ready, ONE + (hp + 1) * U)
                    sp.wait_ge(o_copied, ONE + (hp + 1) * U)
                    weights(hp + 1)
                    group(0)
                for ib in range(RB, NIB):
                    sp.wait_ge(r_ready, ONE + hp * NIB + ib - RB + 1)
                    rel_block(hp, ib)
                if more:
                    sp.wait_ge(v_ready, ONE + (hp + 1) * U + 1)
                    group(1)
                sp.wait_ge(r_added, ONE + (hp + 1) * NIB)
                dst = scr["o"][ds(hp, 1)].rearrange("a p n -> (a p) n")
                src = o_t[:, :, :].rearrange("p b i -> p (b i)")
                sp.dma_start(dst[:, 0:QC * W4], src[:, 0:QC * W4]).then_inc(first_stored, 16)
                for c in range(1, NC):
                    if more:
                        sp.wait_ge(v_ready, ONE + (hp + 1) * U + c + 1)
                        group(c + 1)
                    sp.dma_start(dst[:, c * QC * W4:(c + 1) * QC * W4],
                                 src[:, c * QC * W4:(c + 1) * QC * W4]).then_inc(rest_stored, 16)

            weights(0)
            group(0)
            sp.dma_start(rel_k[:, :, :], bass.AP(tensor=d["pk"].tensor, offset=P - 1,
                                                 ap=[[NR - 1, P], [P * NR, H], [1, P]])).then_inc(rk_in, 16)
            for g in range(1, NC + 1):
                sp.wait_ge(v_ready, ONE + g)
                group(g)
            with sp.Fori(0, NP - 1) as hp:
                one_pair(hp, True)
            one_pair(NP - 1, False)
            sp.wait_ge(first_stored, ONE + 16 * NP)
            sp.wait_ge(rest_stored, ONE + 16 * NP * (NC - 1))

        @block.tensor
        def _(pe):
            def project(hp, u):
                pe.wait_ge(w_in, ONE + hp * 32 + 32)
                pe.wait_ge(x_in, ONE + u * 16 + 16)
                pe.wait_ge(q_copied, ONE + u)
                nc.tensor.matmul(ps_q[:, :], wqkv[:, 0, :], xg[:, :], start=True, stop=True).then_inc(q_ready, 1)
                pe.wait_ge(k_copied, ONE + u)
                nc.tensor.matmul(ps_k[:, :], wqkv[:, 1, :], xg[:, :], start=True, stop=True).then_inc(k_ready, 1)
                pe.wait_ge(v_copied, ONE + u)
                for t in range(QT):
                    last = nc.tensor.matmul(ps_v[:, t * P:(t + 1) * P], xg[:, t * P:(t + 1) * P], wqkv[:, 2, :],
                                            start=True, stop=True)
                last.then_inc(v_ready, 1)

            def scores(u):
                pe.wait_ge(q_copied, ONE + u + 1)
                pe.wait_ge(k_copied, ONE + u + 1)
                for h in range(2):
                    pe.wait_ge(s_added, ONE + u * 2)
                    for t in range(QT):
                        r = slice(h * DK, (h + 1) * DK)
                        c = slice(t * P, (t + 1) * P)
                        last = nc.tensor.matmul(ps_s[h][:, c], q_t[r, c], k_t[r, c], start=True, stop=True)
                        if t == QT - 1:
                            last.then_inc(s_ready, 1)

            def transposes(hp, u, h):
                pe.wait_ge(r_added, ONE + hp * NIB)
                pe.wait_ge(p_done, ONE + u * 2 + h + 1)
                pe.wait_ge(t_copied, ONE + u * 2)
                for t in range(QT):
                    last = nc.tensor.transpose(ps_t[h][:, t * P:(t + 1) * P], p_s[:, h, t, :], cst["ident"][:, :])
                last.then_inc(t_ready, 1)

            def values(u):
                pe.wait_ge(v_copied, ONE + u + 1)
                pe.wait_ge(o_copied, ONE + u)
                for h in range(2):
                    pe.wait_ge(t_copied, ONE + u * 2 + h + 1)
                    r = slice(h * DK, (h + 1) * DK)
                    for t in range(QT):
                        last = nc.tensor.matmul(ps_o[r, t * P:(t + 1) * P], v_s[:, t, r],
                                                p_now[:, h, t, :], start=True, stop=True)
                last.then_inc(o_ready, 1)

            def one_pair(hp, more):
                with pe.Fori(0, U - 1) as g:
                    u = hp * U + g
                    project(hp, u + 1)
                    transposes(hp, u, 0)
                    scores(u + 1)
                    transposes(hp, u, 1)
                    values(u)
                for h in range(2):
                    transposes(hp, hp * U + (U - 1), h)
                values(hp * U + (U - 1))
                pe.wait_ge(t_kept, ONE + hp * (2 * U) + 2 * U)
                for ib in range(NIB):
                    if more and ib == LATE:
                        project(hp + 1, (hp + 1) * U)
                        scores((hp + 1) * U)
                    b = ib % RB
                    pe.wait_ge(rv_in[b], ONE + hp * (32 * (NIB // RB)) + (ib // RB) * 32 + 32)
                    pe.wait_ge(r_added, ONE + hp * NIB + max(ib - 1, 0))
                    for i in range(IB):
                        for h in range(2):
                            last = nc.tensor.matmul(
                                ps_t[ib % 2][h * DK:(h + 1) * DK, (IB - 1 - i) * SEQ:(IB - i) * SEQ],
                                rel_v[:, b, h, i, :], p_t[:, h, :, P - 1 - (ib * IB + i)], start=True, stop=True)
                    last.then_inc(r_ready, 1)

            project(0, 0)
            scores(0)
            with pe.Fori(0, NP - 1) as hp:
                one_pair(hp, True)
            one_pair(NP - 1, False)

        @block.scalar
        def _(act):
            def project(hp, u):
                act.wait_ge(w_in, ONE + hp * 32 + 32)
                act.wait_ge(q_ready, ONE + u + 1)
                act.wait_ge(s_ready, ONE + u * 2)
                nc.scalar.activation(q_t[:, :], ps_q[:, :], ACT.Identity, bias=bqkv[:, 0:1]).then_inc(q_copied, 1)

            def exps(u):
                act.wait_ge(t_ready, ONE + u * 2)
                act.wait_ge(rz_done, ONE + u * 2)
                for h in range(2):
                    act.wait_ge(ntop_done, ONE + u * 2 + h + 1)
                    for t in range(QT):
                        last = nc.scalar.activation(p_s[:, h, t, :], s_s[:, h, t, :], ACT.Exp,
                                                    bias=ntop[:, h, t:t + 1], scale=SCALE,
                                                    accum_out=z[:, h, t:t + 1])
                    last.then_inc(exp_done, 1)

            def copies(u):
                act.wait_ge(o_ready, ONE + u)
                act.wait_ge(t_kept, ONE + u * 2)
                for h in range(2):
                    act.wait_ge(t_ready, ONE + u * 2 + h + 1)
                    nc.scalar.copy(p_now[:, h].rearrange("p t n -> p (t n)"), ps_t[h][:, :]).then_inc(t_copied, 1)

            def out(hp, u, g, stored):
                act.wait_ge(stored, ONE + hp * (16 if stored is first_stored else 16 * (NC - 1)))
                act.wait_ge(o_ready, ONE + u + 1)
                nc.scalar.activation(o_t[:, ds(g * QT, QT), :].rearrange("p t n -> p (t n)"), ps_o[:, :],
                                     ACT.Identity, bias=bqkv[:, 2:3]).then_inc(o_copied, 1)

            def one_pair(hp, more):
                project(hp, hp * U + 1)
                copies(hp * U)
                exps(hp * U + 1)
                for lo, hi, stored in ((0, QC, first_stored), (QC, U - 2, rest_stored)):
                    with act.Fori(lo, hi) as g:
                        u = hp * U + g
                        project(hp, u + 2)
                        out(hp, u, g, stored)
                        copies(u + 1)
                        exps(u + 2)
                out(hp, hp * U + (U - 2), U - 2, rest_stored)
                copies(hp * U + (U - 1))
                out(hp, hp * U + (U - 1), U - 1, rest_stored)
                if more:
                    project(hp + 1, (hp + 1) * U)
                    exps((hp + 1) * U)

            project(0, 0)
            exps(0)
            with act.Fori(0, NP - 1) as hp:
                one_pair(hp, True)
            one_pair(NP - 1, False)

        @block.gpsimd
        def _(pool):
            with pool.Fori(0, NP) as hp:
                wait_apart(pool, cst, r_ready, hp * NIB)
                with pool.Fori(0, U) as g:
                    for h in range(2):
                        pool.wait_ge(t_copied, ONE + hp * (2 * U) + g * 2 + h + 1)
                        nc.gpsimd.tensor_copy(p_t[:, h, ds(g * QT, QT), :], p_now[:, h]).then_inc(t_kept, 1)

        @block.vector
        def _(v):
            def key_copy(hp, u):
                v.wait_ge(w_in, ONE + hp * 32 + 32)
                v.wait_ge(k_ready, ONE + u + 1)
                v.wait_ge(s_ready, ONE + u * 2)
                nc.vector.tensor_scalar(k_t[:, :], ps_k[:, :], bqkv[:, 1:2], None, ALU.add).then_inc(k_copied, 1)

            def value_copy(u):
                v.wait_ge(v_ready, ONE + u + 1)
                v.wait_ge(o_ready, ONE + u)
                nc.vector.tensor_copy(v_s[:, :, :].rearrange("p t n -> p (t n)"), ps_v[:, :]).then_inc(v_copied, 1)

            def bias_and_top(hp, u):
                for h in range(2):
                    v.wait_ge(exp_done, ONE + u * 2)
                    v.wait_ge(s_ready, ONE + u * 2 + h + 1)
                    nc.vector.tensor_tensor(s_s[:, h], ps_s[h][:, :].rearrange("p (t n) -> p t n", t=QT),
                                            rel_k[:, ds(hp * 2 + h, 1), :].broadcast_to([P, QT, P]),
                                            ALU.add).then_inc(s_added, 1)
                    v.wait_ge(s_added, ONE + u * 2 + h + 1)
                    nc.vector.tensor_reduce(top[:, h], s_s[:, h], X, ALU.max).then_inc(top_done, 1)
                    v.wait_ge(top_done, ONE + u * 2 + h + 1)
                    nc.vector.tensor_scalar(ntop[:, h], top[:, h], -SCALE, None, ALU.mult).then_inc(ntop_done, 1)

            def divide(u, h):
                v.wait_ge(exp_done, ONE + u * 2 + h + 1)
                nc.vector.reciprocal(rz[:, h], z[:, h]).then_inc(rz_done, 1)
                v.wait_ge(rz_done, ONE + u * 2 + h + 1)
                nc.vector.tensor_tensor(p_s[:, h], p_s[:, h],
                                        rz[:, h].unsqueeze(2).broadcast_to([P, QT, P]),
                                        ALU.mult).then_inc(p_done, 1)

            def add_relative(hp, ib):
                wait_apart(v, cst, r_ready, hp * NIB + ib + 1)
                lo = P - IB - ib * IB
                o_view = o_t[:, :, lo:lo + IB].rearrange("p b i -> p i b")
                nc.vector.tensor_tensor(o_view, ps_t[ib % 2][:, :].rearrange("p (i b) -> p i b", i=IB),
                                        o_view, ALU.add).then_inc(r_added, 1)

            def unit(hp, u, more):
                bias_and_top(hp, u)
                value_copy(u)
                divide(u, 0)
                if more:
                    key_copy(hp, u + 1)
                divide(u, 1)

            def one_pair(hp, more):
                key_copy(hp, hp * U + 1)
                with v.Fori(1, U - 1) as g:
                    unit(hp, hp * U + g, True)
                unit(hp, hp * U + (U - 1), False)
                v.wait_ge(o_copied, ONE + (hp + 1) * U)
                for ib in range(NIB):
                    if more and ib == LATE:
                        key_copy(hp + 1, (hp + 1) * U)
                        bias_and_top(hp + 1, (hp + 1) * U)
                        value_copy((hp + 1) * U)
                    add_relative(hp, ib)
                if more:
                    for h in range(2):
                        divide((hp + 1) * U, h)

            key_copy(0, 0)
            v.wait_ge(rk_in, ONE + 16)
            unit(0, 0, False)
            with v.Fori(0, NP - 1) as hp:
                one_pair(hp, True)
            one_pair(NP - 1, False)


def mix_phase(nc, d, cst, scr, keep):
    E, TOP = 16, 4
    with ExitStack() as ctx:
        def sb(name, shape, dt=F32):
            return ctx.enter_context(nc.sbuf_tensor(f"mix_{name}", shape, dt))

        sems = []

        def sem(name):
            sems.append(ctx.enter_context(nc.semaphore(f"mix_{name}")))
            return sems[-1]

        wo = sb("wo", [P, 4, P])
        gate = sb("gate", [P, E])
        b2 = sb("b2", [E + 2, P])
        og = sb("og", [P, 2, 4, W4])
        hg = sb("hg", [P, 2, QT, P])
        stats = sb("stats", [P, QT, 6])
        mv = sb("mv", [P, 2, QT, 2])
        rstd = sb("rstd", [P, 2, QT])
        shift = sb("shift", [P, 2, QT])
        xn = sb("xn", [P, 2, QT, P])
        xt = sb("xt", [P, 2, W4])
        logit = sb("logit", [P, SEQ, E])
        prob = sb("prob", [P, SEQ, E])
        above = sb("above", [P, SEQ, E])
        equal = sb("equal", [P, SEQ, E])
        upto = sb("upto", [P, SEQ, E])
        restart = sb("restart", [P, SEQ, E])
        best = sb("best", [P, SEQ, 8])
        row = sb("row", [P, SEQ])
        row2 = sb("row2", [P, SEQ])
        comb_now = sb("comb_now", [P, 2, QT, E + 2])
        comb_t = sb("comb_t", [E + 2, 2, QT, P])
        ps_y = [ctx.enter_context(nc.psum_tensor(f"mix_ps_y{i}", [P, W4], F32)) for i in range(2)]
        ps_t = [ctx.enter_context(nc.psum_tensor(f"mix_ps_t{i}", [P, W4], F32)) for i in range(2)]
        ps_l = [ctx.enter_context(nc.psum_tensor(f"mix_ps_l{i}", [P, W4], F32)) for i in range(2)]

        w_in = sem("w_in")
        gate_in = sem("gate_in")
        g_in = [sem("g_in0"), sem("g_in1")]
        y_ready = sem("y_ready")
        y_added = sem("y_added")
        stats_done = sem("stats_done")
        var_done = sem("var_done")
        rstd_done = sem("rstd_done")
        shift_done = sem("shift_done")
        xn_done = sem("xn_done")
        t_ready = sem("t_ready")
        t_copied = sem("t_copied")
        t_stored = [sem("t_stored0"), sem("t_stored1")]
        l_ready = sem("l_ready")
        l_copied = sem("l_copied")
        step = sem("router_step")
        less_top = sem("less_top")
        exp_done = sem("exp_done")
        restart_done = sem("restart_done")
        comb_done = sem("comb_done")
        c_ready = sem("c_ready")
        c_copied = sem("c_copied")
        b_ready = sem("b_ready")
        b_added = sem("b_added")

        block = ctx.enter_context(nc.Block())
        HG = G // 2
        WL = HG - 2
        W_SLOTS = (E + 2) // WL
        keep["w_loads"] = WL * W_SLOTS + 2

        def before(n):
            return max(n - 1, 0) if isinstance(n, int) else n - 1

        @block.sync
        def _(sp):
            for s in sems + [keep["h1_kept"], keep["comb_kept"]]:
                sp.sem_inc(s, ONE)
            sp.dma_start(wo[:, :, :], d["wo"]).then_inc(w_in, 16)
            def load(gg, p):
                n = gg * 2 + p
                first = isinstance(gg, int)
                if not first:
                    sp.wait_ge(y_ready, ONE + n - 1)
                sp.dma_start(og[:, p], (scr["o"][:, :, n * W4:(n + 1) * W4] if first else
                                        scr["o"][:, :, ds(n * W4, W4)]).rearrange("a p n -> p a n")).then_inc(g_in[p], 16)
                if not first:
                    sp.wait_ge(xn_done, ONE + n - 1)
                    sp.wait_ge(keep["h1_kept"], ONE + n - 1)
                sp.dma_start(hg[:, p].rearrange("p q n -> p (q n)"), (scr["h"][n:n + 1] if first else scr["h"][ds(n, 1)])
                             .rearrange("a p n -> (a p) n")).then_inc(g_in[p], 16)

            load(0, 0)
            sp.dma_start(gate[:, :], d["gate"]).then_inc(gate_in, 16)
            sp.dma_start(b2[:, :], d["b2"]).then_inc(gate_in, 16)
            load(0, 1)
            with sp.Fori(1, HG) as gg:
                for p in range(2):
                    load(gg, p)
            for p in range(2):
                sp.wait_ge(t_stored[p], ONE + 16 * HG)

        @block.tensor
        def _(pe):
            def project(n, p):
                if not isinstance(n, int) or n >= 2:
                    pe.wait_ge(y_added, ONE + n - 1)
                pe.wait_ge(g_in[p], ONE + (n - p) * 16 + 32)
                for t in range(QT):
                    for a in range(4):
                        last = nc.tensor.matmul(ps_y[p][:, t * P:(t + 1) * P], og[:, p, a, t * P:(t + 1) * P],
                                                wo[:, a, :], start=(a == 0), stop=(a == 3))
                last.then_inc(y_ready, 1)

            def transposes(n, p):
                pe.wait_ge(t_copied, ONE + before(n))
                pe.wait_ge(xn_done, ONE + n + 1)
                for t in range(QT):
                    last = nc.tensor.transpose(ps_t[p][:, t * P:(t + 1) * P], xn[:, p, t, :], cst["ident"][:, :])
                last.then_inc(t_ready, 1)

            def logits(n, p):
                pe.wait_ge(l_copied, ONE + before(n))
                pe.wait_ge(t_copied, ONE + n + 1)
                for t in range(QT):
                    last = nc.tensor.matmul(ps_l[p][:, t * E:(t + 1) * E], xt[:, p, t * P:(t + 1) * P],
                                            gate[:, :], start=True, stop=True)
                last.then_inc(l_ready, 1)

            def turn_weights(n, p):
                pe.wait_ge(c_copied, ONE + before(n))
                pe.wait_ge(comb_done, ONE + n + 1)
                for t in range(QT):
                    last = nc.tensor.transpose(ps_t[p][0:E + 2, t * P:(t + 1) * P], comb_now[:, p, t, :],
                                               cst["ident"][:, :])
                last.then_inc(c_ready, 1)

            def bias_terms(n, p):
                pe.wait_ge(b_added, ONE + before(n))
                pe.wait_ge(c_copied, ONE + n + 1)
                for t in range(QT):
                    last = nc.tensor.matmul(ps_y[p][:, t * P:(t + 1) * P], comb_t[:, p, t, :], b2[:, :],
                                            start=True, stop=True)
                last.then_inc(b_ready, 1)

            pe.wait_ge(w_in, ONE + 16)
            project(0, 0)
            project(1, 1)
            transposes(0, 0)
            pe.wait_ge(gate_in, ONE + 32)
            with pe.Fori(1, HG) as gg:
                for n, p in ((gg * 2 - 1, 1), (gg * 2, 0)):
                    project(n + 1, 1 - p)
                    logits(n - 1, 1 - p)
                    transposes(n, p)
            logits(G - 2, 0)
            transposes(G - 1, 1)
            logits(G - 1, 1)
            turn_weights(0, 0)
            with pe.Fori(1, HG) as gg:
                for n, p in ((gg * 2 - 1, 1), (gg * 2, 0)):
                    turn_weights(n, p)
                    bias_terms(n - 1, 1 - p)
            turn_weights(G - 1, 1)
            bias_terms(G - 2, 0)
            bias_terms(G - 1, 1)

        @block.scalar
        def _(act):
            with act.Fori(0, HG) as gg:
                for p in range(2):
                    n = gg * 2 + p
                    act.wait_ge(shift_done, ONE + n + 1)
                    act.wait_ge(t_ready, ONE + gg * 2)
                    for t in range(QT):
                        last = nc.scalar.activation(xn[:, p, t, :], hg[:, p, t, :], ACT.Identity,
                                                    bias=shift[:, p, t:t + 1], scale=rstd[:, p, t:t + 1])
                    last.then_inc(xn_done, 1)
                    act.wait_ge(t_stored[p], ONE + gg * 16)
                    act.wait_ge(l_ready, ONE + gg * 2)
                    act.wait_ge(t_ready, ONE + n + 1)
                    nc.scalar.copy(xt[:, p], ps_t[p][:, :]).then_inc(t_copied, 1)
                    act.wait_ge(t_copied, ONE + n + 1)
                    act.dma_start(scr["xm"][ds(gg * 2 + p, 1)].rearrange("a p n -> (a p) n"),
                                  xt[:, p]).then_inc(t_stored[p], 16)
            flat = lambda x: x[:, :, :].rearrange("p t e -> p (t e)")
            for n in range(2):
                act.wait_ge(less_top, ONE + n + 1)
                nc.scalar.activation(flat(upto), flat(upto), ACT.Exp).then_inc(exp_done, 1)
            with act.Fori(0, HG) as gg:
                for p in range(2):
                    act.wait_ge(b_ready, ONE + gg * 2)
                    act.wait_ge(c_ready, ONE + gg * 2 + p + 1)
                    nc.scalar.copy(comb_t[:, p].rearrange("p t n -> p (t n)"),
                                   ps_t[p][0:E + 2, :]).then_inc(c_copied, 1)

        @block.gpsimd
        def _(pool):
            nc.gpsimd.memset(restart[:, :, :], 1.0).then_inc(restart_done, 1)
            pool.wait_ge(restart_done, ONE + 1)
            nc.gpsimd.memset(restart[:, :, 0:1], 0.0).then_inc(restart_done, 1)
            nc.gpsimd.memset(comb_now[:, :, :, :], 0.5).then_inc(restart_done, 1)
            def inverse_root(n, p):
                pool.wait_ge(var_done, ONE + n + 1)
                nc.gpsimd.tensor_tensor(rstd[:, p], rstd[:, p], cst["neg_half"][:, 0:QT], ALU.pow).then_inc(rstd_done, 1)

            inverse_root(0, 0)
            inverse_root(1, 1)
            with pool.Fori(0, WL) as i:
                for p in range(2):
                    inverse_root(i * 2 + 2 + p, p)
                for q in range(W_SLOTS):
                    pool.dma_start(keep["w1"][:, ds(i * W_SLOTS + q, 1), :].rearrange("p s n -> p (s n)"),
                                   d["w1"][:, ds(i * W_SLOTS + q, 1), :].rearrange("p s n -> p (s n)")
                                   ).then_inc(keep["w_in"], 16)
            inverse_root(G - 2, 0)
            inverse_root(G - 1, 1)
            for name in ("w2", "b1"):
                pool.dma_start(keep[name][:], d[name]).then_inc(keep["w_in"], 16)

        @block.vector
        def _(v):
            def residual(n, p):
                v.wait_ge(y_ready, ONE + n + 1)
                nc.vector.tensor_tensor(hg[:, p].rearrange("p q n -> p (q n)"), ps_y[p][:, :],
                                        hg[:, p].rearrange("p q n -> p (q n)"), ALU.add).then_inc(y_added, 1)
                v.wait_ge(y_added, ONE + n + 1)
                for t in range(QT):
                    last = nc.vector.bn_stats(stats[:, t, :], hg[:, p, t, :])
                last.then_inc(stats_done, 1)
                wait_apart(v, cst, stats_done, n + 1)
                for t in range(QT):
                    last = nc.vector.bn_aggr(mv[:, p, t, :], stats[:, t, :])
                last.then_inc(step, 1)
                v.wait_ge(xn_done, ONE + before(n))
                v.wait_ge(step, ONE + n + 1)
                nc.vector.tensor_scalar(rstd[:, p], mv[:, p, :, 1], EPS, None, ALU.add).then_inc(var_done, 1)
                nc.vector.tensor_copy(keep["h1"][:, slice(n * QT, (n + 1) * QT) if isinstance(n, int) else ds(n * QT, QT), :],
                                      hg[:, p]).then_inc(keep["h1_kept"], 1)
                v.wait_ge(rstd_done, ONE + n + 1)
                nc.vector.scalar_tensor_tensor(out=shift[:, p], in0=mv[:, p, :, 0], scalar=-1.0, in1=rstd[:, p],
                                               op0=ALU.mult, op1=ALU.mult).then_inc(shift_done, 1)

            def keep_logits(n, p):
                v.wait_ge(l_ready, ONE + n + 1)
                t = slice(n * QT, (n + 1) * QT) if isinstance(n, int) else ds(n * QT, QT)
                nc.vector.tensor_copy(logit[:, t, :],
                                      ps_l[p][:, 0:QT * E].rearrange("p (t e) -> p t e", e=E)).then_inc(l_copied, 1)

            for p in range(2):
                residual(p, p)
            with v.Fori(1, HG) as gg:
                for p in range(2):
                    residual(gg * 2 + p, p)
                    keep_logits(gg * 2 + p - 2, p)
            for p in range(2):
                keep_logits(G - 2 + p, p)
            wide = [P, SEQ, E]
            at = [G]

            def done(ins):
                at[0] += 1
                ins.then_inc(step, 1)
                v.wait_ge(step, ONE + at[0])

            def rows(x):
                return x.unsqueeze(2).broadcast_to(wide)

            v.wait_ge(l_copied, ONE + G)
            done(nc.vector.tensor_reduce(row[:, :], logit[:, :, :], X, ALU.max))
            nc.vector.tensor_tensor(upto[:, :, :], logit[:, :, :], rows(row[:, :]), ALU.subtract).then_inc(less_top, 1)
            v.wait_ge(exp_done, ONE + 1)
            done(nc.vector.tensor_reduce(row[:, :], upto[:, :, :], X, ALU.add))
            done(nc.vector.reciprocal(row2[:, :], row[:, :]))
            done(nc.vector.tensor_tensor(prob[:, :, :], upto[:, :, :], rows(row2[:, :]), ALU.mult))
            for t in range(SEQ):
                last = nc.vector.max(best[:, t, :], prob[:, t, :])
            done(last)
            done(nc.vector.tensor_tensor(above[:, :, :], prob[:, :, :], rows(best[:, :, TOP - 1]), ALU.is_gt))
            done(nc.vector.tensor_tensor(equal[:, :, :], prob[:, :, :], rows(best[:, :, TOP - 1]), ALU.is_equal))
            done(nc.vector.tensor_reduce(row[:, :], above[:, :, :], X, ALU.add))
            done(nc.vector.tensor_scalar(row2[:, :], row[:, :], -1.0, float(TOP), ALU.mult, ALU.add))
            v.wait_ge(restart_done, ONE + 3)
            flat = lambda x: x[:, :, :].rearrange("p t e -> p (t e)")
            done(nc.vector.tensor_tensor_scan(flat(logit), flat(restart), flat(equal), 0.0, ALU.mult, ALU.add))
            done(nc.vector.tensor_tensor(logit[:, :, :], logit[:, :, :], rows(row2[:, :]), ALU.is_le))
            done(nc.vector.tensor_tensor(logit[:, :, :], logit[:, :, :], equal[:, :, :], ALU.mult))
            done(nc.vector.tensor_tensor(above[:, :, :], above[:, :, :], logit[:, :, :], ALU.add))
            nc.vector.tensor_tensor(upto[:, :, :], prob[:, :, :], rows(best[:, :, 0]), ALU.subtract).then_inc(less_top, 1)
            v.wait_ge(exp_done, ONE + 2)
            done(nc.vector.tensor_tensor(upto[:, :, :], upto[:, :, :], above[:, :, :], ALU.mult))
            done(nc.vector.tensor_reduce(row[:, :], upto[:, :, :], X, ALU.add))
            done(nc.vector.reciprocal(row2[:, :], row[:, :]))
            nc.vector.tensor_tensor(keep["comb"][:, :, :], upto[:, :, :], rows(row2[:, :]), ALU.mult).then_inc(keep["comb_kept"], 1)
            v.wait_ge(keep["comb_kept"], ONE + 1)
            def weights_now(n, p):
                v.wait_ge(c_ready, ONE + before(n))
                t = slice(n * QT, (n + 1) * QT) if isinstance(n, int) else ds(n * QT, QT)
                nc.vector.tensor_copy(comb_now[:, p, :, 0:E], keep["comb"][:, t, :]).then_inc(comb_done, 1)

            def add_biases(n, p):
                v.wait_ge(b_ready, ONE + n + 1)
                t = slice(n * QT, (n + 1) * QT) if isinstance(n, int) else ds(n * QT, QT)
                nc.vector.tensor_tensor(keep["h1"][:, t, :], ps_y[p][:, :].rearrange("p (t n) -> p t n", t=QT),
                                        keep["h1"][:, t, :], ALU.add).then_inc(b_added, 1)

            for p in range(2):
                weights_now(p, p)
            with v.Fori(1, HG) as gg:
                for p in range(2):
                    weights_now(gg * 2 + p, p)
                    add_biases(gg * 2 + p - 2, p)
            for p in range(2):
                add_biases(G - 2 + p, p)


def tower_phase(nc, d, cst, scr, keep, out):
    E, SH, F = 16, 2, 512
    S = E + SH
    FC = F // P
    H1, D1 = 8, 16
    N_IN, N_PR, D_PV, N_OUT = 512, 256, 64, 512
    K_IN, K_PR, K_OUT = 64, 128, 64
    R_IN, R_PR, R_OUT = K_IN // 8, K_PR // 8, K_OUT // 8
    SCALE = float(P) ** -0.5
    GONE, IS_GONE = -3e38, -1e38
    ND = QT * (R_IN + R_PR + R_OUT)
    with ExitStack() as ctx:
        def sb(name, shape, dt=F32):
            return ctx.enter_context(nc.sbuf_tensor(f"tow_{name}", shape, dt))

        sems = []

        def sem(name):
            sems.append(ctx.enter_context(nc.semaphore(f"tow_{name}")))
            return sems[-1]

        w1, w2, b1 = keep["w1"], keep["w2"], keep["b1"]
        h1, comb = keep["h1"], keep["comb"]
        xm = sb("xm", [P, W4])
        hid = sb("hid", [P, 2, FC, W4])
        wqkv = sb("wqkv1", [P, 3 * P])
        bqkv = sb("bqkv1", [P, 3 * P])
        wo = sb("wo1", [P, P])
        bo = sb("bo1", [1, P])
        gb = sb("gb", [P, 4])
        odd = sb("odd", [P, 2])
        gbk = sb("gbk", [P, 2, 2])
        stats = sb("stats", [P, 2 * QT, 6])
        mv = sb("mv", [P, 2 * QT, 2])
        pt = [sb(f"pool_tmp{i}", [P, 2 * QT]) for i in range(6)]
        sx = sb("sx", [P, QT, P])
        xt = sb("xt", [P, W4])
        qkv = sb("qkv", [P, QT, 3 * P])
        qk_n = sb("qk_n", [P, 2, QT, P])
        q_t = sb("q_t", [P, W4])
        k_t = sb("k_t", [P, 2, W4])
        top = sb("top", [P, 2, 4])
        ntop = sb("ntop", [P, 2, 4])
        z = sb("z", [P, QT, H1])
        rz = sb("rz", [P, QT, H1])
        p_s = sb("p_s", [P, 2, 4, P])
        p_t = sb("p_t", [P, 2, 4, P])
        w_in_t = sb("w_in_t", [P, N_IN])
        w_pr_t = sb("w_pr_t", [P, N_IN // P, N_PR])
        w_val = sb("w_val", [P, N_PR // P, D_PV])
        w_oi_t = sb("w_oi_t", [D_PV, N_OUT])
        w_out = sb("w_out", [P, N_OUT // P, P])
        acts = sb("acts", [P, QT, N_IN])
        oacts = sb("oacts", [P, QT, N_OUT])
        pacts = sb("pacts", [P, QT, N_PR])
        pexp = sb("pexp", [P, 2, N_PR])
        work = sb("work", [P, 2, N_IN])
        best = sb("best", [P, 2, 8])
        ptop = sb("ptop", [P, QT])
        chosen = sb("chosen", [P, 2, N_IN])
        ch_t = sb("ch_t", [P, N_IN])
        zp = sb("zp", [P, QT])
        rzp = sb("rzp", [P, QT])
        agg_t = sb("agg_t", [D_PV, 2, P])
        h_out = sb("h_out", [P, QT, P])
        bank = lambda name: ctx.enter_context(nc.psum_tensor(f"tow_{name}", [P, W4], F32))
        ps_h = [bank("ps_h0"), bank("ps_h1")]
        ps_y = [bank("ps_y0"), bank("ps_y1")]
        x0, x1, x2, x3 = [bank(f"ps_x{i}") for i in range(4)]

        def unit(u):
            r = u % 4
            return r, [(2 * (u // 4) + a, b, 2 * r + b) for a in range(2) for b in range(2)]

        names = """c_in c_half gbk_done xm_in h_ready hid_done y_ready y_added a_stats a_var a_pool a_scale a_silu a_t
            a_xt a_qkv a_bias a_stats2 a_var2 a_pool2 a_rstd2 a_norm a_qkt a_qkc a_s a_top a_ntop a_exp a_pt a_ptc a_pv
            a_rz a_on a_silu2 a_ot a_otc a_y h2_done f_stats f_var f_pool f_rstd f_norm f_t f_xt f_act f_acted found
            cleared chosen_done f_ct f_ctc f_pr f_practed f_exp f_rz f_agg f_aggc f_oact f_oacted f_out f_res
            out_done""".split()
        sm = {n: sem(n) for n in names}
        block = ctx.enter_context(nc.Block())

        R0 = {17: (0, 1), 18: (1, 2)}
        R1 = {0: (2, 5), 1: (5, 8), 2: (8, 10), 3: (10, 13), 4: (13, 16)}
        R2 = {5: (0, 5), 6: (5, 9), 7: (9, 14), 8: (14, 18), 9: (18, 23), 10: (23, 28), 11: (28, 32)}
        R3 = {11: (0, 1), 12: (1, 4), 13: (4, 7), 14: (7, 10), 15: (10, 12), 16: (12, 14), 17: (14, 16)}
        S2 = {3: (0, 1), 5: (2, 3)}
        SE = {7: (0, 1), 9: (2, 3)}
        S3 = {10: (0, 1), 12: (2, 3)}
        S4 = {16: (0, 1), 18: (2, 3)}
        IN, QKV, TURN, SC, OUT, FIN, S1 = 1, 2, 4, 5, 11, 13, 14

        @block.sync
        def _(sp):
            for s in sems:
                sp.sem_inc(s, ONE)
            def load(k):
                sp.wait_ge(sm["h_ready"], ONE + k * (S * FC))
                sp.dma_start(xm[:, :], scr["xm"][ds(k, 1)].rearrange("a p n -> (a p) n")).then_inc(sm["xm_in"], 16)

            def store(f):
                sp.wait_ge(sm["f_res"], ONE + f * QT + QT)
                sp.dma_start(out[ds(f * QT, QT), :, :].rearrange("t p n -> p t n"),
                             h_out[:, :, :]).then_inc(sm["out_done"], 16)

            load(0)
            for dst, src in ((wqkv[:, :], "wqkv1"), (wo[:, :], "wo1"), (bo[:, :], "bo1"), (gb[:, :], "gb"),
                             (odd[:, :], "odd"), (w_in_t[:, :], "ip"), (w_pr_t[:, :, :], "piw"),
                             (w_val[:, :, :], "pval"), (w_oi_t[:, :], "oiw"), (w_out[:, :, :], "op")):
                sp.dma_start(dst, d[src]).then_inc(sm["c_in"], 16)
            sp.dma_start(bqkv[:, :], d["bqkv1"].partition_broadcast(P)).then_inc(sm["c_in"], 16)
            for k in (1, 2):
                load(k)
            with sp.Fori(3, G) as k:
                load(k)
                store(k - 3)
            for f in range(G - 3, G):
                store(f)
            sp.wait_ge(sm["out_done"], ONE + 16 * G)

        @block.gpsimd
        def _(pool):
            nh = cst["neg_half"]
            with pool.Fori(0, G) as j:
                n = [0]

                def done(ins):
                    n[0] += 1
                    ins.then_inc(sm["a_pool"], 1)
                    wait_apart(pool, cst, sm["a_pool"], j * 8 + n[0])

                wait_apart(pool, cst, sm["a_var"], j + 1)
                m, var = mv[:, 0:QT, 0], mv[:, 0:QT, 1]
                r1, sq, r2, sc, sh = (t[:, 0:QT] for t in pt[0:5])
                done(nc.gpsimd.tensor_scalar(sq, var, EPS, None, ALU.add))
                done(nc.gpsimd.tensor_tensor(r1, sq, nh[:, 0:QT], ALU.pow))
                done(nc.gpsimd.tensor_tensor(sq, r1, r1, ALU.mult))
                done(nc.gpsimd.tensor_tensor(sq, sq, var, ALU.mult))
                done(nc.gpsimd.tensor_scalar(sq, sq, EPS, None, ALU.add))
                done(nc.gpsimd.tensor_tensor(r2, sq, nh[:, 0:QT], ALU.pow))
                done(nc.gpsimd.tensor_tensor(sc, r1, r2, ALU.mult))
                done(nc.gpsimd.tensor_tensor(sh, m, sc, ALU.mult))
                nc.gpsimd.tensor_scalar(sh, sh, -1.0, None, ALU.mult).then_inc(sm["a_scale"], 1)
                wait_apart(pool, cst, sm["a_var2"], j + 1)
                nc.gpsimd.tensor_scalar(pt[5][:, :], mv[:, :, 1], EPS, None, ALU.add).then_inc(sm["a_pool2"], 1)
                pool.wait_ge(sm["a_pool2"], ONE + j * 3 + 1)
                nc.gpsimd.tensor_tensor(pt[5][:, :], pt[5][:, :], nh[:, 0:2 * QT], ALU.pow).then_inc(sm["a_pool2"], 1)
                pool.wait_ge(sm["a_pool2"], ONE + j * 3 + 2)
                nc.gpsimd.tensor_tensor(pt[4][:, :], mv[:, :, 0], pt[5][:, :], ALU.mult).then_inc(sm["a_pool2"], 1)
                wait_apart(pool, cst, sm["a_pool2"], j * 3 + 3)
                nc.gpsimd.tensor_scalar(pt[4][:, :], pt[4][:, :], -1.0, None, ALU.mult).then_inc(sm["a_rstd2"], 1)
                wait_apart(pool, cst, sm["f_var"], j + 1)
                nc.gpsimd.tensor_scalar(sq, var, EPS, None, ALU.add).then_inc(sm["f_pool"], 1)
                pool.wait_ge(sm["f_pool"], ONE + j * 3 + 1)
                nc.gpsimd.tensor_tensor(sc, sq, nh[:, 0:QT], ALU.pow).then_inc(sm["f_pool"], 1)
                pool.wait_ge(sm["f_pool"], ONE + j * 3 + 2)
                nc.gpsimd.tensor_tensor(sh, m, sc, ALU.mult).then_inc(sm["f_pool"], 1)
                wait_apart(pool, cst, sm["f_pool"], j * 3 + 3)
                nc.gpsimd.tensor_scalar(sh, sh, -1.0, None, ALU.mult).then_inc(sm["f_rstd"], 1)

        @block.tensor
        def _(pe):
            mm, tr, ident = nc.tensor.matmul, nc.tensor.transpose, cst["ident"]
            col = lambda t: slice(t * P, (t + 1) * P)

            def hidden(k, s):
                if s == 0:
                    pe.wait_ge(sm["xm_in"], ONE + k * 16 + 16)
                for c in range(FC):
                    n = s * FC + c
                    pe.wait_ge(sm["hid_done"], ONE + k * (S * FC) + max(n - 1, 0))
                    mm(ps_h[n % 2][:, :], w1[:, s, col(c)], xm[:, :], start=True, stop=True).then_inc(sm["h_ready"], 1)

            def expert_out(k, s, half):
                if half == 0:
                    pe.wait_ge(sm["hid_done"], ONE + k * (S * FC) + (s + 1) * FC)
                    pe.wait_ge(sm["y_added"], ONE + k * S + max(s - 1, 0))
                for t in (2 * half, 2 * half + 1):
                    for c in range(FC):
                        last = mm(ps_y[s % 2][:, col(t)], hid[:, s % 2, c, col(t)], w2[:, s, c, :],
                                  start=(c == 0), stop=(c == FC - 1))
                if half == 1:
                    last.then_inc(sm["y_ready"], 1)

            def attn_in(a):
                pe.wait_ge(sm["f_acted"], ONE + a * QT)
                if not isinstance(a, int) or a >= 2:
                    pe.wait_ge(sm["f_oacted"], ONE + (a - 1) * QT)
                pe.wait_ge(sm["a_silu"], ONE + a + 1)
                for t in range(QT):
                    last = tr(x0[:, col(t)], sx[:, t, :], ident[:, :])
                last.then_inc(sm["a_t"], 1)

            def attn_qkv(a, tiles):
                pe.wait_ge(sm["a_xt"], ONE + a + 1)
                for t in tiles:
                    if t >= 2:
                        pe.wait_ge(sm["a_bias"], ONE + a * QT + t - 1)
                    mm((x0, x1)[t % 2][:, 0:3 * P], xt[:, col(t)], wqkv[:, :],
                       start=True, stop=True).then_inc(sm["a_qkv"], 1)

            def attn_turn(a):
                pe.wait_ge(sm["a_norm"], ONE + a + 1)
                for i, x in enumerate((x0, x1)):
                    for t in range(QT):
                        last = tr(x[:, col(t)], qk_n[:, i, t, :], ident[:, :])
                    last.then_inc(sm["a_qkt"], 1)

            def attn_scores(a, u):
                if u >= 2:
                    pe.wait_ge(sm["a_exp"], ONE + a * 8 + u - 1)
                else:
                    pe.wait_ge(sm["a_qkc"], ONE + a * 3 + 3)
                r, cells = unit(u)
                rows = slice(32 * r, 32 * r + 32)
                for c, (t, b, h) in enumerate(cells):
                    last = mm((x0, x1)[u % 2][:, col(c)], q_t[rows, col(t)], k_t[rows, b, col(t)],
                              start=True, stop=True)
                last.then_inc(sm["a_s"], 1)

            def attn_turn_probs(a, u):
                pe.wait_ge(sm["a_exp"], ONE + a * 8 + u + 1)
                pe.wait_ge(sm["a_ptc"], ONE + a * 8 + u)
                for c in range(4):
                    last = tr(x2[:, col(c)], p_s[:, u % 2, c, :], ident[:, :])
                last.then_inc(sm["a_pt"], 1)

            def attn_values(a, u):
                if u == 0 and (not isinstance(a, int) or a >= 1):
                    pe.wait_ge(sm["f_practed"], ONE + (a - 1) * QT + QT)
                if u % 2 == 0:
                    pe.wait_ge(sm["a_on"], ONE + a * 4 + u // 2)
                pe.wait_ge(sm["a_ptc"], ONE + a * 8 + u + 1)
                for c, (t, b, h) in enumerate(unit(u)[1]):
                    last = mm(x3[:, t * P + h * D1:t * P + (h + 1) * D1], p_t[:, u % 2, c, :],
                              qkv[:, t, 2 * P + h * D1:2 * P + (h + 1) * D1], start=True, stop=True)
                last.then_inc(sm["a_pv"], 1)

            def attn_out_turn(a, f):
                pe.wait_ge(sm["a_silu2"], ONE + a + 1)
                if f is not None:
                    pe.wait_ge(sm["f_oacted"], ONE + f * QT + 2)
                for t in range(QT):
                    last = tr(x0[:, col(t)], sx[:, t, :], ident[:, :])
                last.then_inc(sm["a_ot"], 1)

            def attn_out(a):
                pe.wait_ge(sm["a_otc"], ONE + a + 1)
                for t in range(QT):
                    mm(x1[:, col(t)], xt[:, col(t)], wo[:, :], start=True, stop=False)
                    last = mm(x1[:, col(t)], cst["ones_row"][:, :], bo[:, :], start=False, stop=True)
                last.then_inc(sm["a_y"], 1)

            def ffn_in(a, f):
                pe.wait_ge(sm["f_norm"], ONE + a + 1)
                if f is not None:
                    pe.wait_ge(sm["f_oacted"], ONE + f * QT + QT)
                for t in range(QT):
                    last = tr(x0[:, col(t)], sx[:, t, :], ident[:, :])
                last.then_inc(sm["f_t"], 1)

            def input_acts(a, tiles):
                pe.wait_ge(sm["f_xt"], ONE + a + 1)
                for t in tiles:
                    if t >= 2:
                        pe.wait_ge(sm["f_acted"], ONE + a * QT + t - 1)
                    mm((x1, x0)[t % 2][:, :], xt[:, col(t)], w_in_t[:, :], start=True, stop=True).then_inc(sm["f_act"], 1)

            def turn_chosen(f, i, t, chunks):
                n = i * QT + t
                pe.wait_ge(sm["chosen_done"], ONE + f * (3 * QT) + n + 1)
                pe.wait_ge(sm["f_ctc"], ONE + f * (3 * QT) + n)
                for c in range(chunks):
                    last = tr(x2[:, col(c)], chosen[:, t % 2, col(c)], ident[:, :])
                last.then_inc(sm["f_ct"], 1)

            def process_acts(f, t):
                pe.wait_ge(sm["f_ctc"], ONE + f * (3 * QT) + t + 1)
                pe.wait_ge(sm["f_res"], ONE + f * QT)
                pe.wait_ge(sm["f_practed"], ONE + f * QT + t)
                for c in range(N_IN // P):
                    last = mm(x3[:, 0:N_PR], ch_t[:, col(c)], w_pr_t[:, c, :], start=(c == 0), stop=(c == N_IN // P - 1))
                last.then_inc(sm["f_pr"], 1)

            def aggregate(f, a, t):
                if a is not None:
                    pe.wait_ge(sm["a_on"], ONE + a * 4 + 4)
                pe.wait_ge(sm["f_ctc"], ONE + f * (3 * QT) + QT + t + 1)
                pe.wait_ge(sm["f_practed"], ONE + f * QT + QT)
                pe.wait_ge(sm["f_aggc"], ONE + f * QT + t)
                for c in range(N_PR // P):
                    last = mm(x3[0:D_PV, 0:P], w_val[:, c, :], ch_t[:, col(c)], start=(c == 0), stop=(c == N_PR // P - 1))
                last.then_inc(sm["f_agg"], 1)

            def output_acts(f, a, t):
                if a is not None:
                    if t < 2:
                        pe.wait_ge(sm["a_exp"], ONE + a * 8 + 8)
                    else:
                        pe.wait_ge(sm["h2_done"], ONE + a + 1)
                elif t >= 2:
                    pe.wait_ge(sm["f_oacted"], ONE + f * QT + t - 1)
                else:
                    pe.wait_ge(sm["f_acted"], ONE + G * QT)
                pe.wait_ge(sm["f_aggc"], ONE + f * QT + t + 1)
                mm((x0, x1)[t % 2][:, :], agg_t[:, t % 2, :], w_oi_t[:, :], start=True, stop=True).then_inc(sm["f_oact"], 1)

            def outputs(f, t):
                pe.wait_ge(sm["f_ctc"], ONE + f * (3 * QT) + 2 * QT + t + 1)
                pe.wait_ge(sm["f_aggc"], ONE + f * QT + QT)
                pe.wait_ge(sm["f_res"], ONE + f * QT + t)
                for c in range(N_OUT // P):
                    last = mm(x3[:, 0:P], ch_t[:, col(c)], w_out[:, c, :], start=(c == 0), stop=(c == N_OUT // P - 1))
                last.then_inc(sm["f_out"], 1)

            def patterns_first(f, s):
                for i, (plan, chunks) in enumerate(((S2, N_IN // P), (S3, N_PR // P), (S4, N_OUT // P))):
                    if s in plan:
                        turn_chosen(f, i, plan[s][0], chunks)

            def patterns_middle(f, a, s):
                if s in S2:
                    process_acts(f, S2[s][0])
                    turn_chosen(f, 0, S2[s][1], N_IN // P)
                if s in S3:
                    aggregate(f, a, S3[s][0])
                    turn_chosen(f, 1, S3[s][1], N_PR // P)
                if s in S4:
                    outputs(f, S4[s][0])
                    turn_chosen(f, 2, S4[s][1], N_OUT // P)

            def patterns_last(f, a, s):
                if s in S2:
                    process_acts(f, S2[s][1])
                if s in S3:
                    aggregate(f, a, S3[s][1])
                    output_acts(f, a, S3[s][0])
                    output_acts(f, a, S3[s][1])
                if s in S4:
                    outputs(f, S4[s][1])

            def one_pass(k, a, f):
                for s in range(S + 1):
                    if k is not None and s < S:
                        hidden(k, s)
                    if a is not None:
                        for u in range(8):
                            if s == SC + 2 + u // 2:
                                attn_values(a, u)
                        if s == QKV:
                            attn_qkv(a, (0, 1))
                        if s == OUT:
                            attn_out_turn(a, f)
                        if s == FIN:
                            ffn_in(a, f)
                        if s == S1:
                            input_acts(a, (0, 1))
                    if f is not None:
                        patterns_first(f, s)
                    if k is not None and s:
                        expert_out(k, s - 1, 0)
                    if f is not None:
                        patterns_middle(f, a, s)
                    if a is not None:
                        if s == S1:
                            input_acts(a, (2, 3))
                    if k is not None and s:
                        expert_out(k, s - 1, 1)
                    if f is not None:
                        patterns_last(f, a, s)
                    if a is not None:
                        if s == IN:
                            attn_in(a)
                        if s == OUT:
                            attn_out(a)
                        if s == QKV:
                            attn_qkv(a, (2, 3))
                        if s == TURN:
                            attn_turn(a)
                        for u in range(10):
                            if u >= 2 and s == SC + u // 2:
                                attn_turn_probs(a, u - 2)
                            if u < 8 and s == SC + u // 2:
                                attn_scores(a, u)

            pe.wait_ge(keep["w_in"], 16 * keep["w_loads"])
            pe.wait_ge(sm["c_half"], ONE + 1)
            one_pass(0, None, None)
            pe.wait_ge(sm["c_in"], ONE + 16 * 11)
            one_pass(1, 0, None)
            with pe.Fori(2, G) as k:
                one_pass(k, k - 1, k - 2)
            one_pass(None, G - 1, G - 2)
            one_pass(None, None, G - 1)

        @block.scalar
        def _(act):
            def hidden(k, s):
                act.wait_ge(sm["y_ready"], ONE + k * S + max(s - 1, 0))
                for c in range(FC):
                    n = s * FC + c
                    act.wait_ge(sm["h_ready"], ONE + k * (S * FC) + n + 1)
                    nc.scalar.activation(hid[:, s % 2, c, :], ps_h[n % 2][:, :], ACT.Gelu,
                                         bias=b1[:, s, c:c + 1]).then_inc(sm["hid_done"], 1)

            def attn_exps(a, u):
                if u >= 2:
                    act.wait_ge(sm["a_pt"], ONE + a * 8 + u - 1)
                act.wait_ge(sm["a_ntop"], ONE + a * 8 + u + 1)
                for c, (t, b, h) in enumerate(unit(u)[1]):
                    last = nc.scalar.activation(p_s[:, u % 2, c, :], (x0, x1)[u % 2][:, c * P:(c + 1) * P],
                                                ACT.Exp, bias=ntop[:, u % 2, c:c + 1], scale=SCALE,
                                                accum_out=z[:, t, h:h + 1])
                last.then_inc(sm["a_exp"], 1)

            def attn_copy(a, u):
                act.wait_ge(sm["a_pt"], ONE + a * 8 + u + 1)
                act.wait_ge(sm["a_pv"], ONE + a * 8 + max(u - 1, 0))
                nc.scalar.copy(p_t[:, u % 2].rearrange("p c n -> p (c n)"), x2[:, :]).then_inc(sm["a_ptc"], 1)

            def copy_queries_keys(a):
                act.wait_ge(sm["a_qkt"], ONE + a * 2 + 1)
                act.wait_ge(sm["a_s"], ONE + a * 8)
                nc.scalar.activation(q_t[:, :], x0[:, :], ACT.Identity, bias=gb[:, 1:2], scale=gb[:, 0:1]).then_inc(sm["a_qkc"], 1)
                act.wait_ge(sm["a_qkt"], ONE + a * 2 + 2)
                for b in range(2):
                    nc.scalar.activation(k_t[:, b, :], x1[:, :], ACT.Identity, bias=gbk[:, 1, b:b + 1],
                                         scale=gbk[:, 0, b:b + 1]).then_inc(sm["a_qkc"], 1)

            def heads_silu(a):
                act.wait_ge(sm["a_on"], ONE + a * 4 + 4)
                act.wait_ge(sm["a_t"], ONE + a + 1)
                flat = sx[:, :, :].rearrange("p t n -> p (t n)")
                nc.scalar.activation(flat, qk_n[:, 0].rearrange("p t n -> p (t n)"), ACT.Silu).then_inc(sm["a_silu2"], 1)

            def attention(a, s, silued):
                if s == IN:
                    act.wait_ge(sm["a_scale"], ONE + a + 1)
                    act.wait_ge(sm["f_t"], ONE + a)
                    for t in range(QT):
                        last = nc.scalar.activation(sx[:, t, :], h1[:, ds(a * QT + t, 1), :].rearrange("p a n -> p (a n)"),
                                                    ACT.Silu, bias=pt[4][:, t:t + 1], scale=pt[3][:, t:t + 1])
                    last.then_inc(sm["a_silu"], 1)
                    act.wait_ge(sm["a_t"], ONE + a + 1)
                    act.wait_ge(sm["f_act"], ONE + a * QT)
                    nc.scalar.copy(xt[:, :], x0[:, :]).then_inc(sm["a_xt"], 1)
                if s == TURN:
                    act.wait_ge(sm["a_rstd2"], ONE + a + 1)
                    act.wait_ge(sm["a_qkt"], ONE + a * 2)
                    for i in range(2):
                        for t in range(QT):
                            n = i * QT + t
                            last = nc.scalar.activation(qk_n[:, i, t, :], qkv[:, t, i * P:(i + 1) * P], ACT.Identity,
                                                        bias=pt[4][:, n:n + 1], scale=pt[5][:, n:n + 1])
                    last.then_inc(sm["a_norm"], 1)
                for u in range(8):
                    if s == SC + 1 + u // 2:
                        attn_exps(a, u)
                for u in range(8):
                    if s == SC + 1 + u // 2:
                        attn_copy(a, u)
                if s == OUT - 1 and not silued:
                    heads_silu(a)
                if s == OUT:
                    act.wait_ge(sm["a_ot"], ONE + a + 1)
                    act.wait_ge(sm["a_qkv"], ONE + a * QT + QT)
                    nc.scalar.copy(xt[:, :], x0[:, :]).then_inc(sm["a_otc"], 1)
                if s == FIN:
                    act.wait_ge(sm["f_t"], ONE + a + 1)
                    act.wait_ge(sm["a_y"], ONE + a + 1)
                    nc.scalar.copy(xt[:, :], x0[:, :]).then_inc(sm["f_xt"], 1)
                if s == S1:
                    for t in range(QT):
                        act.wait_ge(sm["f_act"], ONE + a * QT + t + 1)
                        if not isinstance(a, int) or a >= 1:
                            act.wait_ge(sm["chosen_done"], ONE + (a - 1) * (3 * QT) + QT)
                        nc.scalar.activation(acts[:, t, :], (x1, x0)[t % 2][:, :], ACT.Gelu).then_inc(sm["f_acted"], 1)

            def patterns(f, a, s):
                def turn_chosen(i, t, n):
                    m = i * QT + t
                    act.wait_ge(sm["f_ct"], ONE + f * (3 * QT) + m + 1)
                    if i == 0:
                        act.wait_ge(sm["f_pr"], ONE + f * QT + t)
                        act.wait_ge(sm["f_out"], ONE + f * QT)
                    if i == 1:
                        act.wait_ge(sm["f_agg"], ONE + f * QT + t)
                        act.wait_ge(sm["f_pr"], ONE + f * QT + QT)
                    if i == 2:
                        act.wait_ge(sm["f_out"], ONE + f * QT + t)
                        act.wait_ge(sm["f_agg"], ONE + f * QT + QT)
                    nc.scalar.copy(ch_t[:, 0:n], x2[:, 0:n]).then_inc(sm["f_ctc"], 1)

                def aggregate(t):
                    act.wait_ge(sm["f_agg"], ONE + f * QT + t + 1)
                    if t >= 2:
                        act.wait_ge(sm["f_oact"], ONE + f * QT + t - 1)
                    else:
                        act.wait_ge(sm["f_oact"], ONE + f * QT)
                    nc.scalar.copy(agg_t[:, t % 2, :], x3[0:D_PV, 0:P]).then_inc(sm["f_aggc"], 1)

                def output_act(t):
                    act.wait_ge(sm["f_oact"], ONE + f * QT + t + 1)
                    act.wait_ge(sm["f_rz"], ONE + f * QT + t + 1)
                    nc.scalar.activation(oacts[:, t, :], (x0, x1)[t % 2][:, :], ACT.Gelu, scale=rzp[:, t:t + 1]).then_inc(sm["f_oacted"], 1)

                for t in S2.get(s, ()):
                    turn_chosen(0, t, N_IN)
                    act.wait_ge(sm["f_pr"], ONE + f * QT + t + 1)
                    nc.scalar.activation(pacts[:, t, :], x3[:, 0:N_PR], ACT.Gelu).then_inc(sm["f_practed"], 1)
                for t in SE.get(s, ()):
                    act.wait_ge(sm["cleared"], ONE + f * ND + QT * R_IN + (t // 2) * (2 * R_PR) + t % 2 + 1)
                    if t >= 2:
                        act.wait_ge(sm["chosen_done"], ONE + f * (3 * QT) + QT + t - 1)
                    nc.scalar.activation(pexp[:, t % 2, :], pacts[:, t, :], ACT.Exp, bias=ptop[:, t:t + 1]).then_inc(sm["f_exp"], 1)
                if s in S3:
                    t0, t1 = S3[s]
                    turn_chosen(1, t0, N_PR)
                    aggregate(t0)
                    if s == OUT - 1 and a is not None:
                        heads_silu(a)
                    turn_chosen(1, t1, N_PR)
                    aggregate(t1)
                    output_act(t0)
                    output_act(t1)
                for t in S4.get(s, ()):
                    turn_chosen(2, t, N_OUT)

            def one_pass(k, a, f):
                for s in range(S + 1):
                    if k is not None and s < S:
                        hidden(k, s)
                    if a is not None and s == TURN + 1:
                        copy_queries_keys(a)
                    if f is not None:
                        patterns(f, a, s)
                    if a is not None:
                        attention(a, s, OUT - 1 in S3 and f is not None)

            act.wait_ge(keep["w_in"], 16 * keep["w_loads"])
            one_pass(0, None, None)
            act.wait_ge(sm["c_in"], ONE + 16 * 11)
            act.wait_ge(sm["gbk_done"], ONE + 2)
            one_pass(1, 0, None)
            with act.Fori(2, G) as k:
                one_pass(k, k - 1, k - 2)
            one_pass(None, G - 1, G - 2)
            one_pass(None, None, G - 1)

        @block.vector
        def _(v):
            tt, ts, stt = nc.vector.tensor_tensor, nc.vector.tensor_scalar, nc.vector.scalar_tensor_tensor
            four = lambda x: x[:, :].rearrange("p (t n) -> p t n", t=QT)
            tile = lambda j, t: h1[:, ds(j * QT + t, 1), :].rearrange("p a n -> p (a n)")
            group = lambda j: h1[:, ds(j * QT, QT), :]

            def add_expert(k, s):
                v.wait_ge(sm["y_ready"], ONE + k * S + s + 1)
                v.wait_ge(sm["y_added"], ONE + k * S + s)
                if s < SH:
                    tt(group(k), four(ps_y[s % 2]), group(k), ALU.add).then_inc(sm["y_added"], 1)
                    return
                for t in range(QT):
                    last = stt(out=tile(k, t), in0=ps_y[s % 2][:, t * P:(t + 1) * P],
                               scalar=comb[:, ds(k * QT + t, 1), s - SH], in1=tile(k, t), op0=ALU.mult, op1=ALU.add)
                last.then_inc(sm["y_added"], 1)

            def attn_first(a):
                v.wait_ge(sm["y_added"], ONE + a * S + S)
                wait_apart(v, cst, sm["f_rstd"], a)
                for t in range(QT):
                    last = nc.vector.bn_stats(stats[:, t, :], tile(a, t))
                last.then_inc(sm["a_stats"], 1)
                wait_apart(v, cst, sm["a_stats"], a + 1)
                for t in range(QT):
                    last = nc.vector.bn_aggr(mv[:, t, :], stats[:, t, :])
                last.then_inc(sm["a_var"], 1)

            def attn_bias(a, tiles):
                v.wait_ge(sm["a_pv"], ONE + a * 8)
                for t in tiles:
                    v.wait_ge(sm["a_qkv"], ONE + a * QT + t + 1)
                    tt(qkv[:, t, :], (x0, x1)[t % 2][:, 0:3 * P], bqkv[:, :], ALU.add).then_inc(sm["a_bias"], 1)

            def attn_moments(a):
                v.wait_ge(sm["a_bias"], ONE + a * QT + QT)
                v.wait_ge(sm["a_scale"], ONE + a + 1)
                for i in range(2):
                    for t in range(QT):
                        last = nc.vector.bn_stats(stats[:, i * QT + t, :], qkv[:, t, i * P:(i + 1) * P])
                last.then_inc(sm["a_stats2"], 1)
                wait_apart(v, cst, sm["a_stats2"], a + 1)
                for i in range(2 * QT):
                    last = nc.vector.bn_aggr(mv[:, i, :], stats[:, i, :])
                last.then_inc(sm["a_var2"], 1)

            def attn_top(a, u):
                v.wait_ge(sm["a_s"], ONE + a * 8 + u + 1)
                if u >= 2:
                    v.wait_ge(sm["a_exp"], ONE + a * 8 + u - 1)
                nc.vector.tensor_reduce(top[:, u % 2, :], four((x0, x1)[u % 2]), X, ALU.max).then_inc(sm["a_top"], 1)
                v.wait_ge(sm["a_top"], ONE + a * 8 + u + 1)
                ts(ntop[:, u % 2, :], top[:, u % 2, :], -SCALE, None, ALU.mult).then_inc(sm["a_ntop"], 1)

            def attn_divide(a, j):
                t, h = 2 * (j // 2), 4 * (j % 2)
                v.wait_ge(sm["a_exp"], ONE + a * 8 + 2 * j + 2)
                nc.vector.reciprocal(rz[:, t:t + 2, h:h + 4], z[:, t:t + 2, h:h + 4]).then_inc(sm["a_rz"], 1)
                v.wait_ge(sm["a_rz"], ONE + a * 4 + j + 1)
                v.wait_ge(sm["a_pv"], ONE + a * 8 + 2 * j + 2)
                heads = lambda x: x.rearrange("p t (h d) -> p t h d", h=4)
                tt(heads(qk_n[:, 0, t:t + 2, h * D1:(h + 4) * D1]), heads(four(x3)[:, t:t + 2, h * D1:(h + 4) * D1]),
                   rz[:, t:t + 2, h:h + 4].unsqueeze(3).broadcast_to([P, 2, 4, D1]), ALU.mult).then_inc(sm["a_on"], 1)

            def attn_add(a):
                v.wait_ge(sm["a_y"], ONE + a + 1)
                tt(group(a), four(x1), group(a), ALU.add).then_inc(sm["h2_done"], 1)
                wait_apart(v, cst, sm["h2_done"], a + 1)
                for t in range(QT):
                    last = nc.vector.bn_stats(stats[:, t, :], tile(a, t))
                last.then_inc(sm["f_stats"], 1)
                wait_apart(v, cst, sm["f_stats"], a + 1)
                for t in range(QT):
                    last = nc.vector.bn_aggr(mv[:, t, :], stats[:, t, :])
                last.then_inc(sm["f_var"], 1)

            def ffn_norm(a):
                v.wait_ge(sm["f_rstd"], ONE + a + 1)
                v.wait_ge(sm["a_ot"], ONE + a + 1)
                for t in range(QT):
                    last = ts(sx[:, t, :], tile(a, t), pt[3][:, t:t + 1], pt[4][:, t:t + 1], ALU.mult, ALU.add)
                last.then_inc(sm["f_norm"], 1)

            def choose(f, i, n):
                rounds = (R_IN, R_PR, R_OUT)[i]
                width = (N_IN, N_PR, N_OUT)[i]
                r = n % rounds
                tiles = [2 * (n // rounds), 2 * (n // rounds) + 1]
                at = f * ND + QT * sum((R_IN, R_PR, R_OUT)[:i]) + 2 * n
                src = [(acts, pacts, oacts)[i][:, t, :] if r == 0 else work[:, t % 2, 0:width] for t in tiles]
                for b, t in enumerate(tiles):
                    if r == 0:
                        wait_apart(v, cst, sm[("f_acted", "f_practed", "f_oacted")[i]], f * QT + t + 1)
                    else:
                        wait_apart(v, cst, sm["cleared"], at - 1 + b)
                    nc.vector.max(best[:, b, :], src[b]).then_inc(sm["found"], 1)
                for b, t in enumerate(tiles):
                    if i == 1 and r == 0:
                        v.wait_ge(sm["found"], ONE + at + 1 + b)
                        ts(ptop[:, t:t + 1], best[:, b, 0:1], -1.0, None, ALU.mult)
                    wait_apart(v, cst, sm["found"], at + 1 + b)
                    nc.vector.match_replace(work[:, b, 0:width], best[:, b, :], src[b], GONE).then_inc(sm["cleared"], 1)
                if r < rounds - 1:
                    return
                for b, t in enumerate(tiles):
                    m = i * QT + t
                    v.wait_ge(sm["cleared"], ONE + at + 1 + b)
                    v.wait_ge(sm["f_ct"], ONE + f * (3 * QT) + max(m - 1, 0))
                    wk, ch = work[:, b, 0:width], chosen[:, b, 0:width]
                    if i == 1:
                        v.wait_ge(sm["f_exp"], ONE + f * QT + t + 1)
                        stt(out=ch, in0=wk, scalar=IS_GONE, in1=pexp[:, t % 2, :], op0=ALU.is_lt, op1=ALU.mult,
                            accum_out=zp[:, t:t + 1]).then_inc(sm["chosen_done"], 1)
                        v.wait_ge(sm["chosen_done"], ONE + f * (3 * QT) + m + 1)
                        nc.vector.reciprocal(rzp[:, t:t + 1], zp[:, t:t + 1]).then_inc(sm["f_rz"], 1)
                    else:
                        stt(out=ch, in0=wk, scalar=IS_GONE, in1=(acts, None, oacts)[i][:, t, :], op0=ALU.is_lt,
                            op1=ALU.mult).then_inc(sm["chosen_done"], 1)

            def finish(f, t):
                v.wait_ge(sm["f_out"], ONE + f * QT + t + 1)
                if t == 0:
                    v.wait_ge(sm["out_done"], ONE + f * 16)
                tt(h_out[:, t, :], x3[:, 0:P], tile(f, t), ALU.add).then_inc(sm["f_res"], 1)

            def one_pass(k, a, f):
                for s in range(S + 1):
                    if a is not None:
                        if s == IN - 1:
                            attn_first(a)
                        for u in range(8):
                            if s == SC + 1 + u // 2:
                                attn_top(a, u)
                        if s == OUT + 2:
                            ffn_norm(a)
                    if a is not None and f is not None and s == QKV:
                        attn_bias(a, (0, 1))
                    todo = [(i, n) for i, rounds in enumerate((R1, R2, R3)) for n in range(*rounds.get(s, (0, 0)))]
                    if f is not None:
                        for i, n in todo[:1]:
                            choose(f, i, n)
                    if a is not None:
                        if s == QKV and f is None:
                            attn_bias(a, (0, 1))
                        if s == OUT + 1:
                            attn_add(a)
                        if SC + 2 <= s < SC + 6:
                            attn_divide(a, s - SC - 2)
                    if f is not None:
                        for i, n in todo[1:]:
                            choose(f, i, n)
                    if a is not None:
                        for n in range(*R0.get(s, (0, 0))):
                            choose(a, 0, n)
                        if s == QKV:
                            attn_bias(a, (2, 3))
                            attn_moments(a)
                    if f is not None and s in S4:
                        finish(f, S4[s][0])
                    if k is not None and s:
                        add_expert(k, s - 1)
                    if f is not None and s in S4:
                        finish(f, S4[s][1])

            v.wait_ge(keep["w_in"], 16 * keep["w_loads"])
            shared = w2[:, 0:SH].rearrange("p s c n -> p (s c n)")
            ts(shared, shared, 1.0 / SH, None, ALU.mult).then_inc(sm["c_half"], 1)
            one_pass(0, None, None)
            v.wait_ge(sm["c_in"], ONE + 16 * 11)
            for i in range(2):
                ts(gbk[:, i, :], odd[:, :], gb[:, 2 + i:3 + i], None, ALU.mult).then_inc(sm["gbk_done"], 1)
            one_pass(1, 0, None)
            with v.Fori(2, G) as k:
                one_pass(k, k - 1, k - 2)
            one_pass(None, G - 1, G - 2)
            one_pass(None, None, G - 1)


def lm_tower(nc, d, out):
    E, SH, FC = 16, 2, 4
    scr = {
        "h": nc.dram_tensor("scr_h", [G, P, W4], F32).ap(),
        "xt": nc.dram_tensor("scr_xt", [G, P, W4], F32).ap(),
        "o": nc.dram_tensor("scr_o", [4, P, SEQ * P], F32).ap(),
        "xm": nc.dram_tensor("scr_xm", [G, P, W4], F32).ap(),
    }
    with ExitStack() as ctx:
        cst = {
            "ident": ctx.enter_context(nc.sbuf_tensor("ident", [P, P], F32)),
            "neg_half": ctx.enter_context(nc.sbuf_tensor("neg_half", [P, SEQ], F32)),
            "ones_row": ctx.enter_context(nc.sbuf_tensor("ones_row", [1, P], F32)),
            "pool_step": ctx.enter_context(nc.semaphore("pool_step")),
            "consts_done": ctx.enter_context(nc.semaphore("consts_done")),
        }
        tokens_phase(nc, d, cst, scr)
        attention0_phase(nc, d, cst, scr)
        keep = {
            "h1": ctx.enter_context(nc.sbuf_tensor("h1", [P, SEQ, P], F32)),
            "comb": ctx.enter_context(nc.sbuf_tensor("comb", [P, SEQ, E], F32)),
            "w1": ctx.enter_context(nc.sbuf_tensor("w1", [P, E + SH, FC * P], F32)),
            "w2": ctx.enter_context(nc.sbuf_tensor("w2", [P, E + SH, FC, P], F32)),
            "b1": ctx.enter_context(nc.sbuf_tensor("b1", [P, E + SH, FC], F32)),
            "h1_kept": ctx.enter_context(nc.semaphore("h1_kept")),
            "comb_kept": ctx.enter_context(nc.semaphore("comb_kept")),
            "w_in": ctx.enter_context(nc.semaphore("experts_in")),
        }
        mix_phase(nc, d, cst, scr, keep)
        tower_phase(nc, d, cst, scr, keep, out)


def kernel(**inputs):
    import numpy as np
    import concourse.bacc as bacc
    from concourse import mybir as mb
    from concourse.bass_utils import run_bass_kernel_spmd as run

    a = {k: np.asarray(v) for k, v in inputs.items()}
    L = lambda x: np.ascontiguousarray(x)
    lay = {
        "ids": L(a["x"].T),
        "wt": L(a["L0_tok_W"].T),
        "tok_b": a["L0_tok_b"],
        "bo": a["L0_attn_bo"],
        "wqkv": L(np.stack([a[f"L0_attn_W{n}"].reshape(128, 4, 128) for n in "qkv"], 0).transpose(2, 1, 0, 3)),
        "bqkv": L(np.stack([a[f"L0_attn_b{n}"].reshape(4, 128) for n in "qkv"], 0).transpose(1, 2, 0)),
        "pk": np.tile(a["L0_attn_P_k"].T, (1, 128)),
        "pv": L(a["L0_attn_P_v"].transpose(1, 0, 2)),
        "wo": L(a["L0_attn_Wo"].reshape(4, 128, 128).transpose(1, 0, 2)),
        "gate": L(a["L0_ffn_gate_w"].T),
        "b2": np.concatenate([a["L0_ffn_re_b2"], a["L0_ffn_se_b2"]]),
        "w1": L(np.concatenate([a["L0_ffn_se_w1"], a["L0_ffn_re_w1"]]).transpose(1, 0, 2)),
        "w2": L(np.concatenate([a["L0_ffn_se_w2"], a["L0_ffn_re_w2"]]).reshape(18, 4, 128, 128).transpose(2, 0, 1, 3)),
        "b1": L(np.concatenate([a["L0_ffn_se_b1"], a["L0_ffn_re_b1"]]).reshape(18, 4, 128).transpose(2, 0, 1)),
        "wqkv1": np.concatenate([a[f"L1_attn_w_{n}"] for n in "qkv"], 1),
        "bqkv1": np.concatenate([a[f"L1_attn_b_{n}"] for n in "qkv"]),
        "wo1": a["L1_attn_w_o"],
        "bo1": a["L1_attn_b_o"].reshape(1, 128),
        "gb": L(np.stack([a[f"L1_attn_{n}"] for n in ("g_q", "be_q", "g_k", "be_k")], 1)),
        "odd": np.stack([np.arange(128) // 16 % 2 == b for b in range(2)], 1).astype(np.float32),
        "ip": L(a["L1_ffn_input_patterns"].T),
        "piw": L(a["L1_ffn_process_input_weights"].T.reshape(4, 128, 256).transpose(1, 0, 2)),
        "pval": L(a["L1_ffn_process_values"].reshape(2, 128, 64).transpose(1, 0, 2)),
        "oiw": L(a["L1_ffn_output_input_weights"].T),
        "op": L(a["L1_ffn_output_patterns"].reshape(4, 128, 128).transpose(1, 0, 2)),
    }
    nc = bacc.Bacc("TRN2", target_bir_lowering=False, num_devices=1)
    arrays, args = {}, {}
    for name, arr in lay.items():
        arrays[f"in_{name}"] = arr
        args[name] = nc.dram_tensor(f"in_{name}", arr.shape, mb.dt.from_np(arr.dtype), kind="ExternalInput").ap()
    out = nc.dram_tensor("out_h", (SEQ, P, P), mb.dt.float32, kind="ExternalOutput").ap()
    lm_tower(nc, args, out)
    r = run(nc, [arrays], core_ids=[0])
    return r.results[0]["out_h"]
```
